# Optimizing a Trainium2 kernel written in Bass

```python
import numpy as np
import jax
import jax.numpy as jnp

def _softmax(x, axis=-1):
    return jax.nn.softmax(x, axis=axis)

def _gelu(x):
    return jax.nn.gelu(x, approximate=True)

def _silu(x):
    return jax.nn.silu(x)

def _sigmoid(x):
    return jax.nn.sigmoid(x)

def _layernorm(x, axis=-1, eps=1e-05):
    m = jnp.mean(x, axis=axis, keepdims=True)
    v = jnp.var(x, axis=axis, keepdims=True)
    return (x - m) / jnp.sqrt(v + eps)

def _scatter_add(tgt, idx, src, axis=0):
    return tgt.at[idx].add(src)

def _segment_sum(src, seg, n):
    return jax.ops.segment_sum(src, seg, n)
kernel_name = 'mk_prb_d2_jaxref_r8_6c0ae0'

def setup_inputs(seed: int=0):
    np.random.seed(seed)
    _w = jnp.asarray

    def _L0_attn_setup():
        import jax, jax.numpy as jnp
        import numpy as np
        import math
        NUM_HEADS = 16
        ROPE_BASE = 10000.0
        SLIDING_WINDOW = 64

        def _rope_cos_sin(seq_len, head_dim, dtype):
            inv_freq = 1.0 / ROPE_BASE ** (jnp.arange(0, head_dim, 2, dtype=jnp.float32) / head_dim)
            t = jnp.arange(seq_len, dtype=jnp.float32)
            freqs = t[:, None] * inv_freq[None, :]
            emb = jnp.concatenate([freqs, freqs], axis=-1)
            return (jnp.cos(emb)[None, :, None, :].astype(dtype), jnp.sin(emb)[None, :, None, :].astype(dtype))

        def _rotate_half(x):
            x1, x2 = jnp.split(x, 2, axis=-1)
            return jnp.concatenate([-x2, x1], axis=-1)
        key = jax.random.key(seed)
        ks = jax.random.split(key, 9)
        B, S, E = (2, 256, 256)
        sc = 1.0 / math.sqrt(E)
        return {'hidden_states': jax.random.normal(ks[0], (B, S, E), dtype=jnp.float32), 'Wq': jax.random.normal(ks[1], (E, E), dtype=jnp.float32) * sc, 'bq': jax.random.normal(ks[2], (E,), dtype=jnp.float32) * 0.01, 'Wk': jax.random.normal(ks[3], (E, E), dtype=jnp.float32) * sc, 'bk': jax.random.normal(ks[4], (E,), dtype=jnp.float32) * 0.01, 'Wv': jax.random.normal(ks[5], (E, E), dtype=jnp.float32) * sc, 'bv': jax.random.normal(ks[6], (E,), dtype=jnp.float32) * 0.01, 'Wo': jax.random.normal(ks[7], (E, E), dtype=jnp.float32) * sc, 'bo': jax.random.normal(ks[8], (E,), dtype=jnp.float32) * 0.01}
    _L0_attn_in = _L0_attn_setup()

    def _L0_ffn_setup():
        import jax, jax.numpy as jnp
        import numpy as np
        NUM_EXPERTS = 8
        TOP_K = 2
        MODEL_DIM = 256
        INTER_DIM = 128
        GATE_SCALE = 1.0
        UP_SCALE = 0.0
        key = jax.random.key(seed)
        k1, k2, k3, k4 = jax.random.split(key, 4)
        hidden_states = jax.random.normal(k1, (2, 256, MODEL_DIM), jnp.float32)
        router_gate = jax.random.normal(k2, (NUM_EXPERTS, MODEL_DIM), jnp.float32) * 0.02
        expert_gate_up = jax.random.normal(k3, (NUM_EXPERTS, MODEL_DIM, 2 * INTER_DIM), jnp.float32) * 0.02
        expert_down = jax.random.normal(k4, (NUM_EXPERTS, INTER_DIM, MODEL_DIM), jnp.float32) * 0.02
        return {'hidden_states': hidden_states, 'router_gate': router_gate, 'expert_gate_up': expert_gate_up, 'expert_down': expert_down}
    _L0_ffn_in = _L0_ffn_setup()

    def _L1_attn_setup():
        import jax, jax.numpy as jnp
        import numpy as np
        DIM = 256
        key = jax.random.key(seed)
        ks = jax.random.split(key, 9)
        scale = 1.0 / np.sqrt(DIM)
        x = jax.random.normal(ks[0], (4, 512, DIM), dtype=jnp.float32)

        def lin(kw, kb):
            W = jax.random.uniform(kw, (DIM, DIM), jnp.float32, -scale, scale)
            b = jax.random.uniform(kb, (DIM,), jnp.float32, -scale, scale)
            return (W, b)
        Wq, bq = lin(ks[1], ks[2])
        Wk, bk = lin(ks[3], ks[4])
        Wv, bv = lin(ks[5], ks[6])
        Wg, bg = lin(ks[7], ks[8])
        return {'x': x, 'Wq': Wq, 'bq': bq, 'Wk': Wk, 'bk': bk, 'Wv': Wv, 'bv': bv, 'Wg': Wg, 'bg': bg}
    _L1_attn_in = _L1_attn_setup()

    def _L1_ffn_setup():
        import jax, jax.numpy as jnp
        import numpy as np
        B, S, D = (4, 512, 256)
        DFF = 4 * D
        SKIP = 0.125
        key = jax.random.key(seed)
        ks = jax.random.split(key, 4)
        s_in = 1.0 / np.sqrt(D).astype(np.float32)
        s_ff = 1.0 / np.sqrt(DFF).astype(np.float32)
        return {'x': jax.random.normal(ks[0], (B, S, D), jnp.float32), 'Wr': jax.random.normal(ks[1], (D, 1), jnp.float32) * s_in, 'br': jnp.zeros((1,), jnp.float32), 'W1': jax.random.normal(ks[2], (D, DFF), jnp.float32) * s_in, 'b1': jnp.zeros((DFF,), jnp.float32), 'W2': jax.random.normal(ks[3], (DFF, D), jnp.float32) * s_ff, 'b2': jnp.zeros((D,), jnp.float32)}
    _L1_ffn_in = _L1_ffn_setup()
    _d = {'L0_attn_hidden_states': _L0_attn_in['hidden_states'], 'L0_attn_Wq': _L0_attn_in['Wq'], 'L0_attn_bq': _L0_attn_in['bq'], 'L0_attn_Wk': _L0_attn_in['Wk'], 'L0_attn_bk': _L0_attn_in['bk'], 'L0_attn_Wv': _L0_attn_in['Wv'], 'L0_attn_bv': _L0_attn_in['bv'], 'L0_attn_Wo': _L0_attn_in['Wo'], 'L0_attn_bo': _L0_attn_in['bo'], 'L0_ffn_router_gate': _L0_ffn_in['router_gate'], 'L0_ffn_expert_gate_up': _L0_ffn_in['expert_gate_up'], 'L0_ffn_expert_down': _L0_ffn_in['expert_down'], 'L1_attn_Wq': _L1_attn_in['Wq'], 'L1_attn_bq': _L1_attn_in['bq'], 'L1_attn_Wk': _L1_attn_in['Wk'], 'L1_attn_bk': _L1_attn_in['bk'], 'L1_attn_Wv': _L1_attn_in['Wv'], 'L1_attn_bv': _L1_attn_in['bv'], 'L1_attn_Wg': _L1_attn_in['Wg'], 'L1_attn_bg': _L1_attn_in['bg'], 'L1_ffn_Wr': _L1_ffn_in['Wr'], 'L1_ffn_br': _L1_ffn_in['br'], 'L1_ffn_W1': _L1_ffn_in['W1'], 'L1_ffn_b1': _L1_ffn_in['b1'], 'L1_ffn_W2': _L1_ffn_in['W2'], 'L1_ffn_b2': _L1_ffn_in['b2']}
    _x0 = _d['L0_attn_hidden_states']
    _d['L0_attn_hidden_states'] = jax.random.normal(jax.random.fold_in(jax.random.key(seed), 1), (1, 2048, 256), dtype=_x0.dtype)
    del _x0
    return _d

def reference(L0_attn_hidden_states, L0_attn_Wq, L0_attn_bq, L0_attn_Wk, L0_attn_bk, L0_attn_Wv, L0_attn_bv, L0_attn_Wo, L0_attn_bo, L0_ffn_router_gate, L0_ffn_expert_gate_up, L0_ffn_expert_down, L1_attn_Wq, L1_attn_bq, L1_attn_Wk, L1_attn_bk, L1_attn_Wv, L1_attn_bv, L1_attn_Wg, L1_attn_bg, L1_ffn_Wr, L1_ffn_br, L1_ffn_W1, L1_ffn_b1, L1_ffn_W2, L1_ffn_b2):

    def _L0_attn_ref(hidden_states, Wq, bq, Wk, bk, Wv, bv, Wo, bo):
        import jax, jax.numpy as jnp
        import numpy as np
        import math
        NUM_HEADS = 16
        ROPE_BASE = 10000.0
        SLIDING_WINDOW = 64

        def _rope_cos_sin(seq_len, head_dim, dtype):
            inv_freq = 1.0 / ROPE_BASE ** (jnp.arange(0, head_dim, 2, dtype=jnp.float32) / head_dim)
            t = jnp.arange(seq_len, dtype=jnp.float32)
            freqs = t[:, None] * inv_freq[None, :]
            emb = jnp.concatenate([freqs, freqs], axis=-1)
            return (jnp.cos(emb)[None, :, None, :].astype(dtype), jnp.sin(emb)[None, :, None, :].astype(dtype))

        def _rotate_half(x):
            x1, x2 = jnp.split(x, 2, axis=-1)
            return jnp.concatenate([-x2, x1], axis=-1)
        B, S, E = hidden_states.shape
        H = NUM_HEADS
        D = E // H
        q = (hidden_states @ Wq.T + bq).reshape(B, S, H, D)
        k = (hidden_states @ Wk.T + bk).reshape(B, S, H, D)
        v = (hidden_states @ Wv.T + bv).reshape(B, S, H, D)
        cos, sin = _rope_cos_sin(S, D, q.dtype)
        q = q * cos + _rotate_half(q) * sin
        k = k * cos + _rotate_half(k) * sin
        scale = 1.0 / math.sqrt(D)
        scores = jnp.einsum('bqhd,bkhd->bhqk', q, k) * scale
        attn = jax.nn.softmax(scores, axis=-1)
        out = jnp.einsum('bhqk,bkhd->bqhd', attn, v).reshape(B, S, E)
        return out @ Wo.T + bo

    def _L0_ffn_ref(hidden_states, router_gate, expert_gate_up, expert_down):
        import jax, jax.numpy as jnp
        import numpy as np
        NUM_EXPERTS = 8
        TOP_K = 2
        MODEL_DIM = 256
        INTER_DIM = 128
        GATE_SCALE = 1.0
        UP_SCALE = 0.0
        orig_shape = hidden_states.shape
        hs = hidden_states.reshape(-1, orig_shape[-1])
        T = hs.shape[0]
        logits = hs @ router_gate.T
        probs = jax.nn.softmax(logits.astype(jnp.float32), axis=-1)
        topk_scores, topk_idx = jax.lax.top_k(probs, TOP_K)
        topk_scores = topk_scores / jnp.sum(topk_scores, axis=-1, keepdims=True)
        scores_f = topk_scores.T.reshape(-1).astype(hs.dtype)
        ids_f = topk_idx.T.reshape(-1)
        order = jnp.argsort(ids_f)
        sorted_ids = ids_f[order]
        scores_sorted = scores_f[order]
        token_slots = order % T
        x = hs[token_slots]
        inter = jnp.zeros((x.shape[0], 2 * INTER_DIM), x.dtype)
        for e in range(NUM_EXPERTS):
            m = (sorted_ids == e)[:, None]
            inter = inter + jnp.where(m, x, 0) @ expert_gate_up[e]
        gate = inter[..., 0::2]
        up = inter[..., 1::2]
        h = (up + UP_SCALE) * jax.nn.silu(gate * GATE_SCALE)
        out_rows = jnp.zeros((x.shape[0], MODEL_DIM), x.dtype)
        for e in range(NUM_EXPERTS):
            m = (sorted_ids == e)[:, None]
            out_rows = out_rows + jnp.where(m, h, 0) @ expert_down[e]
        out = jnp.zeros_like(hs).at[token_slots].add(out_rows * scores_sorted[:, None])
        return out.reshape(orig_shape)

    def _L1_attn_ref(x, Wq, bq, Wk, bk, Wv, bv, Wg, bg):
        import jax, jax.numpy as jnp
        import numpy as np
        DIM = 256
        q = jnp.einsum('bsd,ed->bse', x, Wq) + bq
        k = jnp.einsum('bsd,ed->bse', x, Wk) + bk
        v = jnp.einsum('bsd,ed->bse', x, Wv) + bv
        g = jax.nn.sigmoid(jnp.einsum('bsd,ed->bse', x, Wg) + bg)
        kv_state = jnp.cumsum(k * v, axis=1)
        return q * kv_state * g

    def _L1_ffn_ref(x, Wr, br, W1, b1, W2, b2):
        import jax, jax.numpy as jnp
        import numpy as np
        B, S, D = (4, 512, 256)
        DFF = 4 * D
        SKIP = 0.125
        Bs, Ss, Ds = x.shape
        k = max(int(Ss * SKIP), 1)
        logits = (x @ Wr + br)[..., 0]
        weights, idx = jax.lax.top_k(logits, k)
        perm = jnp.argsort(idx, axis=1)
        tokens = jnp.take_along_axis(idx, perm, axis=1)
        fx = jnp.take_along_axis(x, tokens[..., None], axis=1)
        h = jax.nn.gelu(fx @ W1 + b1, approximate=False)
        out_l = h @ W2 + b2
        tw = jax.nn.softmax(weights, axis=1)
        rw = jnp.take_along_axis(tw, perm, axis=1)
        xw = rw[..., None] * out_l
        bidx = jnp.arange(Bs)[:, None]
        return x.at[bidx, tokens].add(xw)
    x = L0_attn_hidden_states
    xn = _layernorm(x, axis=-1)
    x = x + _L0_attn_ref(xn, L0_attn_Wq, L0_attn_bq, L0_attn_Wk, L0_attn_bk, L0_attn_Wv, L0_attn_bv, L0_attn_Wo, L0_attn_bo) + _L0_ffn_ref(xn, L0_ffn_router_gate, L0_ffn_expert_gate_up, L0_ffn_expert_down)
    xn = _layernorm(x, axis=-1)
    x = x + _L1_attn_ref(xn, L1_attn_Wq, L1_attn_bq, L1_attn_Wk, L1_attn_bk, L1_attn_Wv, L1_attn_bv, L1_attn_Wg, L1_attn_bg) + _L1_ffn_ref(xn, L1_ffn_Wr, L1_ffn_br, L1_ffn_W1, L1_ffn_b1, L1_ffn_W2, L1_ffn_b2)
    return x

_drawn_inputs = setup_inputs


def setup_inputs(seed=0):
    import zlib

    import numpy as np

    out = dict(_drawn_inputs(seed))
    spreads = {'L1_ffn_b1': (0.0, 2.0), 'L1_ffn_b2': (0.0, 2.0)}
    factors = {'L0_attn_bq': 64.0,
     'L0_attn_bk': 64.0,
     'L0_attn_bv': 3.126,
     'L0_attn_bo': 3.288,
     'L0_ffn_router_gate': 6.309,
     'L0_ffn_expert_gate_up': 5.512,
     'L0_ffn_expert_down': 5.577,
     'L1_attn_bg': 3.663,
     'L1_ffn_Wr': 8.0,
     'L1_ffn_W1': 8.0,
     'L1_ffn_W2': 8.0}
    for name, (base, spread) in spreads.items():
        noise = np.random.default_rng([zlib.crc32(name.encode()), seed]).standard_normal(out[name].shape)
        drawn = base * np.exp(spread * noise) if base else spread * noise
        out[name] = jnp.asarray(drawn.astype(out[name].dtype))
    for name, factor in factors.items():
        out[name] = (out[name] * factor).astype(out[name].dtype)
    return out
```

```python
from contextlib import ExitStack

import numpy as np

import concourse.bass as bass
from concourse import mybir

F32 = mybir.dt.float32
BF16 = mybir.dt.bfloat16
ALU = mybir.AluOpType
ACT = mybir.ActivationFunctionType
AX = mybir.AxisListType

P = 128
T, E = 2048, 256
NT = T // P
BLK = 512
NB = T // BLK
TPB = BLK // P
KH = E // P
NH, HD = 16, 16
HG = 4
NG = NH // HG
QROWS = [0, 0, 1, 1, 0, 2]
KROWS = [0, 1, 0, 1, 2, 0]
CROWS = 16 * len(QROWS)
MROWS = 3
NEX, INTER = 8, 128
SLOTS = 256
DFF = 1024
FC = DFF // P
EPS = 1e-5
SCALE = 1.0 / HD ** 0.5
NIT = NG * NB
TWO_ONES = float(np.array([0x3F803F80], np.uint32).view(np.float32)[0])
GMASK = NIT - NB
QRING = 8


def program(nc, x, wqk, bqk, cosT, sinT, wvr, bv, bo, wgu, wdn, wo, w4, b4, wrb, br, w1, b1, w2, b2, out):
    parts_d = nc.dram_tensor("parts_scratch", [2, 3, NH, 2, 8, T], BF16).ap()
    max_d = nc.dram_tensor("max_scratch", [NIT, 3 * HG * TPB, P], BF16).ap()

    with ExitStack() as ctx:
        def sb(name, shape, dt=F32):
            return ctx.enter_context(nc.sbuf_tensor(name, shape, dt))

        def sem(name):
            return ctx.enter_context(nc.semaphore(name))

        ps = ctx.enter_context(nc.psum_tensor("ps", [P, 8, BLK], F32))

        xs = sb("xs", [P, NT, E])
        wide = sb("wide", [P, NG * T])
        kbig = sb("kbig", [P, NG * HG * T], BF16)
        qring = sb("qring", [P, QRING * HG * BLK], BF16)
        vall = sb("vall", [P, NT * NH * (HD + 1)])
        vst = sb("vst", [P, NT, HG, 32])
        prob = sb("prob", [P, 2, HG * BLK])
        osb = sb("osb", [P, BLK])
        rl = sb("rl", [P, BLK])
        ident = sb("ident", [P, P])
        identb = sb("identb", [P, P], BF16)
        selb = sb("selb", [P, P])
        stats = sb("stats", [P, NT, 6])
        mv = sb("mv", [P, NT, 2])
        std = sb("std", [P, NT])
        rstd = sb("rstd", [P, NT])
        epsc = sb("epsc", [P, 1])
        bqk_s = sb("bqk_s", [P, 4])
        mraw = sb("mraw", [P, HG * NT * NB])
        mneg = sb("mneg", [P, HG * TPB])
        mres = sb("mres", [P, HG * TPB])
        mpad = sb("mpad", [P, P], BF16)
        mt = sb("mt", [3 * HG * TPB, P], BF16)
        lg = sb("lg", [P, NT, NEX])
        rt = sb("rt", [P, 4, NT, NEX])
        rs = sb("rs", [P, 4, NT])
        wtok = sb("wtok", [P, NEX, NT])

        mpart = mpad[:, 0:3 * HG * TPB].rearrange("p (s n) -> p s n", s=3)
        xn = wide[:, 0:NT * E].rearrange("p (t e) -> p t e", t=NT)
        xnT = wide[:, NT * E:2 * NT * E].rearrange("p (k t) -> p k t", k=KH)
        outT = wide[:, :].rearrange("p (g t) -> p g t", g=NG)
        K = kbig[:, :].rearrange("p (c t) -> p c t", t=T)

        kf = kbig[:, HG * T:].bitcast(F32)
        qf = qring[:, :].bitcast(F32)
        qk = kf[:, 0:2 * 4 * BLK].rearrange("p (b a n) -> p b a n", b=2, a=4)
        tmp = kf[:, 4096:4096 + 8 * BLK].rearrange("p (j a n) -> p j a n", j=4, a=2)
        cos_s = kf[:, 8192:8192 + T]
        sin_s = kf[:, 8192 + T:8192 + 2 * T]
        prt = qring[:, 0:2 * 12 * BLK].rearrange("p (b s a n) -> p b s a n", b=2, s=3, a=4)
        rem = qf[:, 12 * BLK:16 * BLK].rearrange("p (a n) -> p a n", a=4)
        pf = prob[:, :, :].rearrange("p a n -> p (a n)")
        wqk_s = pf[:, 0:1024].rearrange("p (k n) -> p k n", k=KH)
        wvr_s = pf[:, 1024:1024 + KH * 264].rearrange("p (k n) -> p k n", k=KH)
        bv_s = pf[:, 1600:1856]
        bo_s = pf[:, 1856:2112]
        cmp = pf[:, 2112:2112 + NEX * NT * NEX].rearrange("p (a t e) -> p a t e", a=NEX, t=NT)
        moe = sb("moe", [P, 2, 768])
        wgu_s = [moe[:, j, 0:512].rearrange("p (k n) -> p k n", k=KH) for j in range(2)]
        wdn_s = [moe[:, j, 512:768] for j in range(2)]
        sg = [vst[:, 4 * j:4 * j + 4, :, :].rearrange("p a b c -> p (a b c)") for j in range(2)]
        hb = [vst[:, 8 + 4 * j:12 + 4 * j, :, :].rearrange("p a b c -> p (a b c)") for j in range(2)]
        dsc = [pf[:, 2048 * j:2048 * j + 1024].rearrange("p (a n) -> p a n", a=TPB) for j in range(2)]

        x_ld = [sem(f"x_ld{c}") for c in range(NB)]
        wqk_ld, tab_ld, wv_ld, wo_ld, w4_ld, wf_ld = (sem(n) for n in ("wqk_ld", "tab_ld", "wv_ld", "wo_ld", "w4_ld", "wf_ld"))
        ids, consts = sem("ids"), sem("consts")
        dve_s, act_s, pool_s = sem("dve_s"), sem("act_s"), sem("pool_s")
        var_ok, std_ok, xn_ok = sem("var_ok"), sem("std_ok"), sem("xn_ok")
        tr_done, xT_a, xT_v = sem("tr_done"), sem("xT_a"), sem("xT_v")
        qk_done, qk_ok = sem("qk_done"), sem("qk_ok")
        v_done, v_ok = sem("v_done"), sem("v_ok")
        rope_p, rope_in_free = sem("rope_p"), sem("rope_in_free")
        r_ok, rem_ok, hi_ok, mid_ok, lo_ok = (sem(n) for n in ("r_ok", "rem_ok", "hi_ok", "mid_ok", "lo_ok"))
        part_st = [sem("part_st0"), sem("part_st1")]
        lgx_ok, ex_ok, wt_ok = sem("lgx_ok"), sem("ex_ok"), sem("wt_ok")
        k_ld = [sem(f"k_ld{g}") for g in range(NG)]
        ones_ok = sem("ones_ok")
        q_ld = sem("q_ld")
        we_ld = [sem("we_ld0"), sem("we_ld1")]
        gu_done, silu_ok, h_ok, dn_done, dsc_ok, acc_ok = (sem(n) for n in ("gu_done", "silu_ok", "h_ok", "dn_done", "dsc_ok", "acc_ok"))
        s1_done, s1_read = sem("s1_done"), sem("s1_read")
        m_chain, mp_ok, mT_done, mt_ok, md_st, m_ld = (sem(n) for n in ("m_chain", "mp_ok", "mT_done", "mt_ok", "md_st", "m_ld"))
        st_done, exp_ok, pv_done, vst_ok = sem("st_done"), sem("exp_ok"), sem("pv_done"), sem("vst_ok")
        o_ok, lb_done, rl_ok, nrm_ok = sem("o_ok"), sem("lb_done"), sem("rl_ok"), sem("nrm_ok")
        wo_done, wo_read = sem("wo_done"), sem("wo_read")
        out_st = sem("out_st")


        kbf = kbig[:, :].bitcast(F32)
        w4_s = kbf[:, 0:2048].rearrange("p (k n) -> p k n", k=KH)
        w1_s = kbf[:, 2048:4096].rearrange("p (k n) -> p k n", k=KH)
        w2_s = kbf[:, 4096:6144].rearrange("p (c n) -> p c n", c=FC)
        wo_s = kbf[:, 6144:7168].rearrange("p (g n) -> p g n", g=NG)
        wrb_s = kbf[:, 7168:7424].rearrange("p (k n) -> p k n", k=KH)
        b4_s = kbf[:, 7424:7432]
        b1_s = kbf[:, 7432:7440]
        br_s = kbf[:, 7440:7441]
        b2_s = kbf[:, 7448:7704]
        lrow = kbf[:, 8192:8192 + T]
        sel = kbf[:, 10240:14336].rearrange("p (t j) -> p t j", t=NT)
        eq = kbf[:, 14336:16384].rearrange("p (t s) -> p t s", t=NT)
        xn2 = qf[:, 0:4096].rearrange("p (t e) -> p t e", t=NT)
        xnT2 = qf[:, 4096:8192].rearrange("p (k t) -> p k t", k=KH)
        selT = wide[:, 0:2 * T].rearrange("p (k t) -> p k t", k=2)
        junk = wide[:, 0:T]
        rT = wide[:, 2 * T:4 * T].rearrange("p (k t) -> p k t", k=KH)
        hT = vall[:, 0:2048].rearrange("p (c j) -> p c j", c=FC)
        fxT = vall[:, 2048:2560].rearrange("p (k j) -> p k j", k=KH)
        y = vall[:, 2560:3072].rearrange("p (k e) -> p k e", k=2)
        mask = vall[:, 3072:3200]
        slots = vall[:, 3200:3456]
        ones = vall[:, 3456:3584]
        kb_s = [pf[:, 512 * j:512 * (j + 1)] for j in range(2)]
        kv_s, tq_s = pf[:, 1024:1536], pf[:, 1536:2048]
        st_s = [[pf[:, 2048 + 1024 * h + 512 * j:2560 + 1024 * h + 512 * j] for j in range(2)] for h in range(2)]
        gs_s = [vst[:, 4 * j:4 * j + 4, :, :].rearrange("p a b c -> p (a b c)") for j in range(2)]
        lcol = sb("lcol", [P, NT])
        cnt = sb("cnt", [P, 4, NT])
        ew = sb("ew", [P, 3, NT])
        gm = sb("gm", [P, 4])

        tr2_done, xT2_a, xT2_v = sem("tr2_done"), sem("xT2_a"), sem("xT2_v")
        lr_done, lr_ok, lc_done, lc_ok = sem("lr_done"), sem("lr_ok"), sem("lc_done"), sem("lc_ok")
        pj_done, ka_ok, dv_ok, rT_ok = sem("pj_done"), sem("ka_ok"), sem("dv_ok"), sem("rT_ok")
        gm_ok, ew_ok, em_ok, z_done, w_ok = sem("gm_ok"), sem("ew_ok"), sem("em_ok"), sem("z_done"), sem("w_ok")
        sel_ok, fx_done, fx_ok, h1_done, g1_ok = sem("sel_ok"), sem("fx_done"), sem("fx_ok"), sem("h1_done"), sem("g1_ok")
        sT_done, sT_ok, y1_done, y1_ok = sem("sT_done"), sem("sT_ok"), sem("y1_done"), sem("y1_ok")
        rt_done, rt_add, sc_done, y_ok = sem("rt_done"), sem("rt_add"), sem("sc_done"), sem("y_ok")
        xadd_ok, tconst = sem("xadd_ok"), sem("tconst")
        rank_s = sem("rank_s")

        def load_second(sp):
            sp.dma_start(wo_s, wo.rearrange("g p n -> p g n")).then_inc(wo_ld, 16)
            sp.dma_start(wrb_s, wrb.rearrange("(k p) n -> p k n", p=P)).then_inc(w4_ld, 16)
            sp.dma_start(b4_s, b4).then_inc(w4_ld, 16)
            sp.dma_start(br_s, br.partition_broadcast(P)).then_inc(w4_ld, 16)
            sp.dma_start(w4_s, w4.rearrange("(k p) n -> p k n", p=P)).then_inc(w4_ld, 16)
            sp.dma_start(w1_s, w1.rearrange("(k p) n -> p k n", p=P)).then_inc(wf_ld, 16)
            sp.dma_start(w2_s, w2.rearrange("(c p) n -> p c n", p=P)).then_inc(wf_ld, 16)
            sp.dma_start(b1_s, b1).then_inc(wf_ld, 16)
            sp.dma_start(b2_s, b2.partition_broadcast(P)).then_inc(wf_ld, 16)

        def tail_sp(sp):
            for c in range(NB):
                sp.wait_ge(y_ok, TPB * (c + 1))
                sp.dma_start(out[BLK * c:BLK * (c + 1), :].rearrange("(t p) e -> p t e", p=P),
                             xs[:, TPB * c:TPB * (c + 1), :]).then_inc(out_st, 16)
            sp.wait_ge(out_st, 16 * NB)

        def tail_pool(pool):
            pool.wait_ge(pv_done, NIT * NT)
            pool.memset(mask, 1.0).then_inc(tconst, 1)
            pool.wait_ge(tconst, 1)
            pool.affine_select(out=mask, in_=mask, compare_op=ALU.is_gt, fill=0.0, base=0,
                               pattern=[[-1, P]], channel_multiplier=1).then_inc(tconst, 1)
            pool.iota(slots, [[1, SLOTS]], base=0, channel_multiplier=0, allow_small_or_imprecise_dtypes=True).then_inc(tconst, 1)
            pool.memset(ones, 1.0).then_inc(tconst, 1)
            for i in range(NT):
                pool.wait_ge(xn_ok, NT + i + 1)
                pool.tensor_tensor(xs[:, i, :], xs[:, i, :], xn2[:, i, :], ALU.add).then_inc(xadd_ok, 1)

        def tail_pe(pe):
            pe.wait_ge(nrm_ok, NIT)
            pe.wait_ge(wo_ld, 16)

            def project_out(i):
                if i >= 4:
                    pe.wait_ge(wo_read, i - 3)
                for g in range(NG):
                    mm = pe.matmul(ps[:, i % 4, 0:E], outT[:, g, P * i:P * (i + 1)], wo_s[:, g, :],
                                   start=(g == 0), stop=(g == NG - 1))
                mm.then_inc(wo_done, 1)

            def turn(c):
                pe.wait_ge(xn_ok, NT + TPB * (c + 1))
                if c >= 2:
                    pe.wait_ge(xT2_a, c - 1)
                    pe.wait_ge(xT2_v, c - 1)
                for h in range(KH):
                    for j in range(TPB):
                        mm = pe.transpose(ps[:, 4 + 2 * (c % 2) + h, P * j:P * (j + 1)],
                                          xn2[:, TPB * c + j, P * h:P * (h + 1)], ident[:, :])
                    mm.then_inc(tr2_done, 1)

            for c in range(NB):
                for i in range(TPB * c, TPB * (c + 1)):
                    project_out(i)
                if c:
                    turn(c - 1)
            turn(NB - 1)
            pe.wait_ge(w4_ld, 64)
            pe.wait_ge(wo_read, NT)
            for b in range(NB):
                pe.wait_ge(xT2_a, b + 1)
                pe.wait_ge(xT2_v, b + 1)
                for h in range(KH):
                    mm = pe.matmul(ps[:, b, :], wrb_s[:, h, :], xnT2[:, h, BLK * b:BLK * (b + 1)], start=(h == 0), stop=(h == KH - 1))
                mm.then_inc(lr_done, 1)
            pe.wait_ge(lr_ok, NB)
            for i in range(NT):
                mm = pe.transpose(ps[:, 4, i:i + 1], lrow[0:1, P * i:P * (i + 1)], ident[0:1, 0:1])
            mm.then_inc(lc_done, 1)
            for w in range(NB * KH):
                b, h = divmod(w, KH)
                if w == 1:
                    pe.wait_ge(lc_ok, 1)
                if w >= 2:
                    pe.wait_ge(ka_ok, 2 * (w - 1))
                    pe.wait_ge(dv_ok, w - 1)
                for m in range(4):
                    for k in range(KH):
                        mm = pe.matmul(ps[:, 4 * (w % 2) + m, :], w4_s[:, k, E * m + P * h:E * m + P * (h + 1)],
                                       xnT2[:, k, BLK * b:BLK * (b + 1)], start=(k == 0), stop=(k == KH - 1))
                    mm.then_inc(pj_done, 1)
            pe.wait_ge(ka_ok, 4 * NB)
            pe.wait_ge(dv_ok, 2 * NB)
            pe.wait_ge(sel_ok, NT)
            for k in range(KH):
                for i in range(NT):
                    mm = pe.matmul(ps[:, k, 0:SLOTS], xn2[:, i, P * k:P * (k + 1)], sel[:, i, :], start=(i == 0), stop=(i == NT - 1))
                mm.then_inc(fx_done, 1)
            pe.wait_ge(em_ok, 1)
            pe.wait_ge(tconst, 4)
            pe.matmul(ps[:, 7, 0:NT], ones, ew[:, 1, :], start=True, stop=True).then_inc(z_done, 1)

            def turn_sel(n):
                k, c = divmod(n, NB)
                if n == 1:
                    pe.wait_ge(w_ok, 1)
                if n >= 2:
                    pe.wait_ge(sT_ok, n - 1)
                for i in range(TPB):
                    mm = pe.transpose(ps[:, 6 + n % 2, P * i:P * (i + 1)], sel[:, TPB * c + i, P * k:P * (k + 1)], ident[:, :])
                mm.then_inc(sT_done, 1)

            turn_sel(0)
            pe.wait_ge(wf_ld, 64)
            pe.wait_ge(fx_ok, 2)
            for c in range(FC):
                if c >= 4:
                    pe.wait_ge(g1_ok, c - 3)
                for k in range(KH):
                    mm = pe.matmul(ps[:, 2 + c % 4, 0:SLOTS], w1_s[:, k, P * c:P * (c + 1)], fxT[:, k, :], start=(k == 0), stop=(k == KH - 1))
                mm.then_inc(h1_done, 1)
            for n in range(1, 8):
                turn_sel(n)
            pe.wait_ge(g1_ok, FC)
            for k in range(2):
                for c in range(FC):
                    mm = pe.matmul(ps[:, k, 0:E], hT[:, c, P * k:P * (k + 1)], w2_s[:, c, :], start=(c == 0), stop=(c == FC - 1))
                mm.then_inc(y1_done, 1)
            pe.wait_ge(rT_ok, NB * KH)
            for n in range(8):
                if n < 2:
                    pe.wait_ge(sT_ok, 7 + n)
                else:
                    pe.wait_ge(rt_add, n - 1)
                for i in range(2):
                    for h in range(KH):
                        mm = pe.transpose(ps[:, 6 + n % 2, E * i + P * h:E * i + P * (h + 1)],
                                          rT[:, h, P * (2 * n + i):P * (2 * n + i + 1)], ident[:, :])
                mm.then_inc(rt_done, 1)
            pe.wait_ge(y1_ok, 2)
            pe.wait_ge(sT_ok, 8)
            for i in range(NT):
                if i >= 4:
                    pe.wait_ge(y_ok, i - 3)
                for k in range(2):
                    mm = pe.matmul(ps[:, 2 + i % 4, 0:E], selT[:, k, P * i:P * (i + 1)], y[:, k, :], start=(k == 0), stop=(k == 1))
                mm.then_inc(sc_done, 1)

        def tail_act(act):
            for c in range(NB):
                act.wait_ge(var_ok, NB + c + 1)
                act.activation(std[:, TPB * c:TPB * (c + 1)], mv[:, TPB * c:TPB * (c + 1), 1], ACT.Sqrt,
                               bias=epsc[:, :]).then_inc(std_ok, 1)
                if c:
                    take_turned(act, c - 1)
            take_turned(act, NB - 1)
            act.wait_ge(w4_ld, 64)
            for b in range(NB):
                act.wait_ge(lr_done, b + 1)
                act.activation(lrow[:, BLK * b:BLK * (b + 1)], ps[:, b, :], ACT.Identity, bias=br_s).then_inc(lr_ok, 1)
            act.wait_ge(gm_ok, 1)
            act.activation(ew[:, 0, :], lcol[:, :], ACT.Exp, bias=gm[:, 1:2]).then_inc(ew_ok, 1)
            for w in range(NB * KH):
                b, h = divmod(w, KH)
                act.wait_ge(pj_done, 4 * w + 1)
                if w >= 2:
                    act.wait_ge(dv_ok, w - 1)
                act.activation(kb_s[w % 2], ps[:, 4 * (w % 2), :], ACT.Identity, bias=b4_s[:, h:h + 1]).then_inc(ka_ok, 1)
                act.wait_ge(pj_done, 4 * w + 3)
                if w >= 2:
                    act.wait_ge(rT_ok, w - 1)
                act.activation(gs_s[w % 2], ps[:, 4 * (w % 2) + 2, :], ACT.Sigmoid, bias=b4_s[:, 4 + h:5 + h]).then_inc(ka_ok, 1)
            for k in range(KH):
                act.wait_ge(fx_done, k + 1)
                act.activation(fxT[:, k, :], ps[:, k, 0:SLOTS], ACT.Copy).then_inc(fx_ok, 1)

            def take_sel(n):
                k, c = divmod(n, NB)
                act.wait_ge(sT_done, n + 1)
                act.activation(selT[:, k, BLK * c:BLK * (c + 1)], ps[:, 6 + n % 2, :], ACT.Copy).then_inc(sT_ok, 1)

            take_sel(0)
            act.wait_ge(wf_ld, 64)
            for c in range(FC):
                act.wait_ge(h1_done, c + 1)
                act.activation(hT[:, c, :], ps[:, 2 + c % 4, 0:SLOTS], ACT.Gelu, bias=b1_s[:, c:c + 1]).then_inc(g1_ok, 1)
            for n in range(1, 8):
                take_sel(n)

        def take_turned(act, c):
            act.wait_ge(tr2_done, 2 * c + 1)
            act.activation(xnT2[:, 0, BLK * c:BLK * (c + 1)], ps[:, 4 + 2 * (c % 2), :], ACT.Copy).then_inc(xT2_a, 1)

        def tail_dve(dve):
            n_rank = [0]

            def link(ins):
                n_rank[0] += 1
                ins.then_inc(rank_s, 1)
                dve.wait_ge(rank_s, n_rank[0])

            def norm2(c):
                dve.wait_ge(std_ok, NB + c + 1)
                link(dve.reciprocal(rstd[:, TPB * c:TPB * (c + 1)], std[:, TPB * c:TPB * (c + 1)]))
                for i in range(TPB * c, TPB * (c + 1)):
                    dve.tensor_scalar(xn2[:, i, :], xs[:, i, :], mv[:, i, 0:1], rstd[:, i:i + 1],
                                      ALU.subtract, ALU.mult).then_inc(xn_ok, 1)

            def turned(c):
                dve.wait_ge(tr2_done, 2 * c + 2)
                dve.tensor_copy(xnT2[:, 1, BLK * c:BLK * (c + 1)], ps[:, 5 + 2 * (c % 2), :]).then_inc(xT2_v, 1)

            for c in range(NB):
                for i in range(TPB * c, TPB * (c + 1)):
                    dve.wait_ge(wo_done, i + 1)
                    dve.tensor_tensor(xs[:, i, :], ps[:, i % 4, 0:E], xs[:, i, :], ALU.add).then_inc(wo_read, 1)
                dve.wait_ge(wo_read, TPB * (c + 1))
                for i in range(TPB * c, TPB * (c + 1)):
                    ins = dve.bn_stats(stats[:, i, :], xs[:, i, :])
                link(ins)
                for i in range(TPB * c, TPB * (c + 1)):
                    ins = dve.bn_aggr(mv[:, i, :], stats[:, i, :])
                ins.then_inc(var_ok, 1)
                if c:
                    turned_before = c - 2
                    if turned_before >= 0:
                        turned(turned_before)
                norm2(c)
            turned(NB - 2)
            turned(NB - 1)
            dve.wait_ge(lc_done, 1)
            dve.tensor_copy(lcol[:, :], ps[:, 4, 0:NT]).then_inc(lc_ok, 1)
            dve.wait_ge(lr_ok, NB)
            link(dve.tensor_reduce(gm[:, 0:1], lrow, AX.X, ALU.max))
            dve.wait_ge(lc_ok, 1)
            dve.tensor_scalar(gm[:, 1:2], gm[:, 0:1], -1.0, None, ALU.mult).then_inc(gm_ok, 1)
            dve.wait_ge(tconst, 4)
            dve.wait_ge(wo_done, NT)
            dve.memset(cnt[:, 1, 0:1], 0.0)

            def rank(i):
                l = lcol[:, i:i + 1]
                link(dve.tensor_scalar(junk[:, P * i:T], lrow[:, P * i:T], l, 0.0, ALU.is_gt, ALU.add, accum_out=cnt[:, 0, i:i + 1]))
                if i:
                    link(dve.tensor_scalar(junk[:, 0:P * i], lrow[:, 0:P * i], l, 0.0, ALU.is_ge, ALU.add, accum_out=cnt[:, 1, i:i + 1]))
                return dve.tensor_scalar(eq[:, i, :], lrow[:, P * i:P * (i + 1)], l, None, ALU.is_equal)

            for w in range(NB * KH):
                b, h = divmod(w, KH)
                dve.wait_ge(ka_ok, 2 * w + 1)
                dve.wait_ge(pj_done, 4 * w + 2)
                link(dve.scalar_tensor_tensor(out=kv_s, in0=ps[:, 4 * (w % 2) + 1, :], scalar=b4_s[:, 2 + h:3 + h], in1=kb_s[w % 2],
                                              op0=ALU.add, op1=ALU.mult))
                before = 0.0 if b == 0 else st_s[h][(b - 1) % 2][:, BLK - 1:BLK]
                link(dve.tensor_tensor_scan(st_s[h][b % 2], kv_s, kv_s, before, ALU.add, ALU.bypass))
                dve.wait_ge(pj_done, 4 * w + 4)
                dve.scalar_tensor_tensor(out=tq_s, in0=ps[:, 4 * (w % 2) + 3, :], scalar=b4_s[:, 6 + h:7 + h], in1=st_s[h][b % 2],
                                         op0=ALU.add, op1=ALU.mult).then_inc(dv_ok, 1)
                dve.wait_ge(dv_ok, w + 1)
                dve.wait_ge(ka_ok, 2 * w + 2)
                dve.tensor_tensor(rT[:, h, BLK * b:BLK * (b + 1)], tq_s, gs_s[w % 2], ALU.mult).then_inc(rT_ok, 1)
                rank(2 * w)
                ins = rank(2 * w + 1)
            link(ins)
            link(dve.tensor_tensor(eq, eq, mask.unsqueeze(1).to_broadcast([P, NT, P]), ALU.mult))
            link(dve.tensor_reduce(cnt[:, 2, :], eq, AX.X, ALU.add))
            link(dve.tensor_tensor(cnt[:, 3, :], cnt[:, 0, :], cnt[:, 1, :], ALU.add))
            link(dve.tensor_tensor(cnt[:, 3, :], cnt[:, 3, :], cnt[:, 2, :], ALU.add))
            for i in range(NT):
                dve.tensor_scalar(sel[:, i, :], slots, cnt[:, 3, i:i + 1], None, ALU.is_equal).then_inc(sel_ok, 1)
            dve.wait_ge(ew_ok, 1)
            dve.scalar_tensor_tensor(out=ew[:, 1, :], in0=cnt[:, 3, :], scalar=SLOTS - 0.5, in1=ew[:, 0, :],
                                     op0=ALU.is_lt, op1=ALU.mult).then_inc(em_ok, 1)
            dve.wait_ge(z_done, 1)
            link(dve.tensor_reduce(gm[:, 2:3], ps[:, 7, 0:NT], AX.X, ALU.add))
            link(dve.reciprocal(gm[:, 3:4], gm[:, 2:3]))
            dve.tensor_scalar(ew[:, 2, :], ew[:, 1, :], gm[:, 3:4], None, ALU.mult).then_inc(w_ok, 1)
            dve.wait_ge(wf_ld, 64)
            for k in range(2):
                dve.wait_ge(y1_done, k + 1)
                dve.tensor_tensor(y[:, k, :], ps[:, k, 0:E], b2_s, ALU.add).then_inc(y1_ok, 1)
            dve.wait_ge(xadd_ok, NT)
            for n in range(8):
                dve.wait_ge(rt_done, n + 1)
                xc = xs[:, 2 * n:2 * n + 2, :]
                dve.tensor_tensor(xc, ps[:, 6 + n % 2, :].rearrange("p (t e) -> p t e", t=2), xc, ALU.add).then_inc(rt_add, 1)
            dve.wait_ge(rt_add, 8)
            dve.wait_ge(w_ok, 1)
            for i in range(NT):
                dve.wait_ge(sc_done, i + 1)
                dve.scalar_tensor_tensor(out=xs[:, i, :], in0=ps[:, 2 + i % 4, 0:E], scalar=ew[:, 2, i:i + 1], in1=xs[:, i, :],
                                         op0=ALU.mult, op1=ALU.add).then_inc(y_ok, 1)

        mturn = ps[:, 5, 0:P // 2].bitcast(BF16)
        mbank = mturn[0:3 * HG * TPB, :]

        def rot(b):
            return tmp[:, 0:2, :, :].rearrange("p j a n -> p (j a) n")

        block = ctx.enter_context(nc.Block())

        def chain(eng, s, start=0):
            n = [start]

            def link(ins):
                n[0] += 1
                ins.then_inc(s, 1)
                eng.wait_ge(s, n[0])
            return link

        def is_first(it):
            return isinstance(it, int) and it == 0

        def q_slot(it, rows, h, off, n):
            return qring[0:rows, bass.ds((it & (QRING - 1)) * (HG * BLK) + (h * BLK + off), n)]

        def k_part(it, rows, h, off, n):
            return kbig[0:rows, bass.ds((it & GMASK) * T + (h * T + off), n)]

        @block.sync
        def _(sp):
            for c in range(NB):
                sp.dma_start(xs[:, TPB * c:TPB * (c + 1), :],
                             x[BLK * c:BLK * (c + 1), :].rearrange("(t p) e -> p t e", p=P)).then_inc(x_ld[c], 16)
            sp.dma_start(cos_s, cosT).then_inc(tab_ld, 16)
            sp.dma_start(sin_s, sinT).then_inc(tab_ld, 16)

            def load_expert(e, j, free=None):
                if free is not None:
                    sp.wait_ge(dn_done, free)
                sp.dma_start(wgu_s[j], wgu[bass.ds(e, 1), :, :].rearrange("a (k p) n -> p (a k) n", p=P)).then_inc(we_ld[j], 16)
                sp.dma_start(wdn_s[j], wdn[bass.ds(e, 1), :, :].rearrange("a p n -> p (a n)")).then_inc(we_ld[j], 16)

            load_expert(0, 0)
            load_expert(1, 1)
            for b in range(NB):
                sp.wait_ge(hi_ok, b + 1)
                sp.wait_ge(mid_ok, b + 1)
                sp.wait_ge(lo_ok, b + 1)
                for s in range(3):
                    for a in range(4):
                        sp.dma_start(parts_d[a % 2, s, :, a // 2, :, BLK * b:BLK * (b + 1)],
                                     prt[:, b % 2, s, a, :]).then_inc(part_st[b % 2], 16)
            for j in range(2):
                sp.wait_ge(part_st[j], 16 * 12 * 2)

            def load_k(g):
                for r, part in enumerate(KROWS):
                    sp.dma_start(K[16 * r:16 * r + 16, HG * g:HG * (g + 1), :],
                                 parts_d[1, part, HG * g:HG * (g + 1)].rearrange("h s i n -> (s i) h n")).then_inc(k_ld[g], 16)

            def load_q(L, free=None):
                slot, head, col = (L & (QRING - 1)) * (HG * BLK), L & GMASK, (L & 3) * BLK
                if free is not None:
                    sp.wait_ge(st_done, free)
                for r, part in enumerate(QROWS):
                    dst = qring[16 * r:16 * r + 16, bass.ds(slot, HG * BLK)]
                    src = parts_d[0, part, bass.ds(head, HG), :, :, bass.ds(col, BLK)]
                    sp.dma_start(dst.rearrange("p (h n) -> p h n", h=HG),
                                 src.rearrange("h s i n -> (s i) h n")).then_inc(q_ld, 16)

            load_k(0)
            for L in range(QRING):
                load_q(L)
                sp.wait_ge(q_ld, 96 * (L + 1))
            for g in range(1, NG):
                load_k(g)

            for pr in range(NEX // 2 - 1):
                for j in range(2):
                    load_expert(pr * 2 + (2 + j), j, free=pr * 16 + 8 * (j + 1))

            def store_max(L):
                dst = qring[CROWS:CROWS + MROWS, bass.ds((L & (QRING - 1)) * (HG * BLK), HG * BLK)]
                sp.wait_ge(mt_ok, L + 1)
                sp.dma_start(max_d[bass.ds(L, 1), :, :].rearrange("a r p -> (a r) p"), mt[:, :]).then_inc(md_st, 16)
                sp.wait_ge(md_st, L * 16 + 16)
                sp.dma_start(dst, max_d[bass.ds(L, 1), :, :].rearrange("a (s r) p -> (a s) (r p)", s=3)).then_inc(m_ld, 16)

            for L in range(NB):
                store_max(L)
                sp.wait_ge(m_ld, 16 * (L + 1))
            for it in range(1, 9):
                load_q(it + 7, free=it * 32)
                sp.wait_ge(q_ld, it * 96 + 96 * 8)
                store_max(it + 3)
                sp.wait_ge(m_ld, it * 16 + 64)
            load_second(sp)
            for it in range(9, 13):
                store_max(it + 3)
                sp.wait_ge(m_ld, it * 16 + 64)
            tail_sp(sp)

        @block.gpsimd
        def _(pool):
            link = chain(pool, pool_s)
            pool.memset(ident[:, :], 0.0).then_inc(ids, 1)
            pool.wait_ge(ids, 1)
            pool.affine_select(out=ident[:, :], in_=ident[:, :], compare_op=ALU.not_equal, fill=1.0, base=0,
                               pattern=[[-1, P]], channel_multiplier=1).then_inc(ids, 1)
            pool.wait_ge(ids, 2)
            pool.tensor_copy(identb[:, :], ident[:, :]).then_inc(ids, 1)
            link(pool.memset(selb[:, :], 0.0))
            pool.affine_select(out=selb[:, :].rearrange("p (g j) -> p g j", g=HG),
                               in_=selb[:, :].rearrange("p (g j) -> p g j", g=HG), compare_op=ALU.not_equal, fill=1.0,
                               base=-HD, pattern=[[-32, HG], [0, 32]], channel_multiplier=1).then_inc(consts, 1)
            vv = vall[:, :].rearrange("p (c d) -> p c d", d=HD + 1)
            pool.memset(vv[:, :, HD:HD + 1], 1.0).then_inc(consts, 1)

            for b in range(NB):
                pool.wait_ge(qk_ok, 4 * (b + 1))
                pool.wait_ge(tab_ld, 32)
                if b:
                    pool.wait_ge(r_ok, 2 * b)
                c = cos_s[:, BLK * b:BLK * (b + 1)]
                s = sin_s[:, BLK * b:BLK * (b + 1)]
                pool.tensor_tensor(tmp[:, 2, :, :], qk[:, b % 2, 2:4, :], c.unsqueeze(1).to_broadcast([P, 2, BLK]), ALU.mult).then_inc(rope_p, 1)
                pool.tensor_tensor(tmp[:, 3, :, :], qk[:, b % 2, 0:2, :], s.unsqueeze(1).to_broadcast([P, 2, BLK]), ALU.mult).then_inc(rope_p, 1)
            pool.wait_ge(xn_ok, NT)
            pool.wait_ge(wv_ld, 48)
            for c in range(NB):
                xc = xs[:, TPB * c:TPB * (c + 1), :]
                pool.tensor_tensor(xc, xc, bo_s.unsqueeze(1).to_broadcast([P, TPB, E]), ALU.add).then_inc(acc_ok, 1)
            pool.wait_ge(lo_ok, NB)
            pool.wait_ge(acc_ok, NB)
            pool.memset(kbig[CROWS:P, :].bitcast(F32), TWO_ONES).then_inc(ones_ok, 1)
            pool.wait_ge(ones_ok, 1)

            with pool.Fori(0, NEX // 2) as pr:
                for k in range(8):
                    b = k % NB
                    pool.wait_ge(dsc_ok, pr * 8 + k + 1)
                    pool.wait_ge(acc_ok, pr * 8 + k + 1)
                    xc = xs[:, TPB * b:TPB * (b + 1), :]
                    pool.tensor_tensor(xc, xc, dsc[k % 2], ALU.add).then_inc(acc_ok, 1)

            v4 = vall[:, :].rearrange("p (t n) -> p t n", t=NT)
            pool.wait_ge(dn_done, 2 * 4 * NEX)
            pool.wait_ge(v_ok, NT)
            link(pool.memset(vst[:, :, :, :], 0.0))

            def stage_v(it, kt):
                src = v4[:, kt, bass.ds((it & GMASK) * (HD + 1), HG * (HD + 1))]
                pool.tensor_copy(vst[:, kt, :, 0:HD + 1], src.rearrange("p (h d) -> p h d", h=HG)).then_inc(vst_ok, 1)

            for kt in range(NT):
                stage_v(0, kt)
            with pool.Fori(1, NIT) as it:
                for kt in range(NT):
                    pool.wait_ge(pv_done, it * 16 + (kt - 15))
                    stage_v(it, kt)
            tail_pool(pool)

        @block.tensor
        def _(pe):
            pe.wait_ge(ids, 3)
            for c in range(NB):
                pe.wait_ge(xn_ok, TPB * (c + 1))
                for h in range(KH):
                    for j in range(TPB):
                        mm = pe.transpose(ps[:, 2 * c + h, P * j:P * (j + 1)], xn[:, TPB * c + j, P * h:P * (h + 1)], ident[:, :])
                    mm.then_inc(tr_done, 1)
            pe.wait_ge(wqk_ld, 32)
            for n in range(4 * NB):
                b, a = divmod(n, 4)
                c = max(b, n // 2 if n < 8 else NB - 1)
                pe.wait_ge(xT_a, c + 1)
                pe.wait_ge(xT_v, c + 1)
                if n >= 8:
                    pe.wait_ge(qk_ok, n - 7)
                for h in range(KH):
                    mm = pe.matmul(ps[:, n % 8, :], wqk_s[:, h, P * a:P * (a + 1)], xnT[:, h, BLK * b:BLK * (b + 1)],
                                   start=(h == 0), stop=(h == KH - 1))
                mm.then_inc(qk_done, 1)
            pe.wait_ge(wv_ld, 48)
            for i in range(NT):
                if i < 8:
                    pe.wait_ge(qk_ok, i + 9)
                else:
                    pe.wait_ge(v_ok, i - 7)
                for h in range(KH):
                    mm = pe.matmul(ps[:, i % 8, 0:E + NEX], xnT[:, h, P * i:P * (i + 1)], wvr_s[:, h, :],
                                   start=(h == 0), stop=(h == KH - 1))
                mm.then_inc(v_done, 1)

            def pass1(n0, lhs, it, h):
                for kb in range(NB):
                    pe.wait_ge(s1_read, n0 + (kb + 1))
                    pe.matmul(ps[:, 6 + kb % 2, :], lhs, k_part(it, CROWS, h, BLK * kb, BLK),
                              start=True, stop=True).then_inc(s1_done, 1)

            def expert_down(u, k, j):
                pe.wait_ge(h_ok, u + 3)
                pe.wait_ge(acc_ok, u + 4)
                for i in range(TPB):
                    mm = pe.matmul(ps[:, 4 + i // 2, E * (i % 2):E * (i % 2 + 1)], hb[k % 2][:, P * i:P * (i + 1)], wdn_s[j],
                                   start=True, stop=True)
                    if i % 2:
                        mm.then_inc(dn_done, 1)

            pe.wait_ge(v_ok, NT)
            with pe.Fori(0, NEX // 2) as pr:
                for k in range(8):
                    j, b = divmod(k, NB)
                    if b == 0:
                        pe.wait_ge(we_ld[j], pr * 32 + 32)
                    pe.wait_ge(h_ok, pr * 8 + k + 1)
                    for w in range(2):
                        for h in range(KH):
                            mm = pe.matmul(ps[:, 2 * (k % 2) + w, :], wgu_s[j][:, h, P * w:P * (w + 1)],
                                           xnT[:, h, BLK * b:BLK * (b + 1)], start=(h == 0), stop=(h == KH - 1))
                    mm.then_inc(gu_done, 1)
                    if k:
                        expert_down(pr * 8 + (k - 1), k - 1, (k - 1) // NB)
                    if k == 0:
                        pe.wait_ge(k_ld[0], 96)
                    pe.wait_ge(q_ld, 96 * (k // 2 + 1))
                    for i in range(2):
                        off = P * ((2 * k + i) % TPB)
                        lhs = qring[0:CROWS, bass.ds(pr * BLK + (k // 2) * HG * BLK + off, P)]
                        for kb in range(NB):
                            pe.wait_ge(s1_read, pr * 64 + (8 * k + 4 * i + kb + 1))
                            pe.matmul(ps[:, 6 + kb % 2, :], lhs, kbig[0:CROWS, bass.ds(pr * T + BLK * kb, BLK)],
                                      start=True, stop=True).then_inc(s1_done, 1)
                expert_down(pr * 8 + 7, 7, 1)

            def max_transpose(L):
                pe.wait_ge(mp_ok, L + 1)
                pe.transpose(mturn, mpad[:, :], identb[:, :]).then_inc(mT_done, 1)

            pe.wait_ge(dsc_ok, 4 * NEX)
            for L in range(NB):
                if L:
                    pe.wait_ge(mt_ok, L)
                max_transpose(L)

            def scores(it, kt):
                U2 = it * 32 + 2 * kt
                first = isinstance(it, int) and it == 0 and kt == 0
                if kt == 0:
                    pe.wait_ge(m_ld, it * 16 + 16)
                    pe.wait_ge(q_ld, it * 96 + 96)
                for p in range(2):
                    if not first:
                        pe.wait_ge(exp_ok, U2 + (p - 1))
                    for h in (2 * p, 2 * p + 1):
                        mm = pe.matmul(ps[:, h, :], k_part(it, CROWS + MROWS, h, P * kt, P),
                                       q_slot(it, CROWS + MROWS, h, 0, BLK), start=True, stop=True)
                    mm.then_inc(st_done, 1)

            def values(it, kt):
                pe.wait_ge(exp_ok, it * 32 + (2 * kt + 2))
                pe.wait_ge(vst_ok, it * 16 + (kt + 1))
                if kt == 0 and not is_first(it):
                    pe.wait_ge(o_ok, it)
                for h in range(HG):
                    mm = pe.matmul(ps[32 * h:32 * h + 32, 4, :], vst[:, kt, h, :], prob[:, kt % 2, BLK * h:BLK * (h + 1)],
                                   start=(kt == 0), stop=(kt == NT - 1))
                mm.then_inc(pv_done, 1)

            def spread_den(it):
                pe.wait_ge(o_ok, it + 1)
                if not is_first(it):
                    pe.wait_ge(rl_ok, it)
                pe.matmul(ps[:, 5, :], selb[:, :], osb[:, :], start=True, stop=True).then_inc(lb_done, 1)

            def iteration(it, first, pass_1, last, max_before):
                for kt in range(NT):
                    if kt < NT - 1:
                        scores(it, kt + 1)
                    elif not last:
                        scores(it + 1, 0)
                    if kt == 2 and not first:
                        pe.wait_ge(mt_ok, it + 3 if max_before else NIT)
                        spread_den(it - 1)
                    if kt == 4 and max_before:
                        pe.wait_ge(rl_ok, it)
                        max_transpose(it + 3)
                    if pass_1:
                        h, i = divmod(kt, TPB)
                        if kt == 0:
                            pe.wait_ge(q_ld, it * 96 + 480)
                        pass1(it * 64 + (256 + 4 * kt), q_slot(it + 4, CROWS, h, P * i, P), it + 4, h)
                    values(it, kt)

            for g in range(NG):
                pe.wait_ge(k_ld[g], 96)
            pe.wait_ge(consts, 2)
            pe.wait_ge(ones_ok, 1)
            pe.wait_ge(mt_ok, NB)
            scores(0, 0)
            iteration(0, True, True, False, False)
            with pe.Fori(1, 12) as it:
                iteration(it, False, True, False, True)
            iteration(12, False, False, False, True)
            with pe.Fori(13, 15) as it:
                iteration(it, False, False, False, False)
            iteration(15, False, False, True, False)
            spread_den(15)
            tail_pe(pe)

        @block.scalar
        def _(act):
            act.dma_start(wqk_s, wqk.rearrange("(k p) n -> p k n", p=P)).then_inc(wqk_ld, 16)
            act.dma_start(bqk_s[:, :], bqk).then_inc(wqk_ld, 16)
            act.dma_start(wvr_s, wvr.rearrange("(k p) n -> p k n", p=P)).then_inc(wv_ld, 16)
            act.dma_start(bv_s, bv.partition_broadcast(P)).then_inc(wv_ld, 16)
            act.dma_start(bo_s, bo.partition_broadcast(P)).then_inc(wv_ld, 16)
            for c in range(NB):
                act.wait_ge(var_ok, c + 1)
                act.activation(std[:, TPB * c:TPB * (c + 1)], mv[:, TPB * c:TPB * (c + 1), 1], ACT.Sqrt,
                               bias=epsc[:, :]).then_inc(std_ok, 1)
            for c in range(NB):
                act.wait_ge(tr_done, 2 * c + 1)
                act.activation(xnT[:, 0, BLK * c:BLK * (c + 1)], ps[:, 2 * c, :], ACT.Copy).then_inc(xT_a, 1)

            def split(b):
                act.wait_ge(r_ok, 2 * b + 2)
                if b >= 2:
                    act.wait_ge(part_st[b % 2], 192)
                act.activation(prt[:, b % 2, 0, :, :], rot(b), ACT.Copy).then_inc(hi_ok, 1)
                act.wait_ge(rem_ok, b + 1)
                act.activation(prt[:, b % 2, 1, :, :], rem[:, :, :], ACT.Copy).then_inc(mid_ok, 1)

            act.wait_ge(wqk_ld, 32)
            for b in range(NB):
                for a in range(4):
                    n = 4 * b + a
                    act.wait_ge(qk_done, n + 1)
                    if b >= 2:
                        act.wait_ge(lo_ok, b - 1)
                    act.activation(qk[:, b % 2, a, :], ps[:, n % 8, :], ACT.Identity, bias=bqk_s[:, a:a + 1]).then_inc(qk_ok, 1)
                if b:
                    split(b - 1)
            split(NB - 1)
            act.wait_ge(lgx_ok, 1)
            act.activation(rt[:, 1, :, :], rt[:, 0, :, :], ACT.Exp).then_inc(ex_ok, 1)

            def silu(u, k):
                act.wait_ge(gu_done, u + 1)
                act.wait_ge(h_ok, u + 1)
                act.activation(sg[k % 2], ps[:, 2 * (k % 2), :], ACT.Silu).then_inc(silu_ok, 1)

            def scaled(u, k, e):
                act.wait_ge(acc_ok, u + 3)
                for i in range(TPB):
                    if i % 2 == 0:
                        act.wait_ge(dn_done, u * 2 + (i // 2 + 1))
                    t = TPB * (k % NB) + i
                    ins = act.activation(dsc[k % 2][:, i, :], ps[:, 4 + i // 2, E * (i % 2):E * (i % 2 + 1)], ACT.Copy,
                                         scale=wtok[:, bass.ds(e, 1), t])
                ins.then_inc(dsc_ok, 1)

            act.wait_ge(wt_ok, 1)
            with act.Fori(0, NEX // 2) as pr:
                for k in range(8):
                    silu(pr * 8 + k, k)
                    if k:
                        scaled(pr * 8 + (k - 1), k - 1, pr * 2 + (k - 1) // NB)
                scaled(pr * 8 + 7, 7, pr * 2 + 1)

            def exps(it, kt, p):
                act.wait_ge(st_done, it * 32 + (2 * kt + p + 1))
                if not is_first(it) or kt >= 2:
                    act.wait_ge(pv_done, it * 16 + (kt - 1))
                act.activation(prob[:, kt % 2, 2 * BLK * p:2 * BLK * (p + 1)].rearrange("p (a n) -> p a n", a=2), ps[:, 2 * p:2 * p + 2, :], ACT.Exp,
                               scale=SCALE).then_inc(exp_ok, 1)

            def take_sums(it):
                act.wait_ge(pv_done, it * 16 + 16)
                if not is_first(it):
                    act.wait_ge(nrm_ok, it)
                act.activation(osb[:, :], ps[:, 4, :], ACT.Copy).then_inc(o_ok, 1)

            act.wait_ge(acc_ok, 4 * NEX + 4)
            for kt in range(NT):
                exps(0, kt, 0)
                exps(0, kt, 1)
            take0 = [True]

            def iteration(it):
                for kt in range(NT):
                    exps(it, kt, 0)
                    if kt == 0:
                        if take0[0]:
                            act.wait_ge(pv_done, it * 16)
                            act.activation(osb[:, :], ps[:, 4, :], ACT.Copy).then_inc(o_ok, 1)
                        else:
                            take_sums(it - 1)
                    exps(it, kt, 1)

            iteration(1)
            take0[0] = False
            with act.Fori(2, NIT) as it:
                iteration(it)
            take_sums(NIT - 1)
            tail_act(act)

        @block.vector
        def _(dve):
            link = chain(dve, dve_s)
            dve.memset(mpad[:, :], 0.0)
            link(dve.memset(epsc[:, :], EPS))
            for c in range(NB):
                dve.wait_ge(x_ld[c], 16)
                for i in range(TPB * c, TPB * (c + 1)):
                    ins = dve.bn_stats(stats[:, i, :], xs[:, i, :])
                link(ins)
                for i in range(TPB * c, TPB * (c + 1)):
                    ins = dve.bn_aggr(mv[:, i, :], stats[:, i, :])
                ins.then_inc(var_ok, 1)
            for c in range(NB):
                dve.wait_ge(std_ok, c + 1)
                link(dve.reciprocal(rstd[:, TPB * c:TPB * (c + 1)], std[:, TPB * c:TPB * (c + 1)]))
                for i in range(TPB * c, TPB * (c + 1)):
                    dve.tensor_scalar(xn[:, i, :], xs[:, i, :], mv[:, i, 0:1], rstd[:, i:i + 1],
                                      ALU.subtract, ALU.mult).then_inc(xn_ok, 1)
            for c in range(NB):
                dve.wait_ge(tr_done, 2 * c + 2)
                dve.tensor_copy(xnT[:, 1, BLK * c:BLK * (c + 1)], ps[:, 2 * c + 1, :]).then_inc(xT_v, 1)

            def rotate(b):
                dve.wait_ge(qk_ok, 4 * (b + 1))
                dve.wait_ge(tab_ld, 32)
                if b:
                    dve.wait_ge(hi_ok, b)
                c = cos_s[:, BLK * b:BLK * (b + 1)].unsqueeze(1).to_broadcast([P, 2, BLK])
                s = sin_s[:, BLK * b:BLK * (b + 1)].unsqueeze(1).to_broadcast([P, 2, BLK])
                dve.tensor_tensor(tmp[:, 0, :, :], qk[:, b % 2, 0:2, :], c, ALU.mult)
                link(dve.tensor_tensor(tmp[:, 1, :, :], qk[:, b % 2, 2:4, :], s, ALU.mult))
                dve.tensor_tensor(tmp[:, 0, :, :], tmp[:, 0, :, :], tmp[:, 1, :, :], ALU.subtract).then_inc(r_ok, 1)
                dve.wait_ge(rope_p, 2 * b + 2)
                dve.wait_ge(r_ok, 2 * b + 1)
                dve.tensor_tensor(tmp[:, 1, :, :], tmp[:, 2, :, :], tmp[:, 3, :, :], ALU.add).then_inc(r_ok, 1)

            def split(b):
                dve.wait_ge(hi_ok, b + 1)
                dve.wait_ge(r_ok, 2 * b + 2)
                dve.tensor_tensor(rem[:, :, :], rot(b), prt[:, b % 2, 0, :, :], ALU.subtract).then_inc(rem_ok, 1)

            def low(b):
                dve.wait_ge(mid_ok, b + 1)
                dve.wait_ge(rem_ok, b + 1)
                dve.tensor_tensor(prt[:, b % 2, 2, :, :], rem[:, :, :], prt[:, b % 2, 1, :, :], ALU.subtract).then_inc(lo_ok, 1)

            def take_v(i):
                dve.wait_ge(v_done, i + 1)
                dst = vall[:, i * NH * (HD + 1):(i + 1) * NH * (HD + 1)].rearrange("p (h d) -> p h d", h=NH)[:, :, 0:HD]
                dve.tensor_tensor(dst, ps[:, i % 8, 0:E].rearrange("p (h d) -> p h d", h=NH),
                                  bv_s.rearrange("p (h d) -> p h d", h=NH), ALU.add)
                dve.tensor_copy(lg[:, i, :], ps[:, i % 8, E:E + NEX]).then_inc(v_ok, 1)

            for b in range(NB):
                rotate(b)
                split(b)
                if b == NB - 1:
                    dve.wait_ge(wv_ld, 48)
                    for i in range(8):
                        take_v(i)
                low(b)
            for i in range(8, NT):
                take_v(i)

            dve.wait_ge(v_ok, NT)
            link(dve.tensor_reduce(rs[:, 0, :], lg[:, :, :], AX.X, ALU.max))
            dve.tensor_tensor(rt[:, 0, :, :], lg[:, :, :], rs[:, 0, :].unsqueeze(2).to_broadcast([P, NT, NEX]), ALU.subtract).then_inc(lgx_ok, 1)
            dve.wait_ge(ex_ok, 1)
            link(dve.tensor_reduce(rs[:, 1, :], rt[:, 1, :, :], AX.X, ALU.add))
            link(dve.reciprocal(rs[:, 2, :], rs[:, 1, :]))
            link(dve.tensor_tensor(rt[:, 2, :, :], rt[:, 1, :, :], rs[:, 2, :].unsqueeze(2).to_broadcast([P, NT, NEX]), ALU.mult))
            for e in range(NEX):
                mine = rt[:, 2, :, e:e + 1]
                ins = dve.tensor_tensor(cmp[:, e, :, 0:e + 1], mine.to_broadcast([P, NT, e + 1]), rt[:, 2, :, 0:e + 1], ALU.is_gt)
                if e < NEX - 1:
                    ins = dve.tensor_tensor(cmp[:, e, :, e + 1:], mine.to_broadcast([P, NT, NEX - 1 - e]), rt[:, 2, :, e + 1:], ALU.is_ge)
            link(ins)
            link(dve.tensor_reduce(rt[:, 0, :, :], cmp.rearrange("p a t e -> p t e a"), AX.X, ALU.add))
            link(dve.scalar_tensor_tensor(out=rt[:, 3, :, :], in0=rt[:, 0, :, :], scalar=1.5, in1=rt[:, 2, :, :],
                                          op0=ALU.is_lt, op1=ALU.mult))
            link(dve.tensor_reduce(rs[:, 3, :], rt[:, 3, :, :], AX.X, ALU.add))
            link(dve.reciprocal(rs[:, 0, :], rs[:, 3, :]))
            dve.tensor_tensor(wtok[:, :, :].rearrange("p e t -> p t e"), rt[:, 3, :, :],
                              rs[:, 0, :].unsqueeze(2).to_broadcast([P, NT, NEX]), ALU.mult).then_inc(wt_ok, 1)
            dve.wait_ge(wt_ok, 1)
            dve.memset(mneg[:, :], 0.0).then_inc(h_ok, 2)
            dve.memset(mres[:, :], 0.0).then_inc(s1_read, 2)

            def row_max(n, dst, bank):
                dve.wait_ge(s1_done, n)
                dve.tensor_reduce(dst, ps[:, bank, :], AX.X, ALU.max).then_inc(s1_read, 1)

            with dve.Fori(0, NEX // 2) as pr:
                for k in range(8):
                    dve.wait_ge(silu_ok, pr * 8 + k + 1)
                    dve.tensor_tensor(hb[k % 2], sg[k % 2], ps[:, 2 * (k % 2) + 1, :], ALU.mult).then_inc(h_ok, 1)
                    for r in range(8):
                        row_max(pr * 64 + (8 * k + r + 1), mraw[:, bass.ds(pr * 64 + (8 * k + r), 1)], 6 + r % 2)

            def max_parts(L, src):
                def step(j, ins):
                    ins.then_inc(m_chain, 1)
                    dve.wait_ge(m_chain, L * 5 + j)
                step(1, dve.tensor_reduce(mres[:, :].rearrange("p (h t) -> p h t", h=HG), src, AX.X, ALU.max))
                step(2, dve.tensor_scalar(mneg[:, :], mres[:, :], -1.0, None, ALU.mult))
                step(3, dve.tensor_copy(mpart[:, 0, :], mneg[:, :]))
                step(4, dve.tensor_tensor(mres[:, :], mneg[:, :], mpart[:, 0, :], ALU.subtract))
                step(5, dve.tensor_copy(mpart[:, 1, :], mres[:, :]))
                dve.tensor_tensor(mpart[:, 2, :], mres[:, :], mpart[:, 1, :], ALU.subtract).then_inc(mp_ok, 1)

            def take_max(L):
                dve.wait_ge(mT_done, L + 1)
                if not is_first(L):
                    dve.wait_ge(md_st, L * 16)
                dve.tensor_copy(mt[:, :], mbank).then_inc(mt_ok, 1)

            dve.wait_ge(s1_read, 256 + 2)
            m4 = mraw[:, :].rearrange("p (h b t k) -> p h b t k", h=HG, b=NB, t=TPB)
            for L in range(NB):
                if L:
                    dve.wait_ge(mT_done, L)
                max_parts(L, m4[:, :, L, :, :])
                take_max(L)

            mit = mraw[:, 0:HG * TPB * NB].rearrange("p (h t k) -> p h t k", h=HG, t=TPB)

            def normalise(it):
                dve.wait_ge(lb_done, it + 1)
                dve.reciprocal(rl[:, :], ps[:, 5, :]).then_inc(rl_ok, 1)
                dve.wait_ge(rl_ok, it + 1)
                dve.tensor_tensor(wide[:, bass.ds((it & GMASK) * (T // HG) + (it & 3) * BLK, BLK)], osb[:, :], rl[:, :], ALU.mult).then_inc(nrm_ok, 1)

            def iteration(it, first, pass_1, max_before):
                if max_before:
                    dve.wait_ge(s1_read, it * 64 + 258)
                    max_parts(it + 3, mit)
                for kt in range(NT):
                    if pass_1:
                        for kb in range(NB):
                            c = 4 * kt + kb
                            row_max(it * 64 + (256 + c + 1), mraw[:, c:c + 1], 6 + kb % 2)
                    if kt == 1 and not first:
                        normalise(it - 1)
                    if kt == 3 and max_before:
                        take_max(it + 3)

            iteration(0, True, True, False)
            with dve.Fori(1, 12) as it:
                iteration(it, False, True, True)
            iteration(12, False, False, True)
            with dve.Fori(13, 16) as it:
                iteration(it, False, False, False)
            normalise(15)
            tail_dve(dve)


def kernel(**inputs):
    import concourse.bacc as bacc
    from concourse.bass_utils import run_bass_kernel_spmd as run

    a = {k: np.asarray(v) for k, v in inputs.items()}
    c = np.ascontiguousarray
    half = HD // 2
    rows = [np.array([h * HD + s * half + i for h in range(NH) for i in range(half)]) for s in range(2)]
    wq, wk = a["L0_attn_Wq"], a["L0_attn_Wk"]
    bq, bk = a["L0_attn_bq"], a["L0_attn_bk"]
    wqk = c(np.concatenate([wq[rows[0]], wk[rows[0]], wq[rows[1]], wk[rows[1]]]).T)
    bqk = c(np.stack([bq[rows[0]], bk[rows[0]], bq[rows[1]], bk[rows[1]]], axis=1))
    freq = (np.float32(1.0) / np.float32(10000.0) ** (np.arange(0, HD, 2, dtype=np.float32) / np.float32(HD))).astype(np.float32)
    angle = (np.arange(T, dtype=np.float32)[None, :] * freq[:, None]).astype(np.float32)
    cosT = c(np.tile(np.cos(angle).astype(np.float32), (NH, 1)))
    sinT = c(np.tile(np.sin(angle).astype(np.float32), (NH, 1)))
    wvr = c(np.concatenate([a["L0_attn_Wv"], a["L0_ffn_router_gate"]]).T)
    gu = a["L0_ffn_expert_gate_up"]
    wgu = c(np.concatenate([gu[:, :, 0::2], gu[:, :, 1::2]], axis=2))
    woT = np.zeros((NG, HG, 32, E), np.float32)
    woT[:, :, :HD, :] = a["L0_attn_Wo"].T.reshape(NG, HG, HD, E)
    four = ("k", "v", "g", "q")
    w4 = c(np.concatenate([a["L1_attn_W" + m] for m in four]).T)
    b4 = c(np.concatenate([a["L1_attn_b" + m].reshape(KH, P) for m in four]).T)
    feeds = dict(
        x=c(a["L0_attn_hidden_states"][0]), wqk=wqk, bqk=bqk, cosT=cosT, sinT=sinT, wvr=wvr, bv=a["L0_attn_bv"], bo=a["L0_attn_bo"],
        wgu=wgu, wdn=c(a["L0_ffn_expert_down"]), wo=woT.reshape(NG, P, E), w4=w4, b4=b4,
        wrb=c(np.tile(a["L1_ffn_Wr"], (1, P))), br=a["L1_ffn_br"], w1=a["L1_ffn_W1"], b1=c(a["L1_ffn_b1"].reshape(FC, P).T),
        w2=a["L1_ffn_W2"], b2=a["L1_ffn_b2"])
    nc = bacc.Bacc("TRN2", target_bir_lowering=False, num_devices=1)
    arrays = {f"in_{k}": c(v) for k, v in feeds.items()}
    aps = {k: nc.dram_tensor(f"in_{k}", feeds[k].shape, mybir.dt.from_np(feeds[k].dtype), kind="ExternalInput").ap() for k in feeds}
    out = nc.dram_tensor("out_0", (T, E), F32, kind="ExternalOutput").ap()
    program(nc, out=out, **aps)
    r = run(nc, [arrays], core_ids=[0])
    return r.results[0]["out_0"].reshape(1, T, E)
```

```python
from contextlib import ExitStack

import numpy as np

import concourse.bass as bass
from concourse import mybir

F32 = mybir.dt.float32
BF16 = mybir.dt.bfloat16
ALU = mybir.AluOpType
ACT = mybir.ActivationFunctionType
AX = mybir.AxisListType

P = 128
T, E = 2048, 256
NT = T // P
BLK = 512
NB = T // BLK
TPB = BLK // P
KH = E // P
NH, HD = 16, 16
HG = 4
NG = NH // HG
QROWS = [0, 0, 1, 1, 0, 2]
KROWS = [0, 1, 0, 1, 2, 0]
CROWS = 16 * len(QROWS)
MROWS = 3
NEX, INTER = 8, 128
SLOTS = 256
DFF = 1024
FC = DFF // P
EPS = 1e-5
SCALE = 1.0 / HD ** 0.5
NIT = NG * NB
TWO_ONES = float(np.array([0x3F803F80], np.uint32).view(np.float32)[0])
GMASK = NIT - NB
NUNIT = NEX * NB
ROWS_BEFORE = [max(0, NG * HG * NB * NB * (u - 8) // (NUNIT - 8)) for u in range(NUNIT + 1)]
TURN_AT = {next(u for u in range(NUNIT) if ROWS_BEFORE[u] >= 64 * (L + 1)): L for L in range(NB - 1)}
RING = [n % 3 for n in range(63)] + [1]
BEFORE = [max([m for m in range(-64, n) if RING[m % 64] == RING[n]]) for n in range(64)]
S1_BANKS = (3, 6, 7)
PLAIN = HG * (NG - 1)
OUT_AT = (11, 13, 14, 15)
QRING = 8


def program(nc, x, wqk, bqk, cosT, sinT, wvr, bv, bo, wgu, wdn, wo, w4, b4, wrb, br, w1, b1, w2, b2, out):
    parts_d = nc.dram_tensor("parts_scratch", [3, NH, 2 * 8, 2, T], BF16).ap()
    den_d = nc.dram_tensor("den_scratch", [NIT, P, HG * BLK // P], F32).ap()
    max_d = nc.dram_tensor("max_scratch", [NIT, 3 * HG * TPB, P], BF16).ap()

    with ExitStack() as ctx:
        def sb(name, shape, dt=F32):
            return ctx.enter_context(nc.sbuf_tensor(name, shape, dt))

        def sem(name):
            return ctx.enter_context(nc.semaphore(name))

        ps = ctx.enter_context(nc.psum_tensor("ps", [P, 8, BLK], F32))

        xs = sb("xs", [P, NT, E])
        wide = sb("wide", [P, NG * T])
        kbig = sb("kbig", [P, NG * HG * T], BF16)
        qring = sb("qring", [P, QRING * HG * BLK], BF16)
        vall = sb("vall", [P, NT * NH * (HD + 1)])
        vst = sb("vst", [P, NT, HG, 32])
        prob = sb("prob", [P, 2, HG * BLK])
        osb = sb("osb", [P, BLK])
        ident = sb("ident", [P, P])
        identb = sb("identb", [P, P], BF16)
        selb = sb("selb", [P, P])
        stats = sb("stats", [P, NT, 6])
        mv = sb("mv", [P, NT, 2])
        std = sb("std", [P, NT])
        rstd = sb("rstd", [P, NT])
        epsc = sb("epsc", [P, 1])
        bqk_s = sb("bqk_s", [P, 4])
        mraw = sb("mraw", [P, HG * NT * NB])
        mnew = sb("mnew", [P, HG * TPB * NB])
        den = sb("den", [P, BLK])
        dcol = sb("dcol", [P, 2, HG * BLK // P])
        mneg = sb("mneg", [P, HG * TPB])
        mres = sb("mres", [P, HG * TPB])
        mpad = sb("mpad", [P, P], BF16)
        mt = sb("mt", [3 * HG * TPB, P], BF16)
        lg = sb("lg", [P, NT, NEX])
        rt = sb("rt", [P, 4, NT, NEX])
        rs = sb("rs", [P, 4, NT])
        wtok = sb("wtok", [P, NEX, NT])

        mpart = mpad[:, 0:3 * HG * TPB].rearrange("p (s n) -> p s n", s=3)
        xn = wide[:, 0:NT * E].rearrange("p (t e) -> p t e", t=NT)
        xnT = wide[:, NT * E:2 * NT * E].rearrange("p (k t) -> p k t", k=KH)
        outT = wide[:, :].rearrange("p (g t) -> p g t", g=NG)
        K = kbig[:, :].rearrange("p (c t) -> p c t", t=T)

        kf = kbig[:, HG * T:].bitcast(F32)
        qf = qring[:, :].bitcast(F32)
        qk = kf[:, 0:2 * 4 * BLK].rearrange("p (b a n) -> p b a n", b=2, a=4)
        tmp = kf[:, 4096:4096 + 8 * BLK].rearrange("p (j a n) -> p j a n", j=4, a=2)
        cos_s = kf[:, 8192:8192 + T]
        sin_s = kf[:, 8192 + T:8192 + 2 * T]
        rotb = kbig[:, 0:HG * T].bitcast(F32).rearrange("p (b a n) -> p b a n", b=2, a=4)
        prt = qring[:, 0:2 * 12 * BLK].rearrange("p (b s a n) -> p b s a n", b=2, s=3, a=4)
        rem = qf[:, 12 * BLK:16 * BLK].rearrange("p (a n) -> p a n", a=4)
        pf = prob[:, :, :].rearrange("p a n -> p (a n)")
        wqk_s = pf[:, 0:1024].rearrange("p (k n) -> p k n", k=KH)
        wvr_s = pf[:, 1024:1024 + KH * 264].rearrange("p (k n) -> p k n", k=KH)
        bv_s = pf[:, 1600:1856]
        bo_s = pf[:, 1856:2112]
        cmp = pf[:, 2112:2112 + NEX * NT * NEX].rearrange("p (a t e) -> p a t e", a=NEX, t=NT)
        moe = sb("moe", [P, 2, 768])
        wgu_s = [moe[:, j, 0:512].rearrange("p (k n) -> p k n", k=KH) for j in range(2)]
        wdn_s = [moe[:, j, 512:768] for j in range(2)]
        sg = [vst[:, 4 * j:4 * j + 4, :, :].rearrange("p a b c -> p (a b c)") for j in range(2)]
        hb = [vst[:, 8 + 4 * j:12 + 4 * j, :, :].rearrange("p a b c -> p (a b c)") for j in range(2)]
        dsc = [pf[:, 2048 * j:2048 * j + 1024].rearrange("p (a n) -> p a n", a=TPB) for j in range(2)]

        x_ld = [sem(f"x_ld{c}") for c in range(NB)]
        wqk_ld, tab_ld, wv_ld, wo_ld, w4_ld, wf_ld = (sem(n) for n in ("wqk_ld", "tab_ld", "wv_ld", "wo_ld", "w4_ld", "wf_ld"))
        ids, consts = sem("ids"), sem("consts")
        dve_s, act_s, pool_s = sem("dve_s"), sem("act_s"), sem("pool_s")
        var_ok, std_ok, xn_ok = sem("var_ok"), sem("std_ok"), sem("xn_ok")
        tr_done, xT_a, xT_v = sem("tr_done"), sem("xT_a"), sem("xT_v")
        qk_done, qk_ok = sem("qk_done"), sem("qk_ok")
        v_done, v_ok = sem("v_done"), sem("v_ok")
        rope_p, rope_in_free = sem("rope_p"), sem("rope_in_free")
        r_ok, rem_ok, hi_ok, mid_ok, lo_ok = (sem(n) for n in ("r_ok", "rem_ok", "hi_ok", "mid_ok", "lo_ok"))
        part_st = [sem("part_st0"), sem("part_st1")]
        lgx_ok, ex_ok, wt_ok = sem("lgx_ok"), sem("ex_ok"), sem("wt_ok")
        k_ld = [sem(f"k_ld{g}") for g in range(NG)]
        ones_ok = sem("ones_ok")
        q_ld = sem("q_ld")
        we_ld = [sem("we_ld0"), sem("we_ld1")]
        gu_done, silu_ok, h_ok, dn_done, dsc_ok, acc_ok = (sem(n) for n in ("gu_done", "silu_ok", "h_ok", "dn_done", "dsc_ok", "acc_ok"))
        s1_done, s1_read = sem("s1_done"), sem("s1_read")
        m_chain, mp_ok, mT_done, mt_ok, md_st, m_ld = (sem(n) for n in ("m_chain", "mp_ok", "mT_done", "mt_ok", "md_st", "m_ld"))
        st_done, exp_ok, pv_done, vst_ok = sem("st_done"), sem("exp_ok"), sem("pv_done"), sem("vst_ok")
        dn_ld, inv_ok, inv_st, den_ld = sem("dn_ld"), sem("inv_ok"), sem("inv_st"), sem("den_ld")
        o_ok, lb_done, den_ok, nrm_ok = sem("o_ok"), sem("lb_done"), sem("den_ok"), sem("nrm_ok")
        wo_done, wo_read, st2_ok, var2_ok = sem("wo_done"), sem("wo_read"), sem("st2_ok"), sem("var2_ok")
        out_st = sem("out_st")


        kbf = kbig[:, :].bitcast(F32)
        w4_s = kbf[:, 0:2048].rearrange("p (k n) -> p k n", k=KH)
        w1_s = kbf[:, 2048:4096].rearrange("p (k n) -> p k n", k=KH)
        w2_s = kbf[:, 4096:6144].rearrange("p (c n) -> p c n", c=FC)
        wo_s = kbf[:, 6144:7168].rearrange("p (g n) -> p g n", g=NG)
        wrb_s = kbf[:, 7168:7424].rearrange("p (k n) -> p k n", k=KH)
        b4_s = kbf[:, 7424:7432]
        b1_s = kbf[:, 7432:7440]
        br_s = kbf[:, 7440:7441]
        b2_s = kbf[:, 7448:7704]
        lrow = kbf[:, 8192:8192 + T]
        sel = kbf[:, 10240:14336].rearrange("p (t j) -> p t j", t=NT)
        eq = kbf[:, 14336:16384].rearrange("p (t s) -> p t s", t=NT)
        xn2 = qf[:, 0:4096].rearrange("p (t e) -> p t e", t=NT)
        xnT2 = qf[:, 4096:8192].rearrange("p (k t) -> p k t", k=KH)
        selT = wide[:, 0:2 * T].rearrange("p (k t) -> p k t", k=2)
        junk = wide[:, 0:T]
        rT = wide[:, 2 * T:4 * T].rearrange("p (k t) -> p k t", k=KH)
        hT = vall[:, 0:2048].rearrange("p (c j) -> p c j", c=FC)
        fxT = vall[:, 2048:2560].rearrange("p (k j) -> p k j", k=KH)
        y = vall[:, 2560:3072].rearrange("p (k e) -> p k e", k=2)
        mask = vall[:, 3072:3200]
        slots = vall[:, 3200:3456]
        ones = vall[:, 3456:3584]
        kb_s = [pf[:, 512 * j:512 * (j + 1)] for j in range(2)]
        kv_s = pf[:, 1024:1536]
        tq_s = [pf[:, 1536:2048], osb[:, :]]
        st_s = [[pf[:, 2048 + 1024 * h + 512 * j:2560 + 1024 * h + 512 * j] for j in range(2)] for h in range(2)]
        gs_s = [vst[:, 4 * j:4 * j + 4, :, :].rearrange("p a b c -> p (a b c)") for j in range(2)]
        lcol = sb("lcol", [P, NT])
        cnt = sb("cnt", [P, 4, NT])
        ew = sb("ew", [P, 3, NT])
        gm = sb("gm", [P, 4])

        tr2_done, xT2_a, xT2_v = sem("tr2_done"), sem("xT2_a"), sem("xT2_v")
        lr_done, lr_ok, lc_done, lc_ok = sem("lr_done"), sem("lr_ok"), sem("lc_done"), sem("lc_ok")
        pj_done, ka_ok, dv_ok, rT_ok = sem("pj_done"), sem("ka_ok"), sem("dv_ok"), sem("rT_ok")
        gm_ok, ew_ok, em_ok, z_done, w_ok = sem("gm_ok"), sem("ew_ok"), sem("em_ok"), sem("z_done"), sem("w_ok")
        sel_ok, fx_done, fx_ok, h1_done, g1_ok = sem("sel_ok"), sem("fx_done"), sem("fx_ok"), sem("h1_done"), sem("g1_ok")
        sT_done, sT_ok, y1_done, y1_ok = sem("sT_done"), sem("sT_ok"), sem("y1_done"), sem("y1_ok")
        rt_done, rt_add, sc_done, y_ok = sem("rt_done"), sem("rt_add"), sem("sc_done"), sem("y_ok")
        xadd_ok, tconst = sem("xadd_ok"), sem("tconst")
        rank_s, eq_ok, tie_ok = sem("rank_s"), sem("eq_ok"), sem("tie_ok")

        def load_second(sp):
            sp.dma_start(wo_s, wo.rearrange("g p n -> p g n")).then_inc(wo_ld, 16)
            sp.dma_start(wrb_s, wrb.rearrange("(k p) n -> p k n", p=P)).then_inc(w4_ld, 16)
            sp.dma_start(b4_s, b4).then_inc(w4_ld, 16)
            sp.dma_start(br_s, br.partition_broadcast(P)).then_inc(w4_ld, 16)
            sp.dma_start(w4_s, w4.rearrange("(k p) n -> p k n", p=P)).then_inc(w4_ld, 16)
            sp.dma_start(w1_s, w1.rearrange("(k p) n -> p k n", p=P)).then_inc(wf_ld, 16)
            sp.dma_start(w2_s, w2.rearrange("(c p) n -> p c n", p=P)).then_inc(wf_ld, 16)
            sp.dma_start(b1_s, b1).then_inc(wf_ld, 16)
            sp.dma_start(b2_s, b2.partition_broadcast(P)).then_inc(wf_ld, 16)

        def tail_sp(sp):
            for c in range(NB):
                sp.wait_ge(y_ok, TPB * (c + 1))
                sp.dma_start(out[BLK * c:BLK * (c + 1), :].rearrange("(t p) e -> p t e", p=P),
                             xs[:, TPB * c:TPB * (c + 1), :]).then_inc(out_st, 16)
            sp.wait_ge(out_st, 16 * NB)

        def tail_pool(pool):
            pool.wait_ge(pv_done, NIT * NT)
            pool.memset(mask, 1.0).then_inc(tconst, 1)
            pool.wait_ge(tconst, 1)
            pool.affine_select(out=mask, in_=mask, compare_op=ALU.is_gt, fill=0.0, base=0,
                               pattern=[[-1, P]], channel_multiplier=1).then_inc(tconst, 1)
            pool.iota(slots, [[1, SLOTS]], base=0, channel_multiplier=0, allow_small_or_imprecise_dtypes=True).then_inc(tconst, 1)
            pool.memset(ones, 1.0).then_inc(tconst, 1)
            for i in range(NT):
                pool.wait_ge(xn_ok, NT + i + 1)
                pool.tensor_tensor(xs[:, i, :], xs[:, i, :], xn2[:, i, :], ALU.add).then_inc(xadd_ok, 1)

            def gate(w):
                b, h = divmod(w, KH)
                pool.wait_ge(dv_ok, w + 1)
                pool.wait_ge(ka_ok, 2 * w + 2)
                pool.tensor_tensor(rT[:, h, BLK * b:BLK * (b + 1)], tq_s[w % 2], gs_s[w % 2], ALU.mult).then_inc(rT_ok, 1)

            pool.wait_ge(lc_ok, 1)
            pool.wait_ge(lr_ok, NB)
            for i in range(NT):
                pool.tensor_scalar(eq[:, i, :], lrow[:, P * i:P * (i + 1)], lcol[:, i:i + 1], None, ALU.is_equal).then_inc(eq_ok, 1)
                if i % 4 == 3:
                    gate(i // 4)
            pool.wait_ge(eq_ok, NT)
            gate(4)
            gate(5)
            pool.tensor_tensor(eq, eq, mask.unsqueeze(1).to_broadcast([P, NT, P]), ALU.mult).then_inc(tie_ok, 1)
            gate(6)
            gate(7)

        def tail_pe(pe, project_out):
            def turn(c):
                pe.wait_ge(xn_ok, NT + TPB * (c + 1))
                if c >= 2:
                    pe.wait_ge(xT2_a, c - 1)
                    pe.wait_ge(xT2_v, c - 1)
                for h in range(KH):
                    for j in range(TPB):
                        mm = pe.transpose(ps[:, 2 * (c % 2) + h, P * j:P * (j + 1)],
                                          xn2[:, TPB * c + j, P * h:P * (h + 1)], ident[:, :])
                    mm.then_inc(tr2_done, 1)

            for i in range(NT - TPB, NT):
                project_out(i)
            for c in range(NB):
                turn(c)
            pe.wait_ge(w4_ld, 64)
            pe.wait_ge(wo_read, NT)
            for b in range(NB):
                pe.wait_ge(xT2_a, b + 1)
                pe.wait_ge(xT2_v, b + 1)
                for h in range(KH):
                    mm = pe.matmul(ps[:, 4 + b, :], wrb_s[:, h, :], xnT2[:, h, BLK * b:BLK * (b + 1)], start=(h == 0), stop=(h == KH - 1))
                mm.then_inc(lr_done, 1)
            pe.wait_ge(lr_ok, NB)
            for i in range(NT):
                mm = pe.transpose(ps[:, 4, i:i + 1], lrow[0:1, P * i:P * (i + 1)], ident[0:1, 0:1])
            mm.then_inc(lc_done, 1)
            for w in range(NB * KH):
                b, h = divmod(w, KH)
                if w == 1:
                    pe.wait_ge(lc_ok, 1)
                if w >= 2:
                    pe.wait_ge(ka_ok, 2 * (w - 1))
                    pe.wait_ge(dv_ok, w - 1)
                for m in range(4):
                    for k in range(KH):
                        mm = pe.matmul(ps[:, 4 * (w % 2) + m, :], w4_s[:, k, E * m + P * h:E * m + P * (h + 1)],
                                       xnT2[:, k, BLK * b:BLK * (b + 1)], start=(k == 0), stop=(k == KH - 1))
                    mm.then_inc(pj_done, 1)
            pe.wait_ge(ka_ok, 4 * NB)
            pe.wait_ge(dv_ok, 2 * NB)
            pe.wait_ge(rT_ok, NB * KH)
            for n in range(8):
                if n >= 2:
                    pe.wait_ge(rt_add, n - 1)
                for i in range(2):
                    for h in range(KH):
                        mm = pe.transpose(ps[:, 6 + n % 2, E * i + P * h:E * i + P * (h + 1)],
                                          rT[:, h, P * (2 * n + i):P * (2 * n + i + 1)], ident[:, :])
                mm.then_inc(rt_done, 1)
            pe.wait_ge(sel_ok, NT)
            for k in range(KH):
                for i in range(NT):
                    mm = pe.matmul(ps[:, k, 0:SLOTS], xn2[:, i, P * k:P * (k + 1)], sel[:, i, :], start=(i == 0), stop=(i == NT - 1))
                mm.then_inc(fx_done, 1)
            pe.wait_ge(em_ok, 1)
            pe.wait_ge(tconst, 4)
            pe.wait_ge(rt_add, 8)
            pe.matmul(ps[:, 7, 0:NT], ones, ew[:, 1, :], start=True, stop=True).then_inc(z_done, 1)

            def turn_sel(n):
                k, c = divmod(n, NB)
                if n == 1:
                    pe.wait_ge(w_ok, 1)
                if n >= 2:
                    pe.wait_ge(sT_ok, n - 1)
                for i in range(TPB):
                    mm = pe.transpose(ps[:, 6 + n % 2, P * i:P * (i + 1)], sel[:, TPB * c + i, P * k:P * (k + 1)], ident[:, :])
                mm.then_inc(sT_done, 1)

            turn_sel(0)
            pe.wait_ge(wf_ld, 64)
            pe.wait_ge(fx_ok, 2)
            for c in range(FC):
                if c >= 4:
                    pe.wait_ge(g1_ok, c - 3)
                for k in range(KH):
                    mm = pe.matmul(ps[:, 2 + c % 4, 0:SLOTS], w1_s[:, k, P * c:P * (c + 1)], fxT[:, k, :], start=(k == 0), stop=(k == KH - 1))
                mm.then_inc(h1_done, 1)
            for n in range(1, 8):
                turn_sel(n)
            pe.wait_ge(g1_ok, FC)
            for k in range(2):
                for c in range(FC):
                    mm = pe.matmul(ps[:, k, 0:E], hT[:, c, P * k:P * (k + 1)], w2_s[:, c, :], start=(c == 0), stop=(c == FC - 1))
                mm.then_inc(y1_done, 1)
            pe.wait_ge(y1_ok, 2)
            pe.wait_ge(sT_ok, 8)
            for i in range(NT):
                if i >= 4:
                    pe.wait_ge(y_ok, i - 3)
                for k in range(2):
                    mm = pe.matmul(ps[:, 2 + i % 4, 0:E], selT[:, k, P * i:P * (i + 1)], y[:, k, :], start=(k == 0), stop=(k == 1))
                mm.then_inc(sc_done, 1)

        def tail_act(act):
            act.wait_ge(var2_ok, NT)
            act.activation(std[:, :], mv[:, :, 1], ACT.Sqrt, bias=epsc[:, :]).then_inc(std_ok, 1)
            for c in range(NB):
                take_turned(act, c)
            act.wait_ge(w4_ld, 64)
            for b in range(NB):
                act.wait_ge(lr_done, b + 1)
                act.activation(lrow[:, BLK * b:BLK * (b + 1)], ps[:, 4 + b, :], ACT.Identity, bias=br_s).then_inc(lr_ok, 1)
            act.wait_ge(gm_ok, 1)
            act.activation(ew[:, 0, :], lcol[:, :], ACT.Exp, bias=gm[:, 1:2]).then_inc(ew_ok, 1)
            for w in range(NB * KH):
                b, h = divmod(w, KH)
                act.wait_ge(pj_done, 4 * w + 1)
                if w >= 2:
                    act.wait_ge(dv_ok, w - 1)
                act.activation(kb_s[w % 2], ps[:, 4 * (w % 2), :], ACT.Identity, bias=b4_s[:, h:h + 1]).then_inc(ka_ok, 1)
                act.wait_ge(pj_done, 4 * w + 3)
                if w >= 2:
                    act.wait_ge(rT_ok, w - 1)
                act.activation(gs_s[w % 2], ps[:, 4 * (w % 2) + 2, :], ACT.Sigmoid, bias=b4_s[:, 4 + h:5 + h]).then_inc(ka_ok, 1)
            for k in range(KH):
                act.wait_ge(fx_done, k + 1)
                act.activation(fxT[:, k, :], ps[:, k, 0:SLOTS], ACT.Copy).then_inc(fx_ok, 1)

            def take_sel(n):
                k, c = divmod(n, NB)
                act.wait_ge(sT_done, n + 1)
                act.activation(selT[:, k, BLK * c:BLK * (c + 1)], ps[:, 6 + n % 2, :], ACT.Copy).then_inc(sT_ok, 1)

            take_sel(0)
            act.wait_ge(wf_ld, 64)
            for c in range(FC):
                act.wait_ge(h1_done, c + 1)
                act.activation(hT[:, c, :], ps[:, 2 + c % 4, 0:SLOTS], ACT.Gelu, bias=b1_s[:, c:c + 1]).then_inc(g1_ok, 1)
            for n in range(1, 8):
                take_sel(n)

        def take_turned(act, c):
            act.wait_ge(tr2_done, 2 * c + 1)
            act.activation(xnT2[:, 0, BLK * c:BLK * (c + 1)], ps[:, 2 * (c % 2), :], ACT.Copy).then_inc(xT2_a, 1)

        def tail_dve(dve):
            n_rank = [0]

            def link(ins):
                n_rank[0] += 1
                ins.then_inc(rank_s, 1)
                dve.wait_ge(rank_s, n_rank[0])

            def norm2(c):
                dve.wait_ge(std_ok, NB + 1)
                link(dve.reciprocal(rstd[:, TPB * c:TPB * (c + 1)], std[:, TPB * c:TPB * (c + 1)]))
                for i in range(TPB * c, TPB * (c + 1)):
                    dve.tensor_scalar(xn2[:, i, :], xs[:, i, :], mv[:, i, 0:1], rstd[:, i:i + 1],
                                      ALU.subtract, ALU.mult).then_inc(xn_ok, 1)

            def turned(c):
                dve.wait_ge(tr2_done, 2 * c + 2)
                dve.tensor_copy(xnT2[:, 1, BLK * c:BLK * (c + 1)], ps[:, 1 + 2 * (c % 2), :]).then_inc(xT2_v, 1)

            norm2(0)
            norm2(1)
            turned(0)
            norm2(2)
            turned(1)
            norm2(3)
            turned(2)
            turned(3)
            dve.wait_ge(lc_done, 1)
            dve.tensor_copy(lcol[:, :], ps[:, 4, 0:NT]).then_inc(lc_ok, 1)
            dve.wait_ge(lr_ok, NB)
            link(dve.tensor_reduce(gm[:, 0:1], lrow, AX.X, ALU.max))
            dve.wait_ge(lc_ok, 1)
            dve.tensor_scalar(gm[:, 1:2], gm[:, 0:1], -1.0, None, ALU.mult).then_inc(gm_ok, 1)
            dve.wait_ge(tconst, 4)
            dve.wait_ge(wo_done, NT)
            dve.memset(cnt[:, 1, 0:1], 0.0)

            def rank(i):
                l = lcol[:, i:i + 1]
                link(dve.tensor_scalar(junk[:, P * i:T], lrow[:, P * i:T], l, 0.0, ALU.is_gt, ALU.add, accum_out=cnt[:, 0, i:i + 1]))
                if i:
                    link(dve.tensor_scalar(junk[:, 0:P * i], lrow[:, 0:P * i], l, 0.0, ALU.is_ge, ALU.add, accum_out=cnt[:, 1, i:i + 1]))

            for w in range(NB * KH):
                b, h = divmod(w, KH)
                dve.wait_ge(ka_ok, 2 * w + 1)
                dve.wait_ge(pj_done, 4 * w + 2)
                link(dve.scalar_tensor_tensor(out=kv_s, in0=ps[:, 4 * (w % 2) + 1, :], scalar=b4_s[:, 2 + h:3 + h], in1=kb_s[w % 2],
                                              op0=ALU.add, op1=ALU.mult))
                before = 0.0 if b == 0 else st_s[h][(b - 1) % 2][:, BLK - 1:BLK]
                link(dve.tensor_tensor_scan(st_s[h][b % 2], kv_s, kv_s, before, ALU.add, ALU.bypass))
                dve.wait_ge(pj_done, 4 * w + 4)
                if w >= 2:
                    dve.wait_ge(rT_ok, w - 1)
                dve.scalar_tensor_tensor(out=tq_s[w % 2], in0=ps[:, 4 * (w % 2) + 3, :], scalar=b4_s[:, 6 + h:7 + h], in1=st_s[h][b % 2],
                                         op0=ALU.add, op1=ALU.mult).then_inc(dv_ok, 1)
                rank(2 * w)
                rank(2 * w + 1)
            dve.wait_ge(tie_ok, 1)
            link(dve.tensor_reduce(cnt[:, 2, :], eq, AX.X, ALU.add))
            link(dve.tensor_tensor(cnt[:, 3, :], cnt[:, 0, :], cnt[:, 1, :], ALU.add))
            link(dve.tensor_tensor(cnt[:, 3, :], cnt[:, 3, :], cnt[:, 2, :], ALU.add))
            for i in range(NT):
                dve.tensor_scalar(sel[:, i, :], slots, cnt[:, 3, i:i + 1], None, ALU.is_equal).then_inc(sel_ok, 1)
            dve.wait_ge(xadd_ok, NT)
            for n in range(8):
                dve.wait_ge(rt_done, n + 1)
                xc = xs[:, 2 * n:2 * n + 2, :]
                dve.tensor_tensor(xc, ps[:, 6 + n % 2, :].rearrange("p (t e) -> p t e", t=2), xc, ALU.add).then_inc(rt_add, 1)
            dve.wait_ge(ew_ok, 1)
            dve.scalar_tensor_tensor(out=ew[:, 1, :], in0=cnt[:, 3, :], scalar=SLOTS - 0.5, in1=ew[:, 0, :],
                                     op0=ALU.is_lt, op1=ALU.mult).then_inc(em_ok, 1)
            dve.wait_ge(z_done, 1)
            link(dve.tensor_reduce(gm[:, 2:3], ps[:, 7, 0:NT], AX.X, ALU.add))
            link(dve.reciprocal(gm[:, 3:4], gm[:, 2:3]))
            dve.tensor_scalar(ew[:, 2, :], ew[:, 1, :], gm[:, 3:4], None, ALU.mult).then_inc(w_ok, 1)
            dve.wait_ge(wf_ld, 64)
            for k in range(2):
                dve.wait_ge(y1_done, k + 1)
                dve.tensor_tensor(y[:, k, :], ps[:, k, 0:E], b2_s, ALU.add).then_inc(y1_ok, 1)
            dve.wait_ge(rt_add, 8)
            dve.wait_ge(w_ok, 1)
            for i in range(NT):
                dve.wait_ge(sc_done, i + 1)
                dve.scalar_tensor_tensor(out=xs[:, i, :], in0=ps[:, 2 + i % 4, 0:E], scalar=ew[:, 2, i:i + 1], in1=xs[:, i, :],
                                         op0=ALU.mult, op1=ALU.add).then_inc(y_ok, 1)

        mturn = ps[:, 5, 0:P // 2].bitcast(BF16)
        mbank = mturn[0:3 * HG * TPB, :]

        block = ctx.enter_context(nc.Block())

        def chain(eng, s, start=0):
            n = [start]

            def link(ins):
                n[0] += 1
                ins.then_inc(s, 1)
                eng.wait_ge(s, n[0])
            return link

        def is_first(it):
            return isinstance(it, int) and it == 0

        def q_slot(it, rows, h, off, n):
            return qring[0:rows, bass.ds((it & (QRING - 1)) * (HG * BLK) + (h * BLK + off), n)]

        def k_part(it, rows, h, off, n):
            return kbig[0:rows, bass.ds((it & GMASK) * T + (h * T + off), n)]

        @block.sync
        def _(sp):
            for c in range(NB):
                sp.dma_start(xs[:, TPB * c:TPB * (c + 1), :],
                             x[BLK * c:BLK * (c + 1), :].rearrange("(t p) e -> p t e", p=P)).then_inc(x_ld[c], 16)
            sp.dma_start(cos_s, cosT).then_inc(tab_ld, 16)
            sp.dma_start(sin_s, sinT).then_inc(tab_ld, 16)

            def load_expert(e, j, free=None):
                if free is not None:
                    sp.wait_ge(dn_done, free)
                sp.dma_start(wgu_s[j], wgu[bass.ds(e, 1), :, :].rearrange("a (k p) n -> p (a k) n", p=P)).then_inc(we_ld[j], 16)
                sp.dma_start(wdn_s[j], wdn[bass.ds(e, 1), :, :].rearrange("a p n -> p (a n)")).then_inc(we_ld[j], 16)

            load_expert(0, 0)
            load_expert(1, 1)
            for b in range(NB):
                for s, ready in enumerate((hi_ok, mid_ok, lo_ok)):
                    sp.wait_ge(ready, b + 1)
                    sp.dma_start(parts_d[s, :, :, :, BLK * b:BLK * (b + 1)].rearrange("h (i s) w n -> (h i) (s w) n", s=2),
                                 prt[:, b % 2, s, :, :]).then_inc(part_st[b % 2], 16)
            for j in range(2):
                sp.wait_ge(part_st[j], 16 * 3 * 2)

            def operand_rows(w, part, head, col, n):
                return parts_d[part, head:head + HG, :, w, col:col + n].rearrange("h r n -> r h n")

            def load_k(g):
                for r, part in enumerate(KROWS):
                    sp.dma_start(K[16 * r:16 * r + 16, HG * g:HG * (g + 1), :],
                                 operand_rows(1, part, HG * g, 0, T)).then_inc(k_ld[g], 16)

            def load_q(L, free=None):
                slot, head, col = (L & (QRING - 1)) * (HG * BLK), L & GMASK, (L & 3) * BLK
                if free is not None:
                    sp.wait_ge(st_done, free)
                for r, part in enumerate(QROWS):
                    dst = qring[16 * r:16 * r + 16, bass.ds(slot, HG * BLK)]
                    sp.dma_start(dst.rearrange("p (h n) -> p h n", h=HG),
                                 operand_rows(0, part, head, col, BLK)).then_inc(q_ld, 16)

            load_k(0)
            for L in range(QRING):
                load_q(L)
                sp.wait_ge(q_ld, 96 * (L + 1))
            for g in range(1, NG):
                load_k(g)

            def store_max(L):
                dst = qring[CROWS:CROWS + MROWS, bass.ds((L & (QRING - 1)) * (HG * BLK), HG * BLK)]
                sp.wait_ge(mt_ok, L + 1)
                sp.dma_start(max_d[bass.ds(L, 1), :, :].rearrange("a r p -> (a r) p"), mt[:, :]).then_inc(md_st, 16)
                sp.wait_ge(md_st, L * 16 + 16)
                sp.dma_start(dst, max_d[bass.ds(L, 1), :, :].rearrange("a (s r) p -> (a s) (r p)", s=3)).then_inc(m_ld, 16)

            for u in range(NUNIT):
                if u in TURN_AT:
                    store_max(TURN_AT[u])
                    sp.wait_ge(m_ld, 16 * (TURN_AT[u] + 1))
                if u % NB == 0 and 0 < u // NB < NEX - 1:
                    load_expert(u // NB + 1, (u // NB + 1) % 2, free=TPB * u)
            store_max(NB - 1)
            sp.wait_ge(m_ld, 16 * NB)
            for it in range(1, NIT):
                sp.wait_ge(o_ok, it)
                sp.dma_start(dcol[:, 0, :], osb[HD:P:32, :].rearrange("h (a n) -> h a n", a=P // HG)).then_inc(dn_ld, 16)
                if it <= NIT - QRING:
                    sp.wait_ge(q_ld, 96 * (it + 7))
                    load_q(it + 7, free=it * 64)
                if it == 9:
                    load_second(sp)
                sp.wait_ge(inv_ok, it)
                sp.dma_start(den_d[it - 1], dcol[:, 1, :]).then_inc(inv_st, 16)
                sp.wait_ge(inv_st, 16 * it)
                sp.wait_ge(nrm_ok, it)
                for h in range(HG):
                    row = den_d[it - 1, P // HG * h:P // HG * (h + 1), :].rearrange("a n -> (a n)")
                    sp.dma_start(den[32 * h:32 * h + 32, :], row.partition_broadcast(32)).then_inc(den_ld, 16)
                if it + 3 < NIT:
                    store_max(it + 3)
                    sp.wait_ge(m_ld, 16 * (it + 4))
                sp.wait_ge(den_ld, 64 * it)
            tail_sp(sp)

        @block.gpsimd
        def _(pool):
            link = chain(pool, pool_s)
            pool.memset(ident[:, :], 0.0).then_inc(ids, 1)
            pool.wait_ge(ids, 1)
            pool.affine_select(out=ident[:, :], in_=ident[:, :], compare_op=ALU.not_equal, fill=1.0, base=0,
                               pattern=[[-1, P]], channel_multiplier=1).then_inc(ids, 1)
            pool.wait_ge(ids, 2)
            pool.tensor_copy(identb[:, :], ident[:, :]).then_inc(ids, 1)
            link(pool.memset(selb[:, :], 0.0))
            pool.affine_select(out=selb[:, :].rearrange("p (g j) -> p g j", g=HG),
                               in_=selb[:, :].rearrange("p (g j) -> p g j", g=HG), compare_op=ALU.not_equal, fill=1.0,
                               base=-HD, pattern=[[-32, HG], [0, 32]], channel_multiplier=1).then_inc(consts, 1)
            vv = vall[:, :].rearrange("p (c d) -> p c d", d=HD + 1)
            pool.memset(vv[:, :, HD:HD + 1], 1.0).then_inc(consts, 1)

            for b in range(NB):
                pool.wait_ge(qk_ok, 4 * (b + 1))
                pool.wait_ge(tab_ld, 32)
                if b:
                    pool.wait_ge(r_ok, 2 * b)
                c = cos_s[:, BLK * b:BLK * (b + 1)]
                s = sin_s[:, BLK * b:BLK * (b + 1)]
                pool.tensor_tensor(tmp[:, 2, :, :], qk[:, b % 2, 2:4, :], c.unsqueeze(1).to_broadcast([P, 2, BLK]), ALU.mult).then_inc(rope_p, 1)
                pool.tensor_tensor(tmp[:, 3, :, :], qk[:, b % 2, 0:2, :], s.unsqueeze(1).to_broadcast([P, 2, BLK]), ALU.mult).then_inc(rope_p, 1)
            pool.wait_ge(xn_ok, NT)
            pool.wait_ge(wv_ld, 48)
            for c in range(NB):
                xc = xs[:, TPB * c:TPB * (c + 1), :]
                pool.tensor_tensor(xc, xc, bo_s.unsqueeze(1).to_broadcast([P, TPB, E]), ALU.add).then_inc(acc_ok, 1)
            pool.wait_ge(lo_ok, NB)
            pool.wait_ge(acc_ok, NB)
            pool.memset(kbig[CROWS:P, :].bitcast(F32), TWO_ONES).then_inc(ones_ok, 1)
            pool.wait_ge(ones_ok, 1)

            with pool.Fori(0, NEX // 2) as pr:
                for k in range(8):
                    b = k % NB
                    pool.wait_ge(dsc_ok, pr * 8 + k + 1)
                    pool.wait_ge(acc_ok, pr * 8 + k + 1)
                    xc = xs[:, TPB * b:TPB * (b + 1), :]
                    pool.tensor_tensor(xc, xc, dsc[k % 2], ALU.add).then_inc(acc_ok, 1)

            v4 = vall[:, :].rearrange("p (t n) -> p t n", t=NT)
            pool.wait_ge(dn_done, 4 * 4 * NEX)
            pool.wait_ge(v_ok, NT)
            pool.memset(vst[:, :, :, :], 0.0).then_inc(nrm_ok, 1)
            pool.wait_ge(nrm_ok, 1)

            def stage_v(it, kt):
                src = v4[:, kt, bass.ds((it & GMASK) * (HD + 1), HG * (HD + 1))]
                pool.tensor_copy(vst[:, kt, :, 0:HD + 1], src.rearrange("p (h d) -> p h d", h=HG)).then_inc(vst_ok, 1)

            for kt in range(NT):
                stage_v(0, kt)
            def normalise(it):
                if isinstance(it, int) and it == NIT - 1:
                    pool.wait_ge(den_ok, 4)
                else:
                    pool.wait_ge(den_ld, it * 64 + 64)
                pool.tensor_tensor(wide[:, bass.ds((it & GMASK) * (T // HG) + (it & 3) * BLK, BLK)], osb[:, :], den[:, :],
                                   ALU.mult).then_inc(nrm_ok, 1)

            for kt in range(NT):
                pool.wait_ge(pv_done, kt + 1)
                stage_v(1, kt)
            with pool.Fori(2, NIT) as it:
                for kt in range(NT):
                    if kt == 9:
                        normalise(it - 2)
                    pool.wait_ge(pv_done, it * 16 + (kt - 15))
                    stage_v(it, kt)
            normalise(NIT - 2)
            normalise(NIT - 1)
            tail_pool(pool)

        @block.tensor
        def _(pe):
            pe.wait_ge(ids, 3)
            for c in range(NB):
                pe.wait_ge(xn_ok, TPB * (c + 1))
                for h in range(KH):
                    for j in range(TPB):
                        mm = pe.transpose(ps[:, 2 * c + h, P * j:P * (j + 1)], xn[:, TPB * c + j, P * h:P * (h + 1)], ident[:, :])
                    mm.then_inc(tr_done, 1)
            pe.wait_ge(wqk_ld, 32)
            for n in range(4 * NB):
                b, a = divmod(n, 4)
                c = max(b, n // 2 if n < 8 else NB - 1)
                pe.wait_ge(xT_a, c + 1)
                pe.wait_ge(xT_v, c + 1)
                if n >= 8:
                    pe.wait_ge(qk_ok, n - 7)
                for h in range(KH):
                    mm = pe.matmul(ps[:, n % 8, :], wqk_s[:, h, P * a:P * (a + 1)], xnT[:, h, BLK * b:BLK * (b + 1)],
                                   start=(h == 0), stop=(h == KH - 1))
                mm.then_inc(qk_done, 1)
            pe.wait_ge(wv_ld, 48)
            for i in range(NT):
                if i < 8:
                    pe.wait_ge(qk_ok, i + 9)
                else:
                    pe.wait_ge(v_ok, i - 7)
                for h in range(KH):
                    mm = pe.matmul(ps[:, i % 8, 0:E + NEX], xnT[:, h, P * i:P * (i + 1)], wvr_s[:, h, :],
                                   start=(h == 0), stop=(h == KH - 1))
                mm.then_inc(v_done, 1)

            def pass1(it, kt, kb):
                h, i = divmod(kt, TPB)
                n = 4 * kt + kb
                pe.wait_ge(s1_read, 256 + 2 if is_first(it) and BEFORE[n] < 0 else it * 64 + (256 + 2 + BEFORE[n] + 1))
                pe.matmul(ps[:, S1_BANKS[RING[n]], :], q_slot(it + 4, CROWS, h, P * i, P), k_part(it + 4, CROWS, h, BLK * kb, BLK),
                          start=True, stop=True).then_inc(s1_done, 1)

            def expert_down(k, j, i):
                pe.matmul(ps[:, 4 + i // 2, E * (i % 2):E * (i % 2 + 1)], hb[k % 2][:, P * i:P * (i + 1)], wdn_s[j],
                          start=True, stop=True).then_inc(dn_done, 1)

            def await_down(u):
                pe.wait_ge(h_ok, u + 3)
                pe.wait_ge(acc_ok, u + 4)

            def row_scores(c):
                L, h, i, kb = c // 64, c // 16 % HG, c // 4 % TPB, c % NB
                if c == 0:
                    pe.wait_ge(k_ld[0], 96)
                if c % 64 == 0:
                    pe.wait_ge(q_ld, 96 * (L + 1))
                pe.wait_ge(s1_read, c + 1)
                pe.matmul(ps[:, 6 + c % 2, :], q_slot(L, CROWS, h, P * i, P), k_part(0, CROWS, h, BLK * kb, BLK),
                          start=True, stop=True).then_inc(s1_done, 1)

            def max_transpose(L):
                pe.wait_ge(mp_ok, L + 1)
                pe.transpose(mturn, mpad[:, :], identb[:, :]).then_inc(mT_done, 1)

            pe.wait_ge(v_ok, NT)
            for u in range(NUNIT + 1):
                k = u % 8
                j, b = divmod(k, NB)
                if u < NUNIT:
                    c0, n = ROWS_BEFORE[u], ROWS_BEFORE[u + 1] - ROWS_BEFORE[u]
                    if b == 0:
                        pe.wait_ge(we_ld[j], u // 8 * 32 + 32)
                    pe.wait_ge(h_ok, u + 1)
                for step in range(8):
                    if step < 4 and u < NUNIT:
                        w, h = divmod(step, KH)
                        mm = pe.matmul(ps[:, 2 * (k % 2) + w, :], wgu_s[j][:, h, P * w:P * (w + 1)],
                                       xnT[:, h, BLK * b:BLK * (b + 1)], start=(h == 0), stop=(h == KH - 1))
                        if h == KH - 1:
                            mm.then_inc(gu_done, 1)
                        if step == 1 and u in TURN_AT:
                            pe.wait_ge(acc_ok, u + 3)
                            max_transpose(TURN_AT[u])
                    if step >= 4 and u:
                        if step == 4:
                            await_down(u - 1)
                            if u in TURN_AT:
                                pe.wait_ge(mt_ok, TURN_AT[u] + 1)
                        expert_down((u - 1) % 8, (u - 1) // NB % 2, step - 4)
                    if u < NUNIT:
                        for c in range(c0 + step * n // 8, c0 + (step + 1) * n // 8):
                            row_scores(c)

            pe.wait_ge(dsc_ok, 4 * NEX)

            def before_plain(it, n):
                return {4: 3, 5: 1, 6: 2, 7: None}.get(n, n - 4) if it == PLAIN else n - 4

            def scores(it, kt, h):
                n = 4 * kt + h
                if n == 0:
                    pe.wait_ge(m_ld, it * 16 + 16)
                    pe.wait_ge(q_ld, it * 96 + 96)
                before, bank = BEFORE[n], RING[n]
                if isinstance(it, int) and 64 * it + n >= 64 * PLAIN + 4:
                    before, bank = before_plain(it, n), n % 4
                if before is not None and (not is_first(it) or before >= 0):
                    pe.wait_ge(exp_ok, it * 64 + (before + 1))
                pe.matmul(ps[:, bank, :], k_part(it, CROWS + MROWS, h, P * kt, P),
                          q_slot(it, CROWS + MROWS, h, 0, BLK), start=True, stop=True).then_inc(st_done, 1)

            def values(it, kt):
                pe.wait_ge(exp_ok, it * 64 + (4 * kt + 4))
                pe.wait_ge(vst_ok, it * 16 + (kt + 1))
                if kt == 0 and not is_first(it):
                    pe.wait_ge(o_ok, it)
                for h in range(HG):
                    mm = pe.matmul(ps[32 * h:32 * h + 32, 4, :], vst[:, kt, h, :], prob[:, kt % 2, BLK * h:BLK * (h + 1)],
                                   start=(kt == 0), stop=(kt == NT - 1))
                mm.then_inc(pv_done, 1)

            def spread_den(it):
                pe.wait_ge(o_ok, it + 1)
                pe.wait_ge(mt_ok, NIT)
                pe.matmul(ps[:, 5, :], selb[:, :], osb[:, :], start=True, stop=True).then_inc(lb_done, 1)

            def project_out(i):
                pe.wait_ge(nrm_ok, 14 + i // TPB)
                if i >= 2:
                    pe.wait_ge(wo_read, i - 1)
                for g in range(NG):
                    mm = pe.matmul(ps[:, 6 + i % 2, 0:E], outT[:, g, P * i:P * (i + 1)], wo_s[:, g, :],
                                   start=(g == 0), stop=(g == NG - 1))
                mm.then_inc(wo_done, 1)

            def iteration(it, first, pass_1, last, max_before, out_tiles=()):
                for kt in range(NT):
                    if kt == 7 and max_before:
                        pe.wait_ge(mt_ok, it + 3)
                        max_transpose(it + 3)
                    if first and kt == 3:
                        max_transpose(NB - 1)
                    if pass_1:
                        if kt == 0:
                            pe.wait_ge(q_ld, it * 96 + 480)
                    for h in range(HG):
                        if pass_1:
                            pass1(it, kt, h)
                        if not pass_1 and h == HG - 1:
                            values(it, kt)
                        if kt < NT - 1:
                            scores(it, kt + 1, h)
                        elif not last:
                            scores(it + 1, 0, h)
                    if pass_1:
                        values(it, kt)
                    if kt in OUT_AT and out_tiles:
                        project_out(out_tiles[OUT_AT.index(kt)])

            for g in range(NG):
                pe.wait_ge(k_ld[g], 96)
            pe.wait_ge(consts, 2)
            pe.wait_ge(ones_ok, 1)
            for h in range(HG):
                scores(0, 0, h)
            iteration(0, True, True, False, False)
            with pe.Fori(1, 12) as it:
                iteration(it, False, True, False, True)
            pe.wait_ge(s1_read, 64 * 16 + 2)
            iteration(12, False, False, False, True)
            pe.wait_ge(wo_ld, 16)
            for it in range(13, NIT):
                iteration(it, False, False, it == NIT - 1, False, range(TPB * (it - 13), TPB * (it - 12)))
            spread_den(15)
            tail_pe(pe, project_out)

        @block.scalar
        def _(act):
            act.dma_start(wqk_s, wqk.rearrange("(k p) n -> p k n", p=P)).then_inc(wqk_ld, 16)
            act.dma_start(bqk_s[:, :], bqk).then_inc(wqk_ld, 16)
            act.dma_start(wvr_s, wvr.rearrange("(k p) n -> p k n", p=P)).then_inc(wv_ld, 16)
            act.dma_start(bv_s, bv.partition_broadcast(P)).then_inc(wv_ld, 16)
            act.dma_start(bo_s, bo.partition_broadcast(P)).then_inc(wv_ld, 16)
            for c in range(NB):
                act.wait_ge(var_ok, c + 1)
                act.activation(std[:, TPB * c:TPB * (c + 1)], mv[:, TPB * c:TPB * (c + 1), 1], ACT.Sqrt,
                               bias=epsc[:, :]).then_inc(std_ok, 1)
            for c in range(NB):
                act.wait_ge(tr_done, 2 * c + 1)
                act.activation(xnT[:, 0, BLK * c:BLK * (c + 1)], ps[:, 2 * c, :], ACT.Copy).then_inc(xT_a, 1)

            def high(b):
                act.wait_ge(r_ok, 2 * b + 2)
                if b >= 2:
                    act.wait_ge(part_st[b % 2], 48)
                act.activation(prt[:, b % 2, 0, :, :], rotb[:, b % 2, :, :], ACT.Copy).then_inc(hi_ok, 1)

            def middle(b):
                act.wait_ge(rem_ok, b + 1)
                act.activation(prt[:, b % 2, 1, :, :], rem[:, :, :], ACT.Copy).then_inc(mid_ok, 1)

            act.wait_ge(wqk_ld, 32)
            for b in range(NB + 1):
                for a in range(4 if b < NB else 0):
                    n = 4 * b + a
                    act.wait_ge(qk_done, n + 1)
                    if b >= 2:
                        act.wait_ge(r_ok, 2 * b - 2)
                    act.activation(qk[:, b % 2, a, :], ps[:, n % 8, :], ACT.Identity, bias=bqk_s[:, a:a + 1]).then_inc(qk_ok, 1)
                if b:
                    high(b - 1)
                    middle(b - 1)
            act.wait_ge(lgx_ok, 1)
            act.activation(rt[:, 1, :, :], rt[:, 0, :, :], ACT.Exp).then_inc(ex_ok, 1)

            def silu(u, k):
                act.wait_ge(gu_done, u * 2 + 1)
                act.wait_ge(h_ok, u + 1)
                act.activation(sg[k % 2], ps[:, 2 * (k % 2), :], ACT.Silu).then_inc(silu_ok, 1)

            def scaled(u, k, e):
                act.wait_ge(acc_ok, u + 3)
                for i in range(TPB):
                    if i % 2 == 0:
                        act.wait_ge(dn_done, u * 4 + (i + 2))
                    t = TPB * (k % NB) + i
                    ins = act.activation(dsc[k % 2][:, i, :], ps[:, 4 + i // 2, E * (i % 2):E * (i % 2 + 1)], ACT.Copy,
                                         scale=wtok[:, e:e + 1, t] if isinstance(e, int) else wtok[:, bass.ds(e, 1), t])
                ins.then_inc(dsc_ok, 1)

            act.wait_ge(wt_ok, 1)

            def units(pr, n):
                for k in range(8):
                    if k < n:
                        silu(pr * 8 + (k + 1), (k + 1) % 8)
                    scaled(pr * 8 + k, k, pr * 2 + k // NB)

            silu(0, 0)
            with act.Fori(0, NEX // 2 - 1) as pr:
                units(pr, 8)
            units(NEX // 2 - 1, 7)

            def exps(it, kt, h, plain):
                n = 4 * kt + h
                bank = n % 4 if plain and not (isinstance(it, int) and n < 4) else RING[n]
                act.wait_ge(st_done, it * 64 + (n + 1))
                if h == 0 and (not is_first(it) or kt >= 2):
                    act.wait_ge(pv_done, it * 16 + (kt - 1))
                act.activation(prob[:, kt % 2, BLK * h:BLK * (h + 1)], ps[:, bank, :], ACT.Exp, scale=SCALE).then_inc(exp_ok, 1)

            def take_sums(it):
                act.wait_ge(pv_done, it * 16 + 16)
                act.wait_ge(nrm_ok, it + 1)
                act.activation(osb[:, :], ps[:, 4, :], ACT.Copy).then_inc(o_ok, 1)

            act.wait_ge(acc_ok, 4 * NEX + 4)
            def iteration(it, plain=False):
                for kt in range(NT):
                    for h in range(HG):
                        exps(it, kt, h, plain)
                        if kt == 0 and h == 1 and not is_first(it):
                            take_sums(it - 1)

            iteration(0)
            with act.Fori(1, PLAIN) as it:
                iteration(it)
            iteration(PLAIN, True)
            with act.Fori(PLAIN + 1, NIT) as it:
                iteration(it, True)
            take_sums(NIT - 1)
            tail_act(act)

        @block.vector
        def _(dve):
            link = chain(dve, dve_s)
            dve.memset(mpad[:, :], 0.0)
            link(dve.memset(epsc[:, :], EPS))

            def stats1(c):
                dve.wait_ge(x_ld[c], 16)
                for i in range(TPB * c, TPB * (c + 1)):
                    ins = dve.bn_stats(stats[:, i, :], xs[:, i, :])
                link(ins)
                for i in range(TPB * c, TPB * (c + 1)):
                    ins = dve.bn_aggr(mv[:, i, :], stats[:, i, :])
                ins.then_inc(var_ok, 1)

            def norm1(c):
                dve.wait_ge(std_ok, c + 1)
                link(dve.reciprocal(rstd[:, TPB * c:TPB * (c + 1)], std[:, TPB * c:TPB * (c + 1)]))
                for i in range(TPB * c, TPB * (c + 1)):
                    dve.tensor_scalar(xn[:, i, :], xs[:, i, :], mv[:, i, 0:1], rstd[:, i:i + 1],
                                      ALU.subtract, ALU.mult).then_inc(xn_ok, 1)

            stats1(0)
            for c in range(1, NB):
                stats1(c)
                norm1(c - 1)
            norm1(NB - 1)
            for c in range(NB):
                dve.wait_ge(tr_done, 2 * c + 2)
                dve.tensor_copy(xnT[:, 1, BLK * c:BLK * (c + 1)], ps[:, 2 * c + 1, :]).then_inc(xT_v, 1)

            def rotate(b):
                dve.wait_ge(qk_ok, 4 * (b + 1))
                dve.wait_ge(tab_ld, 32)
                if b:
                    dve.wait_ge(r_ok, 2 * b)
                c = cos_s[:, BLK * b:BLK * (b + 1)].unsqueeze(1).to_broadcast([P, 2, BLK])
                s = sin_s[:, BLK * b:BLK * (b + 1)].unsqueeze(1).to_broadcast([P, 2, BLK])
                dve.tensor_tensor(tmp[:, 0, :, :], qk[:, b % 2, 0:2, :], c, ALU.mult)
                link(dve.tensor_tensor(tmp[:, 1, :, :], qk[:, b % 2, 2:4, :], s, ALU.mult))
                dve.tensor_tensor(rotb[:, b % 2, 0:2, :], tmp[:, 0, :, :], tmp[:, 1, :, :], ALU.subtract).then_inc(r_ok, 1)
                dve.wait_ge(rope_p, 2 * b + 2)
                dve.tensor_tensor(rotb[:, b % 2, 2:4, :], tmp[:, 2, :, :], tmp[:, 3, :, :], ALU.add).then_inc(r_ok, 1)

            def split(b):
                dve.wait_ge(hi_ok, b + 1)
                dve.wait_ge(r_ok, 2 * b + 2)
                if b:
                    dve.wait_ge(lo_ok, b)
                dve.tensor_tensor(rem[:, :, :], rotb[:, b % 2, :, :], prt[:, b % 2, 0, :, :], ALU.subtract).then_inc(rem_ok, 1)

            def low(b):
                dve.wait_ge(mid_ok, b + 1)
                dve.wait_ge(rem_ok, b + 1)
                dve.tensor_tensor(prt[:, b % 2, 2, :, :], rem[:, :, :], prt[:, b % 2, 1, :, :], ALU.subtract).then_inc(lo_ok, 1)

            def take_v(i):
                dve.wait_ge(v_done, i + 1)
                dst = vall[:, i * NH * (HD + 1):(i + 1) * NH * (HD + 1)].rearrange("p (h d) -> p h d", h=NH)[:, :, 0:HD]
                dve.tensor_tensor(dst, ps[:, i % 8, 0:E].rearrange("p (h d) -> p h d", h=NH),
                                  bv_s.rearrange("p (h d) -> p h d", h=NH), ALU.add)
                dve.tensor_copy(lg[:, i, :], ps[:, i % 8, E:E + NEX]).then_inc(v_ok, 1)

            for b in range(NB):
                rotate(b)
                if b:
                    low(b - 1)
                if b < NB - 1:
                    split(b)
            dve.wait_ge(wv_ld, 48)
            for i in range(8):
                take_v(i)
            split(NB - 1)
            for i in range(8, NT):
                take_v(i)
            low(NB - 1)

            dve.wait_ge(v_ok, NT)
            link(dve.tensor_reduce(rs[:, 0, :], lg[:, :, :], AX.X, ALU.max))
            dve.tensor_tensor(rt[:, 0, :, :], lg[:, :, :], rs[:, 0, :].unsqueeze(2).to_broadcast([P, NT, NEX]), ALU.subtract).then_inc(lgx_ok, 1)
            dve.wait_ge(ex_ok, 1)
            link(dve.tensor_reduce(rs[:, 1, :], rt[:, 1, :, :], AX.X, ALU.add))
            link(dve.reciprocal(rs[:, 2, :], rs[:, 1, :]))
            link(dve.tensor_tensor(rt[:, 2, :, :], rt[:, 1, :, :], rs[:, 2, :].unsqueeze(2).to_broadcast([P, NT, NEX]), ALU.mult))
            for e in range(NEX):
                mine = rt[:, 2, :, e:e + 1]
                ins = dve.tensor_tensor(cmp[:, e, :, 0:e + 1], mine.to_broadcast([P, NT, e + 1]), rt[:, 2, :, 0:e + 1], ALU.is_gt)
                if e < NEX - 1:
                    ins = dve.tensor_tensor(cmp[:, e, :, e + 1:], mine.to_broadcast([P, NT, NEX - 1 - e]), rt[:, 2, :, e + 1:], ALU.is_ge)
            link(ins)
            link(dve.tensor_reduce(rt[:, 0, :, :], cmp.rearrange("p a t e -> p t e a"), AX.X, ALU.add))
            link(dve.scalar_tensor_tensor(out=rt[:, 3, :, :], in0=rt[:, 0, :, :], scalar=1.5, in1=rt[:, 2, :, :],
                                          op0=ALU.is_lt, op1=ALU.mult))
            link(dve.tensor_reduce(rs[:, 3, :], rt[:, 3, :, :], AX.X, ALU.add))
            link(dve.reciprocal(rs[:, 0, :], rs[:, 3, :]))
            dve.tensor_tensor(wtok[:, :, :].rearrange("p e t -> p t e"), rt[:, 3, :, :],
                              rs[:, 0, :].unsqueeze(2).to_broadcast([P, NT, NEX]), ALU.mult).then_inc(wt_ok, 1)
            dve.wait_ge(wt_ok, 1)
            dve.memset(mneg[:, :], 0.0).then_inc(h_ok, 2)
            dve.memset(mres[:, :], 0.0).then_inc(s1_read, 2)

            def row_max(n, dst, bank):
                dve.wait_ge(s1_done, n)
                dve.tensor_reduce(dst, ps[:, bank, :], AX.X, ALU.max).then_inc(s1_read, 1)

            def max_parts(L, src):
                def step(j, ins):
                    ins.then_inc(m_chain, 1)
                    dve.wait_ge(m_chain, L * 5 + j)
                step(1, dve.tensor_reduce(mres[:, :].rearrange("p (h t) -> p h t", h=HG), src, AX.X, ALU.max))
                step(2, dve.tensor_scalar(mneg[:, :], mres[:, :], -1.0, None, ALU.mult))
                step(3, dve.tensor_copy(mpart[:, 0, :], mneg[:, :]))
                step(4, dve.tensor_tensor(mres[:, :], mneg[:, :], mpart[:, 0, :], ALU.subtract))
                step(5, dve.tensor_copy(mpart[:, 1, :], mres[:, :]))
                dve.tensor_tensor(mpart[:, 2, :], mres[:, :], mpart[:, 1, :], ALU.subtract).then_inc(mp_ok, 1)

            def take_max(L):
                dve.wait_ge(mT_done, L + 1)
                if not is_first(L):
                    dve.wait_ge(md_st, L * 16)
                dve.tensor_copy(mt[:, :], mbank).then_inc(mt_ok, 1)

            m4 = mraw[:, :].rearrange("p (b h t k) -> p b h t k", h=HG, b=NB, t=TPB)
            for u in range(NUNIT):
                k = u % 8
                c0, n = ROWS_BEFORE[u], ROWS_BEFORE[u + 1] - ROWS_BEFORE[u]
                for r in range(n + 1):
                    if r == 3 * n // 8:
                        dve.wait_ge(silu_ok, u + 1)
                        dve.wait_ge(gu_done, 2 * u + 2)
                        dve.tensor_tensor(hb[k % 2], sg[k % 2], ps[:, 2 * (k % 2) + 1, :], ALU.mult).then_inc(h_ok, 1)
                        if u in TURN_AT:
                            take_max(TURN_AT[u])
                    if r < n:
                        c = c0 + r
                        row_max(c + 1, mraw[:, c:c + 1], 6 + c % 2)
                        if c % 64 == 63 and c < 192:
                            dve.wait_ge(s1_read, c + 3)
                            max_parts(c // 64, m4[:, c // 64, :, :, :])
            dve.wait_ge(s1_read, 256 + 2)

            mit = mnew[:, :].rearrange("p (h t k) -> p h t k", h=HG, t=TPB)

            def invert_spread(it):
                dve.wait_ge(dn_ld, it * 16 + 16)
                dve.reciprocal(dcol[:, 1, :], dcol[:, 0, :]).then_inc(inv_ok, 1)

            def invert(it, c):
                if c == 0:
                    dve.wait_ge(lb_done, 1)
                    dve.wait_ge(nrm_ok, it + 1)
                dve.reciprocal(den[:, P * c:P * (c + 1)], ps[:, 5, P * c:P * (c + 1)]).then_inc(den_ok, 1)

            def add_projected(i):
                dve.wait_ge(wo_done, i + 1)
                dve.tensor_tensor(xs[:, i, :], ps[:, 6 + i % 2, 0:E], xs[:, i, :], ALU.add).then_inc(wo_read, 1)
                dve.wait_ge(wo_read, i + 1)
                dve.bn_stats(stats[:, i, :], xs[:, i, :]).then_inc(st2_ok, 1)
                dve.wait_ge(st2_ok, i + 1)
                dve.bn_aggr(mv[:, i, :], stats[:, i, :]).then_inc(var2_ok, 1)

            def iteration(it, first, pass_1, max_before, out_tiles=()):
                if max_before:
                    dve.wait_ge(s1_read, it * 64 + 258)
                    max_parts(it + 3, mit)
                for kt in range(NT):
                    if pass_1:
                        for kb in range(NB):
                            c = 4 * kt + kb
                            row_max(it * 64 + (256 + c + 1), mnew[:, c:c + 1], S1_BANKS[RING[c]])
                    if not first and kt == 3:
                        invert_spread(it - 1)
                    if kt == 7 and max_before:
                        take_max(it + 3)
                    if first and kt == 0:
                        max_parts(NB - 1, m4[:, NB - 1, :, :, :])
                    if first and kt == 4:
                        take_max(NB - 1)
                    if kt in OUT_AT and out_tiles:
                        add_projected(out_tiles[OUT_AT.index(kt)])

            iteration(0, True, True, False)
            with dve.Fori(1, 12) as it:
                iteration(it, False, True, True)
            iteration(12, False, False, True)
            dve.wait_ge(acc_ok, 4 * NEX + 4)
            for it in range(13, NIT):
                iteration(it, False, False, False, range(TPB * (it - 13), TPB * (it - 12)))
            for c in range(4):
                invert(NIT - 1, c)
            for i in range(NT - TPB, NT):
                add_projected(i)
            tail_dve(dve)


def kernel(**inputs):
    import concourse.bacc as bacc
    from concourse.bass_utils import run_bass_kernel_spmd as run

    a = {k: np.asarray(v) for k, v in inputs.items()}
    c = np.ascontiguousarray
    half = HD // 2
    rows = [np.array([h * HD + s * half + i for h in range(NH) for i in range(half)]) for s in range(2)]
    wq, wk = a["L0_attn_Wq"], a["L0_attn_Wk"]
    bq, bk = a["L0_attn_bq"], a["L0_attn_bk"]
    wqk = c(np.concatenate([wq[rows[0]], wk[rows[0]], wq[rows[1]], wk[rows[1]]]).T)
    bqk = c(np.stack([bq[rows[0]], bk[rows[0]], bq[rows[1]], bk[rows[1]]], axis=1))
    freq = (np.float32(1.0) / np.float32(10000.0) ** (np.arange(0, HD, 2, dtype=np.float32) / np.float32(HD))).astype(np.float32)
    angle = (np.arange(T, dtype=np.float32)[None, :] * freq[:, None]).astype(np.float32)
    cosT = c(np.tile(np.cos(angle).astype(np.float32), (NH, 1)))
    sinT = c(np.tile(np.sin(angle).astype(np.float32), (NH, 1)))
    wvr = c(np.concatenate([a["L0_attn_Wv"], a["L0_ffn_router_gate"]]).T)
    gu = a["L0_ffn_expert_gate_up"]
    wgu = c(np.concatenate([gu[:, :, 0::2], gu[:, :, 1::2]], axis=2))
    woT = np.zeros((NG, HG, 32, E), np.float32)
    woT[:, :, :HD, :] = a["L0_attn_Wo"].T.reshape(NG, HG, HD, E)
    four = ("k", "v", "g", "q")
    w4 = c(np.concatenate([a["L1_attn_W" + m] for m in four]).T)
    b4 = c(np.concatenate([a["L1_attn_b" + m].reshape(KH, P) for m in four]).T)
    feeds = dict(
        x=c(a["L0_attn_hidden_states"][0]), wqk=wqk, bqk=bqk, cosT=cosT, sinT=sinT, wvr=wvr, bv=a["L0_attn_bv"], bo=a["L0_attn_bo"],
        wgu=wgu, wdn=c(a["L0_ffn_expert_down"]), wo=woT.reshape(NG, P, E), w4=w4, b4=b4,
        wrb=c(np.tile(a["L1_ffn_Wr"], (1, P))), br=a["L1_ffn_br"], w1=a["L1_ffn_W1"], b1=c(a["L1_ffn_b1"].reshape(FC, P).T),
        w2=a["L1_ffn_W2"], b2=a["L1_ffn_b2"])
    nc = bacc.Bacc("TRN2", target_bir_lowering=False, num_devices=1)
    arrays = {f"in_{k}": c(v) for k, v in feeds.items()}
    aps = {k: nc.dram_tensor(f"in_{k}", feeds[k].shape, mybir.dt.from_np(feeds[k].dtype), kind="ExternalInput").ap() for k in feeds}
    out = nc.dram_tensor("out_0", (T, E), F32, kind="ExternalOutput").ap()
    program(nc, out=out, **aps)
    r = run(nc, [arrays], core_ids=[0])
    return r.results[0]["out_0"].reshape(1, T, E)
```

```python
from contextlib import ExitStack

import numpy as np

import concourse.bass as bass
from concourse import mybir

F32 = mybir.dt.float32
BF16 = mybir.dt.bfloat16
ALU = mybir.AluOpType
ACT = mybir.ActivationFunctionType
AX = mybir.AxisListType

P = 128
T, E = 2048, 256
NT = T // P
BLK = 512
NB = T // BLK
TPB = BLK // P
KH = E // P
NH, HD = 16, 16
HG = 4
NG = NH // HG
QROWS = [0, 0, 1, 1, 0, 2]
KROWS = [0, 1, 0, 1, 2, 0]
CROWS = 16 * len(QROWS)
MROWS = 3
NEX, INTER = 8, 128
SLOTS = 256
DFF = 1024
FC = DFF // P
EPS = 1e-5
SCALE = 1.0 / HD ** 0.5
NIT = NG * NB
TWO_ONES = float(np.array([0x3F803F80], np.uint32).view(np.float32)[0])
GMASK = NIT - NB
NUNIT = NEX * NB
ROW_UNIT = 5
ROWS_BEFORE = [max(0, NG * HG * NB * NB * (u - ROW_UNIT) // (NUNIT - ROW_UNIT)) for u in range(NUNIT + 1)]
STEP_AT = (0, 4, 9, 13, 18, 19, 21, 22, 24)
HIDDEN_AT = 22
TURN_AT = {next(u for u in range(NUNIT) if ROWS_BEFORE[u] >= 64 * (L + 1)): L for L in range(NB - 1)}
RING = [n % 3 for n in range(63)] + [3]
S2_BANKS = (0, 1, 2, 5)
BEFORE = [max([m for m in range(-64, n) if RING[m % 64] == RING[n]]) for n in range(64)]
S1_BANKS = (3, 6, 7, 5)
PLAIN = HG * (NG - 1)
TURN_AFTER = {1: 1, 3: 2, 5: 3}
V_AFTER_HIGH = {NB - 2: range(0, 6), NB - 1: range(12, NT)}
V_AFTER_MIDDLE = {NB - 2: range(6, 12)}
PROJECT_FROM = 8


def project_steps(it, kt):
    x = NT * (it - PLAIN - 1) + kt - PROJECT_FROM
    last = NT * (NIT - PLAIN - 1) - 2 * PROJECT_FROM
    steps = () if x < 0 else (x,) if x < last else (2 * x - last, 2 * x - last + 1)
    return [divmod(n, NG) for n in steps]


POOL_SEL = 3
QRING = 8


def program(nc, x, wqk, bqk, cosT, sinT, wvr, bv, bo, wgu, wdn, wo, w4, b4, wrb, br, w1, b1, w2, b2, out):
    parts_d = nc.dram_tensor("parts_scratch", [3, NH, 2 * 8, 2, T], BF16).ap()
    den_d = nc.dram_tensor("den_scratch", [NIT, P, HG * BLK // P], F32).ap()
    max_d = nc.dram_tensor("max_scratch", [NIT, 3 * HG * TPB, P], BF16).ap()

    with ExitStack() as ctx:
        def sb(name, shape, dt=F32):
            return ctx.enter_context(nc.sbuf_tensor(name, shape, dt))

        def sem(name):
            return ctx.enter_context(nc.semaphore(name))

        ps = ctx.enter_context(nc.psum_tensor("ps", [P, 8, BLK], F32))

        xs = sb("xs", [P, NT, E])
        wide = sb("wide", [P, NG * T])
        kbig = sb("kbig", [P, NG * HG * T], BF16)
        qring = sb("qring", [P, QRING * HG * BLK], BF16)
        vall = sb("vall", [P, NT * NH * (HD + 1)])
        vst = sb("vst", [P, NT, HG, 32])
        prob = sb("prob", [P, 2, HG * BLK])
        osb = sb("osb", [P, BLK])
        ident = sb("ident", [P, P])
        identb = sb("identb", [P, P], BF16)
        selb = sb("selb", [P, P])
        stats = sb("stats", [P, NT, 6])
        mv = sb("mv", [P, NT, 2])
        std = sb("std", [P, NT])
        rstd = sb("rstd", [P, NT])
        epsc = sb("epsc", [P, 1])
        bqk_s = sb("bqk_s", [P, 4])
        mraw = sb("mraw", [P, HG * NT * NB])
        mnew = sb("mnew", [P, HG * TPB * NB])
        den = sb("den", [P, BLK])
        vcredit = sb("vcredit", [P, 1])
        dcol = sb("dcol", [P, 2, HG * BLK // P])
        mneg = sb("mneg", [P, HG * TPB])
        mres = sb("mres", [P, HG * TPB])
        mpad = sb("mpad", [P, P], BF16)
        mt = sb("mt", [3 * HG * TPB, P], BF16)
        lg = sb("lg", [P, NT, NEX])
        rt = sb("rt", [P, 4, NT, NEX])
        rs = sb("rs", [P, 4, NT])
        wtok = sb("wtok", [P, NEX, NT])

        mpart = mpad[:, 0:3 * HG * TPB].rearrange("p (s n) -> p s n", s=3)
        xn = wide[:, 0:NT * E].rearrange("p (t e) -> p t e", t=NT)
        xnT = wide[:, NT * E:2 * NT * E].rearrange("p (k t) -> p k t", k=KH)
        outT = wide[:, :].rearrange("p (g t) -> p g t", g=NG)
        K = kbig[:, :].rearrange("p (c t) -> p c t", t=T)

        kf = kbig[:, HG * T:].bitcast(F32)
        qf = qring[:, :].bitcast(F32)
        qk = kf[:, 0:2 * 4 * BLK].rearrange("p (b a n) -> p b a n", b=2, a=4)
        tmp = kf[:, 4096:4096 + 8 * BLK].rearrange("p (j a n) -> p j a n", j=4, a=2)
        cos_s = kf[:, 8192:8192 + T]
        sin_s = kf[:, 8192 + T:8192 + 2 * T]
        rotb = kbig[:, 0:HG * T].bitcast(F32).rearrange("p (b a n) -> p b a n", b=2, a=4)
        prt = qring[:, 0:2 * 12 * BLK].rearrange("p (b s a n) -> p b s a n", b=2, s=3, a=4)
        rem = qf[:, 12 * BLK:16 * BLK].rearrange("p (a n) -> p a n", a=4)
        pf = prob[:, :, :].rearrange("p a n -> p (a n)")
        wqk_s = pf[:, 0:1024].rearrange("p (k n) -> p k n", k=KH)
        wvr_s = pf[:, 1024:1024 + KH * 264].rearrange("p (k n) -> p k n", k=KH)
        bv_s = pf[:, 1600:1856]
        bo_s = pf[:, 1856:2112]
        cmp = pf[:, 2112:2112 + NEX * NT * NEX].rearrange("p (a t e) -> p a t e", a=NEX, t=NT)
        moe = sb("moe", [P, 2, 768])
        wgu_s = [moe[:, j, 0:512].rearrange("p (k n) -> p k n", k=KH) for j in range(2)]
        wdn_s = [moe[:, j, 512:768] for j in range(2)]
        sg = [vst[:, 4 * j:4 * j + 4, :, :].rearrange("p a b c -> p (a b c)") for j in range(2)]
        hb = [vst[:, 8 + 4 * j:12 + 4 * j, :, :].rearrange("p a b c -> p (a b c)") for j in range(2)]
        dsc = [pf[:, 2048 * j:2048 * j + 1024].rearrange("p (a n) -> p a n", a=TPB) for j in range(2)]

        x_ld = [sem(f"x_ld{c}") for c in range(NB)]
        wqk_ld, tab_ld, wv_ld, wo_ld, w4_ld, wf_ld = (sem(n) for n in ("wqk_ld", "tab_ld", "wv_ld", "wo_ld", "w4_ld", "wf_ld"))
        ids, consts = sem("ids"), sem("consts")
        dve_s, pool_s = sem("dve_s"), sem("pool_s")
        var_ok, std_ok, xn_ok = sem("var_ok"), sem("std_ok"), sem("xn_ok")
        tr_done, xT_ok = sem("tr_done"), sem("xT_ok")
        qk_done, qk_ok = sem("qk_done"), sem("qk_ok")
        v_done, v_ok, vb_ok = sem("v_done"), sem("v_ok"), sem("vb_ok")
        rope_p = sem("rope_p")
        r_ok, rem_ok, hi_ok, mid_ok, lo_ok = (sem(n) for n in ("r_ok", "rem_ok", "hi_ok", "mid_ok", "lo_ok"))
        part_st = [sem("part_st0"), sem("part_st1")]
        lgx_ok, ex_ok, wt_ok = sem("lgx_ok"), sem("ex_ok"), sem("wt_ok")
        k_ld = [sem(f"k_ld{g}") for g in range(NG)]
        ones_ok = sem("ones_ok")
        q_ld = sem("q_ld")
        we_ld = [sem("we_ld0"), sem("we_ld1")]
        gu_done, silu_ok, h_ok, dn_done, dsc_ok, acc_ok = (sem(n) for n in ("gu_done", "silu_ok", "h_ok", "dn_done", "dsc_ok", "acc_ok"))
        s1_done, s1_read = sem("s1_done"), sem("s1_read")
        m_chain, mp_ok, mT_done, mt_ok, md_st, m_ld = (sem(n) for n in ("m_chain", "mp_ok", "mT_done", "mt_ok", "md_st", "m_ld"))
        st_done, exp_ok, pv_done, vst_ok = sem("st_done"), sem("exp_ok"), sem("pv_done"), sem("vst_ok")
        dn_ld, inv_ok, inv_st, den_ld = sem("dn_ld"), sem("inv_ok"), sem("inv_st"), sem("den_ld")
        o_ok, lb_done, den_ok, nrm_ok = sem("o_ok"), sem("lb_done"), sem("den_ok"), sem("nrm_ok")
        wo_done, wo_read, st2_ok, var2_ok = sem("wo_done"), sem("wo_read"), sem("st2_ok"), sem("var2_ok")
        out_st = sem("out_st")


        kbf = kbig[:, :].bitcast(F32)
        w4_s = kbf[:, 0:2048].rearrange("p (k n) -> p k n", k=KH)
        w1_s = kbf[:, 2048:4096].rearrange("p (k n) -> p k n", k=KH)
        w2_s = kbf[:, 4096:6144].rearrange("p (c n) -> p c n", c=FC)
        wo_s = kbf[:, 6144:7168].rearrange("p (g n) -> p g n", g=NG)
        wrb_s = kbf[:, 7168:7424].rearrange("p (k n) -> p k n", k=KH)
        b4_s = kbf[:, 7424:7432]
        b1_s = kbf[:, 7432:7440]
        br_s = kbf[:, 7440:7441]
        b2_s = kbf[:, 7448:7704]
        lrow = kbf[:, 8192:8192 + T]
        sel = kbf[:, 10240:14336].rearrange("p (t j) -> p t j", t=NT)
        eq = kbf[:, 14336:16384].rearrange("p (t s) -> p t s", t=NT)
        xn2 = qf[:, 0:4096].rearrange("p (t e) -> p t e", t=NT)
        xnT2 = qf[:, 4096:8192].rearrange("p (k t) -> p k t", k=KH)
        selb16 = kbig[:, 28672:32768].rearrange("p (t j) -> p t j", t=NT)
        selT = wide[:, 0:T].bitcast(BF16).rearrange("p (k t) -> p k t", k=2)
        junk = [wide[:, T * j:T * (j + 1)] for j in range(2)]
        rT = wide[:, 2 * T:4 * T].rearrange("p (k t) -> p k t", k=KH)
        hT = vall[:, 0:2048].rearrange("p (c j) -> p c j", c=FC)
        fxT = vall[:, 2048:2560].rearrange("p (k j) -> p k j", k=KH)
        y = vall[:, 2560:3072].rearrange("p (k e) -> p k e", k=2)
        yp = vall[:, 3584:4352].bitcast(BF16).rearrange("p (k s e) -> p k s e", k=2, s=3)
        mask = vall[:, 3072:3200]
        slots = vall[:, 3200:3456]
        ones = vall[:, 3456:3584]
        kb_s = [pf[:, 512 * j:512 * (j + 1)] for j in range(2)]
        kv_s = pf[:, 1024:1536]
        qb_s = [pf[:, 1536:2048], osb[:, :]]
        st_s = [[pf[:, 2048 + 1024 * h + 512 * j:2560 + 1024 * h + 512 * j] for j in range(2)] for h in range(2)]
        gs_s = [vst[:, 4 * j:4 * j + 4, :, :].rearrange("p a b c -> p (a b c)") for j in range(2)]
        lcol = sb("lcol", [P, NT])
        cnt = sb("cnt", [P, 4, NT])
        ew = sb("ew", [P, 3, NT])
        gm = sb("gm", [P, 4])

        tr2_done, xT2_a, xT2_v = sem("tr2_done"), sem("xT2_a"), sem("xT2_v")
        lr_done, lr_ok, lc_done, lc_ok = sem("lr_done"), sem("lr_ok"), sem("lc_done"), sem("lc_ok")
        kv_ok, qg_ok = sem("kv_ok"), sem("qg_ok")
        pj_done, ka_ok, dv_ok, rT_ok = sem("pj_done"), sem("ka_ok"), sem("dv_ok"), sem("rT_ok")
        gm_ok, ew_ok, em_ok, z_done, w_ok = sem("gm_ok"), sem("ew_ok"), sem("em_ok"), sem("z_done"), sem("w_ok")
        sel_ok, fx_done, fx_ok, h1_done, g1_ok = sem("sel_ok"), sem("fx_done"), sem("fx_ok"), sem("h1_done"), sem("g1_ok")
        sT_done, sT_ok, y1_done = sem("sT_done"), sem("sT_ok"), sem("y1_done")
        rt_done, rt_add, sc_done, y_ok = sem("rt_done"), sem("rt_add"), sem("sc_done"), sem("y_ok")
        xadd_ok, tconst = sem("xadd_ok"), sem("tconst")
        tab_ok = sem("tab_ok")
        vm_ok, selb_ok, yp_ok = sem("vm_ok"), sem("selb_ok"), sem("yp_ok")
        cnt_ok, cnt3_ok, selp_ok = sem("cnt_ok"), sem("cnt3_ok"), sem("selp_ok")
        rank_s, eq_ok, tie_ok = sem("rank_s"), sem("eq_ok"), sem("tie_ok")

        def load_second(sp):
            sp.dma_start(wo_s, wo.rearrange("g p n -> p g n")).then_inc(wo_ld, 16)
            sp.dma_start(wrb_s, wrb.rearrange("(k p) n -> p k n", p=P)).then_inc(w4_ld, 16)
            sp.dma_start(b4_s, b4).then_inc(w4_ld, 16)
            sp.dma_start(br_s, br.partition_broadcast(P)).then_inc(w4_ld, 16)
            sp.dma_start(w4_s, w4.rearrange("(k p) n -> p k n", p=P)).then_inc(w4_ld, 16)
            sp.dma_start(w1_s, w1.rearrange("(k p) n -> p k n", p=P)).then_inc(wf_ld, 16)
            sp.dma_start(w2_s, w2.rearrange("(c p) n -> p c n", p=P)).then_inc(wf_ld, 16)
            sp.dma_start(b1_s, b1).then_inc(wf_ld, 16)
            sp.dma_start(b2_s, b2.partition_broadcast(P)).then_inc(wf_ld, 16)

        def tail_sp(sp):
            for c in range(NB):
                sp.wait_ge(y_ok, TPB * (c + 1))
                sp.dma_start(out[BLK * c:BLK * (c + 1), :].rearrange("(t p) e -> p t e", p=P),
                             xs[:, TPB * c:TPB * (c + 1), :]).then_inc(out_st, 16)
            sp.wait_ge(out_st, 16 * NB)

        def tail_pool(pool):
            pool.wait_ge(pv_done, NIT * NT)
            pool.memset(mask, 1.0).then_inc(tconst, 1)
            pool.wait_ge(tconst, 1)
            pool.affine_select(out=mask, in_=mask, compare_op=ALU.is_gt, fill=0.0, base=0,
                               pattern=[[-1, P]], channel_multiplier=1).then_inc(tconst, 1)
            pool.iota(slots, [[1, SLOTS]], base=0, channel_multiplier=0, allow_small_or_imprecise_dtypes=True).then_inc(tconst, 1)
            pool.memset(ones, 1.0).then_inc(tconst, 1)
            for i in range(NT):
                pool.wait_ge(xn_ok, NT + i + 1)
                pool.tensor_tensor(xs[:, i, :], xs[:, i, :], xn2[:, i, :], ALU.add).then_inc(xadd_ok, 1)

            def gate(w):
                b, h = divmod(w, KH)
                r = rT[:, h, BLK * b:BLK * (b + 1)]
                pool.wait_ge(ka_ok, 3 * w + 3)
                pool.tensor_tensor(r, qb_s[w % 2], gs_s[w % 2], ALU.mult).then_inc(qg_ok, 1)
                pool.wait_ge(dv_ok, w + 1)
                pool.wait_ge(qg_ok, w + 1)
                pool.tensor_tensor(r, r, st_s[h][b % 2], ALU.mult).then_inc(rT_ok, 1)

            pool.wait_ge(lc_ok, 1)
            pool.wait_ge(lr_ok, NB)
            for i in range(NT):
                pool.tensor_scalar(eq[:, i, :], lrow[:, P * i:P * (i + 1)], lcol[:, i:i + 1], None, ALU.is_equal).then_inc(eq_ok, 1)
                if i % 4 == 3:
                    gate(i // 4)
            pool.wait_ge(eq_ok, NT)
            gate(4)
            gate(5)
            pool.tensor_tensor(eq, eq, mask.unsqueeze(1).to_broadcast([P, NT, P]), ALU.mult).then_inc(tie_ok, 1)
            gate(6)
            pool.wait_ge(cnt3_ok, 1)
            for i in range(NT - POOL_SEL, NT):
                pool.tensor_scalar(sel[:, i, :], slots, cnt[:, 3, i:i + 1], None, ALU.is_equal).then_inc(selp_ok, 1)
            gate(7)

        def tail_pe(pe, project_out):
            def turn(c):
                pe.wait_ge(xn_ok, NT + TPB * (c + 1))
                if c >= 2:
                    pe.wait_ge(xT2_a, c - 1)
                    pe.wait_ge(xT2_v, c - 1)
                for h in range(KH):
                    for j in range(TPB):
                        mm = pe.transpose(ps[:, 2 * (c % 2) + h, P * j:P * (j + 1)],
                                          xn2[:, TPB * c + j, P * h:P * (h + 1)], ident[:, :])
                    mm.then_inc(tr2_done, 1)

            def depth_logits(b):
                pe.wait_ge(xT2_a, b + 1)
                pe.wait_ge(xT2_v, b + 1)
                for h in range(KH):
                    mm = pe.matmul(ps[:, 4 + b, :], wrb_s[:, h, :], xnT2[:, h, BLK * b:BLK * (b + 1)], start=(h == 0), stop=(h == KH - 1))
                mm.then_inc(lr_done, 1)

            def project(w, m):
                b, h = divmod(w, KH)
                for k in range(KH):
                    mm = pe.matmul(ps[:, 4 * (w % 2) + m, :], w4_s[:, k, E * m + P * h:E * m + P * (h + 1)],
                                   xnT2[:, k, BLK * b:BLK * (b + 1)], start=(k == 0), stop=(k == KH - 1))
                mm.then_inc(pj_done, 1)

            turn(0)
            for i in range(NT - TPB, NT):
                project_out(i)
            pe.wait_ge(w4_ld, 64)
            turn(1)
            depth_logits(0)
            turn(2)
            pe.wait_ge(den_ok, 4)
            depth_logits(1)
            pe.wait_ge(wo_read, NT)
            depth_logits(2)
            turn(3)
            project(0, 0)
            depth_logits(3)
            project(0, 1)
            pe.wait_ge(lr_ok, NB)
            for i in range(NT):
                mm = pe.transpose(ps[:, 4, i:i + 1], lrow[0:1, P * i:P * (i + 1)], ident[0:1, 0:1])
            mm.then_inc(lc_done, 1)
            project(0, 2)
            project(0, 3)
            for w in range(1, NB * KH):
                if w == 1:
                    pe.wait_ge(lc_ok, 1)
                if w >= 2:
                    pe.wait_ge(ka_ok, 3 * (w - 1))
                    pe.wait_ge(kv_ok, w - 1)
                for m in range(4):
                    project(w, m)

            def turn_back(n):
                pe.wait_ge(rT_ok, KH * (n // 2 + 1))
                if n >= 6:
                    pe.wait_ge(rt_add, n - 5)
                for i in range(2):
                    for h in range(KH):
                        mm = pe.transpose(ps[:, 2 + n % 6, E * i + P * h:E * i + P * (h + 1)],
                                          rT[:, h, P * (2 * n + i):P * (2 * n + i + 1)], ident[:, :])
                mm.then_inc(rt_done, 1)

            pe.wait_ge(ka_ok, 3 * (NB * KH - 1))
            pe.wait_ge(kv_ok, NB * KH - 1)
            for k in range(KH):
                for i in range(NT):
                    if k == 0 and i < NT - POOL_SEL:
                        pe.wait_ge(sel_ok, i + 1)
                    elif k == 0:
                        pe.wait_ge(selp_ok, i + 1 - (NT - POOL_SEL))
                    mm = pe.matmul(ps[:, k, 0:SLOTS], xn2[:, i, P * k:P * (k + 1)], sel[:, i, :], start=(i == 0), stop=(i == NT - 1))
                mm.then_inc(fx_done, 1)
                if k == 0:
                    pe.wait_ge(ka_ok, 3 * NB * KH)
                    pe.wait_ge(kv_ok, NB * KH)
                    for n in range(6):
                        turn_back(n)
                else:
                    turn_back(6)
                    turn_back(7)

            def sum_chosen():
                pe.wait_ge(em_ok, 1)
                pe.wait_ge(tconst, 4)
                pe.matmul(ps[:, 0, 0:NT], ones, ew[:, 1, :], start=True, stop=True).then_inc(z_done, 1)

            def turn_sel(n):
                k, c = divmod(n, NB)
                if n < 2:
                    pe.wait_ge(rt_add, 5 + n)
                else:
                    pe.wait_ge(sT_ok, n - 1)
                if k == 0:
                    pe.wait_ge(selb_ok, c + 1)
                for i in range(TPB):
                    mm = pe.transpose(sel_bank(n)[:, P * i:P * (i + 1)], selb16[:, TPB * c + i, P * k:P * (k + 1)], identb[:, :])
                mm.then_inc(sT_done, 1)

            turn_sel(0)
            pe.wait_ge(wf_ld, 64)
            pe.wait_ge(fx_ok, 2)
            for c in range(FC):
                if c < 4:
                    pe.wait_ge(rt_add, (3, 4, 7, 8)[c])
                else:
                    pe.wait_ge(g1_ok, c - 3)
                for k in range(KH):
                    mm = pe.matmul(ps[:, 2 + (c + 2) % 4, 0:SLOTS], w1_s[:, k, P * c:P * (c + 1)], fxT[:, k, :], start=(k == 0), stop=(k == KH - 1))
                mm.then_inc(h1_done, 1)
                if c + 1 < 8:
                    turn_sel(c + 1)
                if c == 1:
                    sum_chosen()
            pe.wait_ge(w_ok, 1)
            for k in range(2):
                for c in range(FC):
                    if k == 0:
                        pe.wait_ge(g1_ok, c + 1)
                    mm = pe.matmul(ps[:, k, 0:E], hT[:, c, P * k:P * (k + 1)], w2_s[:, c, :], start=(c == 0), stop=(c == FC - 1))
                mm.then_inc(y1_done, 1)
            pe.wait_ge(sT_ok, 8)

            def scatter(i, k):
                if k == 0 and i >= 6:
                    pe.wait_ge(y_ok, i - 5)
                for part in range(3):
                    if i == 0:
                        pe.wait_ge(yp_ok, 3 * k + part + 1)
                    mm = pe.matmul(ps[:, 2 + i % 6, 0:E], selT[:, k, P * i:P * (i + 1)], yp[:, k, part, :],
                                   start=(k == 0 and part == 0), stop=(k == 1 and part == 2))
                if k == 1:
                    mm.then_inc(sc_done, 1)

            for i in range(4):
                scatter(i, 0)
            for i in range(NT):
                scatter(i, 1)
                if i + 4 < NT:
                    scatter(i + 4, 0)

        def tail_act(act, take_sums):
            def deviations(t0, t1):
                act.wait_ge(var2_ok, t1)
                act.activation(std[:, t0:t1], mv[:, t0:t1, 1], ACT.Sqrt, bias=epsc[:, :]).then_inc(std_ok, 1)

            def take_logits(b):
                act.wait_ge(lr_done, b + 1)
                act.activation(lrow[:, BLK * b:BLK * (b + 1)], ps[:, 4 + b, :], ACT.Identity, bias=br_s).then_inc(lr_ok, 1)

            deviations(0, 2 * TPB)
            take_sums(NIT - 1)
            deviations(2 * TPB, NT - TPB)
            take_turned(act, 0)
            take_turned(act, 1)
            deviations(NT - TPB, NT)
            act.wait_ge(w4_ld, 64)
            take_logits(0)
            take_turned(act, 2)
            take_logits(1)
            take_turned(act, 3)
            take_logits(2)
            take_logits(3)
            for w in range(NB * KH):
                b, h = divmod(w, KH)
                act.wait_ge(pj_done, 4 * w + 1)
                if w >= 2:
                    act.wait_ge(kv_ok, w - 1)
                act.activation(kb_s[w % 2], ps[:, 4 * (w % 2), :], ACT.Identity, bias=b4_s[:, h:h + 1]).then_inc(ka_ok, 1)
                act.wait_ge(pj_done, 4 * w + 3)
                if w >= 2:
                    act.wait_ge(rT_ok, w - 1)
                act.activation(gs_s[w % 2], ps[:, 4 * (w % 2) + 2, :], ACT.Sigmoid, bias=b4_s[:, 4 + h:5 + h]).then_inc(ka_ok, 1)
                act.wait_ge(pj_done, 4 * w + 4)
                act.activation(qb_s[w % 2], ps[:, 4 * (w % 2) + 3, :], ACT.Identity, bias=b4_s[:, 6 + h:7 + h]).then_inc(ka_ok, 1)
            for c in range(NB):
                act.wait_ge(sel_ok, min(TPB * (c + 1), NT - POOL_SEL))
                if c == NB - 1:
                    act.wait_ge(selp_ok, POOL_SEL)
                act.activation(selb16[:, TPB * c:TPB * (c + 1), :], sel[:, TPB * c:TPB * (c + 1), :], ACT.Copy).then_inc(selb_ok, 1)
            for k in range(KH):
                act.wait_ge(fx_done, k + 1)
                act.activation(fxT[:, k, :], ps[:, k, 0:SLOTS], ACT.Copy).then_inc(fx_ok, 1)
                if k == 0:
                    act.wait_ge(gm_ok, 1)
                    act.activation(ew[:, 0, :], lcol[:, :], ACT.Exp, bias=gm[:, 1:2]).then_inc(ew_ok, 1)
                    act.activation(std[:, 0:1], epsc[:, :], ACT.Gelu).then_inc(tab_ok, 1)

            def take_sel(n):
                k, c = divmod(n, NB)
                act.wait_ge(sT_done, n + 1)
                act.activation(selT[:, k, BLK * c:BLK * (c + 1)], sel_bank(n), ACT.Copy).then_inc(sT_ok, 1)

            take_sel(0)
            act.wait_ge(wf_ld, 64)
            for c in range(FC):
                act.wait_ge(h1_done, c + 1)
                act.activation(hT[:, c, :], ps[:, 2 + (c + 2) % 4, 0:SLOTS], ACT.Gelu, bias=b1_s[:, c:c + 1]).then_inc(g1_ok, 1)
                if c + 1 < 8:
                    take_sel(c + 1)

        def sel_bank(n):
            return ps[:, 6 + n % 2, 0:BLK // 2].bitcast(BF16)

        def take_turned(act, c):
            act.wait_ge(tr2_done, 2 * c + 1)
            act.activation(xnT2[:, 0, BLK * c:BLK * (c + 1)], ps[:, 2 * (c % 2), :], ACT.Copy).then_inc(xT2_a, 1)

        def tail_dve(dve, invert, add_projected):
            n_rank = [0]

            def link(ins):
                n_rank[0] += 1
                ins.then_inc(rank_s, 1)
                dve.wait_ge(rank_s, n_rank[0])

            def norm2(c):
                dve.wait_ge(std_ok, NB + max(1, c))
                link(dve.reciprocal(rstd[:, TPB * c:TPB * (c + 1)], std[:, TPB * c:TPB * (c + 1)]))
                for i in range(TPB * c, TPB * (c + 1)):
                    dve.tensor_scalar(xn2[:, i, :], xs[:, i, :], mv[:, i, 0:1], rstd[:, i:i + 1],
                                      ALU.subtract, ALU.mult).then_inc(xn_ok, 1)

            def turned(c):
                dve.wait_ge(tr2_done, 2 * c + 2)
                dve.tensor_copy(xnT2[:, 1, BLK * c:BLK * (c + 1)], ps[:, 1 + 2 * (c % 2), :]).then_inc(xT2_v, 1)

            norm2(0)
            invert(NIT - 1, 0)
            add_projected(NT - 5)
            invert(NIT - 1, 1)
            invert(NIT - 1, 2)
            add_projected(NT - 4)
            turned(0)
            invert(NIT - 1, 3)
            add_projected(NT - 3)
            norm2(1)
            add_projected(NT - 2)
            norm2(2)
            add_projected(NT - 1)
            turned(1)
            norm2(3)
            turned(2)
            turned(3)
            dve.wait_ge(lc_done, 1)
            dve.tensor_copy(lcol[:, :], ps[:, 4, 0:NT]).then_inc(lc_ok, 1)
            dve.wait_ge(lr_ok, NB)
            dve.wait_ge(lc_ok, 1)
            dve.wait_ge(tconst, 4)
            dve.wait_ge(wo_done, NT)
            dve.memset(cnt[:, 1, 0:1], 0.0)

            ranks = []

            def rank(lo, hi, i, op, row):
                if len(ranks) >= 2:
                    dve.wait_ge(cnt_ok, len(ranks) - 1)
                dve.tensor_scalar(junk[len(ranks) % 2][:, lo:hi], lrow[:, lo:hi], lcol[:, i:i + 1], 0.0, op, ALU.add,
                                  accum_out=cnt[:, row, i:i + 1]).then_inc(cnt_ok, 1)
                ranks.append(i)

            def slots_of_tokens():
                dve.wait_ge(cnt_ok, len(ranks))
                dve.wait_ge(tie_ok, 1)
                link(dve.tensor_reduce(cnt[:, 2, :], eq, AX.X, ALU.add))
                link(dve.tensor_tensor(cnt[:, 3, :], cnt[:, 0, :], cnt[:, 1, :], ALU.add))
                link(dve.tensor_tensor(cnt[:, 3, :], cnt[:, 3, :], cnt[:, 2, :], ALU.add))
                dve.memset(gm[:, 2:3], 0.0).then_inc(cnt3_ok, 1)
                for i in range(NT - POOL_SEL):
                    dve.tensor_scalar(sel[:, i, :], slots, cnt[:, 3, i:i + 1], None, ALU.is_equal).then_inc(sel_ok, 1)

            jobs = [(P * i, T, i, ALU.is_gt, 0) for i in range(NT)] + [(0, P * i, i, ALU.is_ge, 1) for i in range(1, NT)]
            rank(*jobs.pop(0))
            for w in range(NB * KH):
                b, h = divmod(w, KH)
                dve.wait_ge(ka_ok, 3 * w + 1)
                dve.wait_ge(pj_done, 4 * w + 2)
                if w:
                    dve.wait_ge(dv_ok, w)
                dve.scalar_tensor_tensor(out=kv_s, in0=ps[:, 4 * (w % 2) + 1, :], scalar=b4_s[:, 2 + h:3 + h], in1=kb_s[w % 2],
                                         op0=ALU.add, op1=ALU.mult).then_inc(kv_ok, 1)
                mine = jobs[w::NB * KH - 1] if w < NB * KH - 1 else []
                for job in mine[:1]:
                    rank(*job)
                before = 0.0 if b == 0 else st_s[h][(b - 1) % 2][:, BLK - 1:BLK]
                dve.wait_ge(kv_ok, w + 1)
                if w >= 4:
                    dve.wait_ge(rT_ok, w - 3)
                dve.tensor_tensor_scan(st_s[h][b % 2], kv_s, kv_s, before, ALU.add, ALU.bypass).then_inc(dv_ok, 1)
                for job in mine[1:]:
                    rank(*job)
                if w == NB * KH - 2:
                    slots_of_tokens()
            dve.wait_ge(xadd_ok, NT)
            for n in range(8):
                if n == 6:
                    link(dve.tensor_reduce(gm[:, 0:1], lrow, AX.X, ALU.max))
                    dve.tensor_scalar(gm[:, 1:2], gm[:, 0:1], -1.0, None, ALU.mult).then_inc(gm_ok, 1)
                dve.wait_ge(rt_done, n + 1)
                xc = xs[:, 2 * n:2 * n + 2, :]
                dve.tensor_tensor(xc, ps[:, 2 + n % 6, :].rearrange("p (t e) -> p t e", t=2), xc, ALU.add).then_inc(rt_add, 1)
            dve.wait_ge(ew_ok, 1)
            dve.scalar_tensor_tensor(out=ew[:, 1, :], in0=cnt[:, 3, :], scalar=SLOTS - 0.5, in1=ew[:, 0, :],
                                     op0=ALU.is_lt, op1=ALU.mult).then_inc(em_ok, 1)
            dve.wait_ge(z_done, 1)
            link(dve.tensor_reduce(gm[:, 2:3], ps[:, 0, 0:NT], AX.X, ALU.add))
            link(dve.reciprocal(gm[:, 3:4], gm[:, 2:3]))
            dve.tensor_scalar(ew[:, 2, :], ew[:, 1, :], gm[:, 3:4], None, ALU.mult).then_inc(w_ok, 1)
            dve.wait_ge(wf_ld, 64)
            for k in range(2):
                dve.wait_ge(y1_done, k + 1)
                link(dve.tensor_tensor(y[:, k, :], ps[:, k, 0:E], b2_s, ALU.add))
                dve.tensor_copy(yp[:, k, 0, :], y[:, k, :]).then_inc(yp_ok, 1)
                dve.wait_ge(yp_ok, 3 * k + 1)
                link(dve.tensor_tensor(y[:, k, :], y[:, k, :], yp[:, k, 0, :], ALU.subtract))
                dve.tensor_copy(yp[:, k, 1, :], y[:, k, :]).then_inc(yp_ok, 1)
                dve.wait_ge(yp_ok, 3 * k + 2)
                dve.tensor_tensor(yp[:, k, 2, :], y[:, k, :], yp[:, k, 1, :], ALU.subtract).then_inc(yp_ok, 1)
            dve.wait_ge(rt_add, 8)
            dve.wait_ge(w_ok, 1)
            for i in range(NT):
                dve.wait_ge(sc_done, i + 1)
                dve.scalar_tensor_tensor(out=xs[:, i, :], in0=ps[:, 2 + i % 6, 0:E], scalar=ew[:, 2, i:i + 1], in1=xs[:, i, :],
                                         op0=ALU.mult, op1=ALU.add).then_inc(y_ok, 1)

        mturn = ps[:, 5, 0:P // 2].bitcast(BF16)
        mbank = mturn[0:3 * HG * TPB, :]

        block = ctx.enter_context(nc.Block())

        def chain(eng, s, start=0):
            n = [start]

            def link(ins):
                n[0] += 1
                ins.then_inc(s, 1)
                eng.wait_ge(s, n[0])
            return link

        def is_first(it):
            return isinstance(it, int) and it == 0

        def q_slot(it, rows, h, off, n):
            return qring[0:rows, bass.ds((it & (QRING - 1)) * (HG * BLK) + (h * BLK + off), n)]

        def k_part(it, rows, h, off, n):
            return kbig[0:rows, bass.ds((it & GMASK) * T + (h * T + off), n)]

        @block.sync
        def _(sp):
            for c in range(NB):
                sp.dma_start(xs[:, TPB * c:TPB * (c + 1), :],
                             x[BLK * c:BLK * (c + 1), :].rearrange("(t p) e -> p t e", p=P)).then_inc(x_ld[c], 16)
            sp.dma_start(cos_s, cosT).then_inc(tab_ld, 16)
            sp.dma_start(sin_s, sinT).then_inc(tab_ld, 16)

            def load_expert(e, j, free=None):
                if free is not None:
                    sp.wait_ge(dn_done, free)
                sp.dma_start(wgu_s[j], wgu[bass.ds(e, 1), :, :].rearrange("a (k p) n -> p (a k) n", p=P)).then_inc(we_ld[j], 16)
                sp.dma_start(wdn_s[j], wdn[bass.ds(e, 1), :, :].rearrange("a p n -> p (a n)")).then_inc(we_ld[j], 16)

            load_expert(0, 0)
            load_expert(1, 1)
            for b in range(NB):
                for s, ready in enumerate((hi_ok, mid_ok, lo_ok)):
                    sp.wait_ge(ready, b + 1)
                    sp.dma_start(parts_d[s, :, :, :, BLK * b:BLK * (b + 1)].rearrange("h (i s) w n -> (h i) (s w) n", s=2),
                                 prt[:, b % 2, s, :, :]).then_inc(part_st[b % 2], 16)
            for j in range(2):
                sp.wait_ge(part_st[j], 16 * 3 * 2)

            def operand_rows(w, part, head, col, n):
                return parts_d[part, head:head + HG, :, w, col:col + n].rearrange("h r n -> r h n")

            def load_k(g):
                for r, part in enumerate(KROWS):
                    sp.dma_start(K[16 * r:16 * r + 16, HG * g:HG * (g + 1), :],
                                 operand_rows(1, part, HG * g, 0, T)).then_inc(k_ld[g], 16)

            def load_q(L, free=None):
                slot, head, col = (L & (QRING - 1)) * (HG * BLK), L & GMASK, (L & 3) * BLK
                if free is not None:
                    sp.wait_ge(st_done, free)
                for r, part in enumerate(QROWS):
                    dst = qring[16 * r:16 * r + 16, bass.ds(slot, HG * BLK)]
                    sp.dma_start(dst.rearrange("p (h n) -> p h n", h=HG),
                                 operand_rows(0, part, head, col, BLK)).then_inc(q_ld, 16)

            load_k(0)

            def load_q_alone(L):
                load_q(L)
                sp.wait_ge(q_ld, 96 * (L + 1))

            for L in range(NB):
                load_q_alone(L)

            def store_max(L):
                dst = qring[CROWS:CROWS + MROWS, bass.ds((L & (QRING - 1)) * (HG * BLK), HG * BLK)]
                sp.wait_ge(mt_ok, L + 1)
                sp.dma_start(max_d[bass.ds(L, 1), :, :].rearrange("a r p -> (a r) p"), mt[:, :]).then_inc(md_st, 16)
                sp.wait_ge(md_st, L * 16 + 16)
                sp.dma_start(dst, max_d[bass.ds(L, 1), :, :].rearrange("a (s r) p -> (a s) (r p)", s=3)).then_inc(m_ld, 16)

            for u in range(NUNIT):
                if u in TURN_AT:
                    store_max(TURN_AT[u])
                    sp.wait_ge(m_ld, 16 * (TURN_AT[u] + 1))
                if u % NB == 0 and 0 < u // NB < NEX - 1:
                    load_expert(u // NB + 1, (u // NB + 1) % 2, free=TPB * u)
                    n = u // NB
                    if n % 2:
                        load_k(n // 2 + 1)
                    elif NB + n - 1 < QRING:
                        load_q_alone(NB + n - 2)
                        load_q_alone(NB + n - 1)
            store_max(NB - 1)
            sp.wait_ge(m_ld, 16 * NB)
            for it in range(1, NIT):
                sp.wait_ge(o_ok, it)
                sp.dma_start(dcol[:, 0, :], osb[HD:P:32, :].rearrange("h (a n) -> h a n", a=P // HG)).then_inc(dn_ld, 16)
                if it <= NIT - QRING:
                    sp.wait_ge(q_ld, 96 * (it + 7))
                    load_q(it + 7, free=it * 64)
                if it == 9:
                    load_second(sp)
                sp.wait_ge(inv_ok, it)
                sp.dma_start(den_d[it - 1], dcol[:, 1, :]).then_inc(inv_st, 16)
                sp.wait_ge(inv_st, 16 * it)
                sp.wait_ge(nrm_ok, it)
                for h in range(HG):
                    row = den_d[it - 1, P // HG * h:P // HG * (h + 1), :].rearrange("a n -> (a n)")
                    sp.dma_start(den[32 * h:32 * h + 32, :], row.partition_broadcast(32)).then_inc(den_ld, 16)
                if it + 3 < NIT:
                    store_max(it + 3)
                    sp.wait_ge(m_ld, 16 * (it + 4))
                sp.wait_ge(den_ld, 64 * it)
            tail_sp(sp)

        @block.gpsimd
        def _(pool):
            link = chain(pool, pool_s)
            pool.memset(ident[:, :], 0.0).then_inc(ids, 1)
            pool.wait_ge(ids, 1)
            pool.affine_select(out=ident[:, :], in_=ident[:, :], compare_op=ALU.not_equal, fill=1.0, base=0,
                               pattern=[[-1, P]], channel_multiplier=1).then_inc(ids, 1)
            pool.wait_ge(ids, 2)
            pool.tensor_copy(identb[:, :], ident[:, :]).then_inc(ids, 1)
            link(pool.memset(selb[:, :], 0.0))
            pool.affine_select(out=selb[:, :].rearrange("p (g j) -> p g j", g=HG),
                               in_=selb[:, :].rearrange("p (g j) -> p g j", g=HG), compare_op=ALU.not_equal, fill=1.0,
                               base=-HD, pattern=[[-32, HG], [0, 32]], channel_multiplier=1).then_inc(consts, 1)
            vv = vall[:, :].rearrange("p (c d) -> p c d", d=HD + 1)
            pool.memset(vv[:, :, HD:HD + 1], 1.0).then_inc(consts, 1)

            for b in range(NB):
                pool.wait_ge(qk_ok, 4 * (b + 1))
                pool.wait_ge(tab_ld, 32)
                if b:
                    pool.wait_ge(r_ok, 2 * b)
                c = cos_s[:, BLK * b:BLK * (b + 1)]
                s = sin_s[:, BLK * b:BLK * (b + 1)]
                pool.tensor_tensor(tmp[:, 2, :, :], qk[:, b % 2, 2:4, :], c.unsqueeze(1).to_broadcast([P, 2, BLK]), ALU.mult).then_inc(rope_p, 1)
                pool.tensor_tensor(tmp[:, 3, :, :], qk[:, b % 2, 0:2, :], s.unsqueeze(1).to_broadcast([P, 2, BLK]), ALU.mult).then_inc(rope_p, 1)
            pool.wait_ge(xn_ok, NT)
            pool.wait_ge(wv_ld, 48)
            for c in range(NB):
                xc = xs[:, TPB * c:TPB * (c + 1), :]
                pool.tensor_tensor(xc, xc, bo_s.unsqueeze(1).to_broadcast([P, TPB, E]), ALU.add).then_inc(acc_ok, 1)
            pool.wait_ge(v_ok, NT)
            v5 = vall[:, :].rearrange("p (t h d) -> p t h d", t=NT, h=NH)
            for i in range(NT):
                vi = v5[:, i, :, 0:HD]
                pool.tensor_tensor(vi, vi, bv_s.rearrange("p (h d) -> p h d", h=NH), ALU.add).then_inc(vb_ok, 1)
            pool.wait_ge(vb_ok, NT)

            def add_output(u, k):
                b = k % NB
                pool.wait_ge(dsc_ok, u + 1)
                pool.wait_ge(acc_ok, u + 1)
                xc = xs[:, TPB * b:TPB * (b + 1), :]
                pool.tensor_tensor(xc, xc, dsc[k % 2], ALU.add).then_inc(acc_ok, 1)

            for u in range(8):
                add_output(u, u)
                if u % 2:
                    pool.wait_ge(lo_ok, NB)
                    pool.wait_ge(acc_ok, u + 5)
                    pool.memset(kbig[CROWS:P, u // 2 * HG * T:(u // 2 + 1) * HG * T].bitcast(F32), TWO_ONES).then_inc(ones_ok, 1)
                    pool.wait_ge(ones_ok, u // 2 + 1)
            with pool.Fori(1, NEX // 2 - 1) as pr:
                for k in range(8):
                    add_output(pr * 8 + k, k)
            v4 = vall[:, :].rearrange("p (t n) -> p t n", t=NT)

            def stage_v(it, kt):
                src = v4[:, kt, bass.ds((it & GMASK) * (HD + 1), HG * (HD + 1))]
                pool.tensor_copy(vst[:, kt, :, 0:HD + 1], src.rearrange("p (h d) -> p h d", h=HG)).then_inc(vst_ok, 1)

            def first_v(q):
                pool.wait_ge(vm_ok, q + 1)
                for kt in range(4 * q, 4 * q + 4):
                    stage_v(0, kt)

            for u in range(NUNIT - 8, NUNIT - 1):
                add_output(u, u % 8)
            pool.wait_ge(h_ok, NUNIT + 1)
            pool.memset(vst[:, 0:4, :, :], 0.0).then_inc(vm_ok, 1)
            add_output(NUNIT - 1, (NUNIT - 1) % 8)
            first_v(0)
            pool.wait_ge(dn_done, TPB * NUNIT)
            for q in range(1, 4):
                pool.memset(vst[:, 4 * q:4 * q + 4, :, :], 0.0).then_inc(vm_ok, 1)
                first_v(q)
            pool.memset(vcredit[:, :], 0.0).then_inc(nrm_ok, 1)


            def normalise(it):
                pool.wait_ge(den_ld, it * 64 + 64)
                pool.tensor_tensor(wide[:, bass.ds((it & GMASK) * (T // HG) + (it & 3) * BLK, BLK)], osb[:, :], den[:, :],
                                   ALU.mult).then_inc(nrm_ok, 1)

            for kt in range(NT):
                pool.wait_ge(pv_done, kt + 1)
                stage_v(1, kt)
            with pool.Fori(2, NIT) as it:
                for kt in range(NT):
                    if kt == 6:
                        normalise(it - 2)
                    pool.wait_ge(pv_done, it * 16 + (kt - 15))
                    stage_v(it, kt)
            normalise(NIT - 2)
            for c in range(TPB):
                pool.wait_ge(den_ok, c + 1)
                pool.tensor_tensor(outT[:, NG - 1, T - BLK + P * c:T - BLK + P * (c + 1)], osb[:, P * c:P * (c + 1)],
                                   den[:, P * c:P * (c + 1)], ALU.mult).then_inc(nrm_ok, 1)
            tail_pool(pool)

        @block.tensor
        def _(pe):
            pe.wait_ge(ids, 3)

            def turn_block(c):
                pe.wait_ge(xn_ok, TPB * (c + 1))
                if c:
                    pe.wait_ge(xT_ok, 2 * c)
                for h in range(KH):
                    for j in range(TPB):
                        mm = pe.transpose(ps[:, h, P * j:P * (j + 1)], xn[:, TPB * c + j, P * h:P * (h + 1)], ident[:, :])
                    mm.then_inc(tr_done, 1)

            turn_block(0)
            pe.wait_ge(wqk_ld, 32)
            for n in range(4 * NB):
                b, a = divmod(n, 4)
                pe.wait_ge(xT_ok, 2 * b + 2)
                if n >= 6:
                    pe.wait_ge(qk_ok, n - 5)
                for h in range(KH):
                    mm = pe.matmul(ps[:, 2 + n % 6, :], wqk_s[:, h, P * a:P * (a + 1)], xnT[:, h, BLK * b:BLK * (b + 1)],
                                   start=(h == 0), stop=(h == KH - 1))
                mm.then_inc(qk_done, 1)
                if n in TURN_AFTER:
                    turn_block(TURN_AFTER[n])
            pe.wait_ge(wv_ld, 48)
            for i in range(NT):
                if i < 2:
                    pe.wait_ge(xT_ok, KH * NB)
                elif i < 8:
                    pe.wait_ge(qk_ok, max(n + 1 for n in range(4 * NB) if 2 + n % 6 == i))
                else:
                    pe.wait_ge(v_ok, i - 7)
                for h in range(KH):
                    mm = pe.matmul(ps[:, i % 8, 0:E + NEX], xnT[:, h, P * i:P * (i + 1)], wvr_s[:, h, :],
                                   start=(h == 0), stop=(h == KH - 1))
                mm.then_inc(v_done, 1)

            def pass1(it, kt, kb):
                h, i = divmod(kt, TPB)
                n = 4 * kt + kb
                pe.wait_ge(s1_read, 256 + 2 if is_first(it) and BEFORE[n] < 0 else it * 64 + (256 + 2 + BEFORE[n] + 1))
                if n == 63:
                    pe.wait_ge(exp_ok, it * 64 + 64)
                pe.matmul(ps[:, S1_BANKS[RING[n]], :], q_slot(it + 4, CROWS, h, P * i, P), k_part(it + 4, CROWS, h, BLK * kb, BLK),
                          start=True, stop=True).then_inc(s1_done, 1)

            def expert_down(k, j, i):
                pe.matmul(ps[:, 4 + i // 2, E * (i % 2):E * (i % 2 + 1)], hb[k % 2][:, P * i:P * (i + 1)], wdn_s[j],
                          start=True, stop=True).then_inc(dn_done, 1)

            def await_down(u):
                pe.wait_ge(h_ok, u + 3)
                if u:
                    pe.wait_ge(dsc_ok, u)

            def row_scores(c):
                L, h, i, kb = c // 64, c // 16 % HG, c // 4 % TPB, c % NB
                if c == 0:
                    pe.wait_ge(k_ld[0], 96)
                if c % 64 == 0:
                    pe.wait_ge(q_ld, 96 * (L + 1))
                pe.wait_ge(s1_read, c + 1)
                pe.matmul(ps[:, 6 + c % 2, :], q_slot(L, CROWS, h, P * i, P), k_part(0, CROWS, h, BLK * kb, BLK),
                          start=True, stop=True).then_inc(s1_done, 1)

            def max_transpose(L):
                pe.wait_ge(mp_ok, L + 1)
                pe.transpose(mturn, mpad[:, :], identb[:, :]).then_inc(mT_done, 1)

            def before_plain(it, n):
                return {4: 3, 5: 1, 6: 2, 7: None}.get(n, n - 4) if it == PLAIN else n - 4

            def scores(it, kt, h):
                n = 4 * kt + h
                if n == 0:
                    pe.wait_ge(m_ld, it * 16 + 16)
                    pe.wait_ge(q_ld, it * 96 + 96)
                before, bank = BEFORE[n], S2_BANKS[RING[n]]
                if isinstance(it, int) and 64 * it + n >= 64 * PLAIN + 4:
                    before, bank = before_plain(it, n), n % 4
                elif n == 63:
                    pe.wait_ge(mt_ok, it + 4)
                if before is None:
                    pe.wait_ge(s1_read, 64 * 16 + 2)
                elif not is_first(it) or before >= 0:
                    pe.wait_ge(exp_ok, it * 64 + (before + 1))
                pe.matmul(ps[:, bank, :], k_part(it, CROWS + MROWS, h, P * kt, P),
                          q_slot(it, CROWS + MROWS, h, 0, BLK), start=True, stop=True).then_inc(st_done, 1)

            for u in range(NUNIT + 1):
                k = u % 8
                j, b = divmod(k, NB)
                if u < 2:
                    pe.wait_ge(v_ok, 10 + 2 * u)
                if u < NUNIT:
                    c0, n = ROWS_BEFORE[u], ROWS_BEFORE[u + 1] - ROWS_BEFORE[u]
                    if b == 0:
                        pe.wait_ge(we_ld[j], u // 8 * 32 + 32)
                    pe.wait_ge(h_ok, u + 1)
                for step in range(8):
                    if step < 4 and u < NUNIT:
                        w, h = divmod(step, KH)
                        mm = pe.matmul(ps[:, 2 * (k % 2) + w, :], wgu_s[j][:, h, P * w:P * (w + 1)],
                                       xnT[:, h, BLK * b:BLK * (b + 1)], start=(h == 0), stop=(h == KH - 1))
                        if h == KH - 1:
                            mm.then_inc(gu_done, 1)
                        if step == 1 and u in TURN_AT:
                            pe.wait_ge(dsc_ok, u - 1)
                            max_transpose(TURN_AT[u])
                    if step >= 4 and u:
                        if step == 4:
                            if u == NUNIT:
                                pe.wait_ge(h_ok, NUNIT + 1)
                                for g in range(NG):
                                    pe.wait_ge(k_ld[g], 96)
                                pe.wait_ge(consts, 2)
                                pe.wait_ge(ones_ok, 4)
                                scores(0, 0, 0)
                                scores(0, 0, 1)
                            if u == 1:
                                pe.wait_ge(v_ok, NT)
                            await_down(u - 1)
                        if step == 6 and u in TURN_AT:
                            pe.wait_ge(mt_ok, TURN_AT[u] + 1)
                        expert_down((u - 1) % 8, (u - 1) // NB % 2, step - 4)
                    if u < NUNIT:
                        for c in range(c0 + STEP_AT[step] * n // 24, c0 + STEP_AT[step + 1] * n // 24):
                            row_scores(c)

            def values(it, kt):
                pe.wait_ge(exp_ok, it * 64 + (4 * kt + 4))
                pe.wait_ge(vst_ok, it * 16 + (kt + 1))
                if kt == 0:
                    if is_first(it):
                        pe.wait_ge(dsc_ok, NUNIT)
                    else:
                        pe.wait_ge(o_ok, it)
                for h in range(HG):
                    mm = pe.matmul(ps[32 * h:32 * h + 32, 4, :], vst[:, kt, h, :], prob[:, kt % 2, BLK * h:BLK * (h + 1)],
                                   start=(kt == 0), stop=(kt == NT - 1))
                mm.then_inc(pv_done, 1)

            def spread_den(it):
                pe.wait_ge(o_ok, it + 1)
                pe.wait_ge(mt_ok, NIT)
                pe.matmul(ps[:, 5, :], selb[:, :], osb[:, :], start=True, stop=True).then_inc(lb_done, 1)

            def project_part(i, g):
                if g == 0:
                    pe.wait_ge(nrm_ok, 14 + i // TPB if i < NT - TPB else 17 + i - (NT - TPB))
                    if i >= 2:
                        pe.wait_ge(wo_read, i - 1)
                mm = pe.matmul(ps[:, 6 + i % 2, 0:E], outT[:, g, P * i:P * (i + 1)], wo_s[:, g, :],
                               start=(g == 0), stop=(g == NG - 1))
                if g == NG - 1:
                    mm.then_inc(wo_done, 1)

            def project_out(i):
                for g in range(NG):
                    project_part(i, g)

            def iteration(it, first, pass_1, last, max_before, projects=False):
                for kt in range(NT):
                    if kt == 7 and max_before:
                        pe.wait_ge(mt_ok, it + 3)
                        max_transpose(it + 3)
                    if first and kt == 3:
                        max_transpose(NB - 1)
                    if pass_1:
                        if kt == 0:
                            pe.wait_ge(q_ld, it * 96 + 480)
                    for h in range(HG):
                        if pass_1:
                            pass1(it, kt, h)
                        if kt < NT - 1:
                            scores(it, kt + 1, h)
                        elif not last:
                            scores(it + 1, 0, h)
                    values(it, kt)
                    if projects:
                        for i, g in project_steps(it, kt):
                            project_part(i, g)

            pe.wait_ge(h_ok, NUNIT + 2)
            scores(0, 0, 2)
            scores(0, 0, 3)
            iteration(0, True, True, False, False)
            with pe.Fori(1, 12) as it:
                iteration(it, False, True, False, True)
            iteration(12, False, False, False, True)
            pe.wait_ge(wo_ld, 16)
            for it in range(13, NIT):
                iteration(it, False, False, it == NIT - 1, False, projects=True)
            spread_den(15)
            tail_pe(pe, project_out)

        @block.scalar
        def _(act):
            act.dma_start(wqk_s, wqk.rearrange("(k p) n -> p k n", p=P)).then_inc(wqk_ld, 16)
            act.dma_start(bqk_s[:, :], bqk).then_inc(wqk_ld, 16)
            act.dma_start(wvr_s, wvr.rearrange("(k p) n -> p k n", p=P)).then_inc(wv_ld, 16)
            act.dma_start(bv_s, bv.partition_broadcast(P)).then_inc(wv_ld, 16)
            act.dma_start(bo_s, bo.partition_broadcast(P)).then_inc(wv_ld, 16)
            def deviation(c):
                act.wait_ge(var_ok, c + 1)
                act.activation(std[:, TPB * c:TPB * (c + 1)], mv[:, TPB * c:TPB * (c + 1), 1], ACT.Sqrt,
                               bias=epsc[:, :]).then_inc(std_ok, 1)

            def take_block(c):
                for h in range(KH):
                    act.wait_ge(tr_done, 2 * c + h + 1)
                    act.activation(xnT[:, h, BLK * c:BLK * (c + 1)], ps[:, h, :], ACT.Copy).then_inc(xT_ok, 1)

            def high(b):
                act.wait_ge(r_ok, 2 * b + 2)
                if b >= 2:
                    act.wait_ge(part_st[b % 2], 48)
                act.activation(prt[:, b % 2, 0, :, :], rotb[:, b % 2, :, :], ACT.Copy).then_inc(hi_ok, 1)

            def middle(b):
                act.wait_ge(rem_ok, b + 1)
                act.activation(prt[:, b % 2, 1, :, :], rem[:, :, :], ACT.Copy).then_inc(mid_ok, 1)

            def take_v(i):
                act.wait_ge(v_done, i + 1)
                dst = vall[:, i * NH * (HD + 1):(i + 1) * NH * (HD + 1)].rearrange("p (h d) -> p h d", h=NH)[:, :, 0:HD]
                act.activation(dst, ps[:, i % 8, 0:E].rearrange("p (h d) -> p h d", h=NH), ACT.Copy)
                act.activation(lg[:, i, :], ps[:, i % 8, E:E + NEX], ACT.Copy).then_inc(v_ok, 1)

            def silu(u, k):
                act.wait_ge(gu_done, u * 2 + 1)
                act.wait_ge(h_ok, u + 1)
                act.activation(sg[k % 2], ps[:, 2 * (k % 2), :], ACT.Silu).then_inc(silu_ok, 1)

            deviation(0)
            take_block(0)
            deviation(1)
            act.wait_ge(wqk_ld, 32)
            for b in range(NB + 1):
                for a in range(4 if b < NB else 0):
                    n = 4 * b + a
                    if n == 0:
                        deviation(2)
                    if n == 1:
                        deviation(3)
                    if n - 1 in TURN_AFTER:
                        take_block(TURN_AFTER[n - 1])
                    act.wait_ge(qk_done, n + 1)
                    if b >= 2:
                        act.wait_ge(r_ok, 2 * b - 2)
                    act.activation(qk[:, b % 2, a, :], ps[:, 2 + n % 6, :], ACT.Identity, bias=bqk_s[:, a:a + 1]).then_inc(qk_ok, 1)
                if b:
                    high(b - 1)
                    for i in V_AFTER_HIGH.get(b - 1, ()):
                        take_v(i)
                    if b == NB:
                        silu(0, 0)
                    if b == NB:
                        act.wait_ge(lgx_ok, 1)
                        act.activation(rt[:, 1, :, :], rt[:, 0, :, :], ACT.Exp).then_inc(ex_ok, 1)
                    middle(b - 1)
                    for i in V_AFTER_MIDDLE.get(b - 1, ()):
                        take_v(i)
            silu(1, 1)
            def scaled(u, k, e):
                act.wait_ge(wt_ok, 1)
                act.wait_ge(acc_ok, u + 3)
                for i in range(TPB):
                    if i % 2 == 0:
                        act.wait_ge(dn_done, u * 4 + (i + 2))
                    t = TPB * (k % NB) + i
                    ins = act.activation(dsc[k % 2][:, i, :], ps[:, 4 + i // 2, E * (i % 2):E * (i % 2 + 1)], ACT.Copy,
                                         scale=wtok[:, e:e + 1, t] if isinstance(e, int) else wtok[:, bass.ds(e, 1), t])
                ins.then_inc(dsc_ok, 1)

            def units(pr):
                for k in range(8):
                    if not (is_first(pr) and k == 0) and not (isinstance(pr, int) and pr * 8 + k == NUNIT - 1):
                        silu(pr * 8 + (k + 1), (k + 1) % 8)
                    if isinstance(pr, int) and pr * 8 + k == NUNIT - 1:
                        act.activation(osb[:, 0:1], epsc[:, :], ACT.Exp).then_inc(tab_ok, 1)
                    scaled(pr * 8 + k, k, pr * 2 + k // NB)

            units(0)
            with act.Fori(1, NEX // 2 - 1) as pr:
                units(pr)
            units(NEX // 2 - 1)

            def exps(it, kt, h, plain):
                n = 4 * kt + h
                bank = n % 4 if plain and not (isinstance(it, int) and n < 4) else S2_BANKS[RING[n]]
                act.wait_ge(st_done, it * 64 + (n + 1))
                if is_first(it) and h == 0 and kt < 2:
                    act.wait_ge(acc_ok, NUNIT + 3 + kt)
                if h == 0 and (not is_first(it) or kt >= 2):
                    act.wait_ge(pv_done, it * 16 + (kt - 1))
                act.activation(prob[:, kt % 2, BLK * h:BLK * (h + 1)], ps[:, bank, :], ACT.Exp, scale=SCALE).then_inc(exp_ok, 1)

            def take_sums(it):
                act.wait_ge(pv_done, it * 16 + 16)
                act.wait_ge(nrm_ok, it + 1)
                act.activation(osb[:, :], ps[:, 4, :], ACT.Copy).then_inc(o_ok, 1)

            def iteration(it, plain=False):
                for kt in range(NT):
                    for h in range(HG):
                        exps(it, kt, h, plain)
                        if kt == 0 and h == HG - 1 and not is_first(it):
                            take_sums(it - 1)

            iteration(0)
            with act.Fori(1, PLAIN) as it:
                iteration(it)
            iteration(PLAIN, True)
            with act.Fori(PLAIN + 1, NIT) as it:
                iteration(it, True)
            tail_act(act, take_sums)

        @block.vector
        def _(dve):
            link = chain(dve, dve_s)
            dve.memset(mpad[:, :], 0.0)
            dve.memset(mneg[:, :], 0.0).then_inc(h_ok, 2)
            dve.memset(mres[:, :], 0.0).then_inc(s1_read, 2)
            link(dve.memset(epsc[:, :], EPS))

            def stats1(c):
                dve.wait_ge(x_ld[c], 16)
                for i in range(TPB * c, TPB * (c + 1)):
                    ins = dve.bn_stats(stats[:, i, :], xs[:, i, :])
                link(ins)
                for i in range(TPB * c, TPB * (c + 1)):
                    ins = dve.bn_aggr(mv[:, i, :], stats[:, i, :])
                ins.then_inc(var_ok, 1)

            def norm1(c):
                dve.wait_ge(std_ok, c + 1)
                link(dve.reciprocal(rstd[:, TPB * c:TPB * (c + 1)], std[:, TPB * c:TPB * (c + 1)]))
                for i in range(TPB * c, TPB * (c + 1)):
                    dve.tensor_scalar(xn[:, i, :], xs[:, i, :], mv[:, i, 0:1], rstd[:, i:i + 1],
                                      ALU.subtract, ALU.mult).then_inc(xn_ok, 1)

            for c in range(NB):
                stats1(c)
                norm1(c)

            def rotate(b):
                dve.wait_ge(qk_ok, 4 * (b + 1))
                dve.wait_ge(tab_ld, 32)
                if b:
                    dve.wait_ge(r_ok, 2 * b)
                c = cos_s[:, BLK * b:BLK * (b + 1)].unsqueeze(1).to_broadcast([P, 2, BLK])
                s = sin_s[:, BLK * b:BLK * (b + 1)].unsqueeze(1).to_broadcast([P, 2, BLK])
                dve.tensor_tensor(tmp[:, 0, :, :], qk[:, b % 2, 0:2, :], c, ALU.mult)
                link(dve.tensor_tensor(tmp[:, 1, :, :], qk[:, b % 2, 2:4, :], s, ALU.mult))
                dve.tensor_tensor(rotb[:, b % 2, 0:2, :], tmp[:, 0, :, :], tmp[:, 1, :, :], ALU.subtract).then_inc(r_ok, 1)
                dve.wait_ge(rope_p, 2 * b + 2)
                dve.tensor_tensor(rotb[:, b % 2, 2:4, :], tmp[:, 2, :, :], tmp[:, 3, :, :], ALU.add).then_inc(r_ok, 1)

            def split(b):
                dve.wait_ge(hi_ok, b + 1)
                dve.wait_ge(r_ok, 2 * b + 2)
                if b:
                    dve.wait_ge(lo_ok, b)
                dve.tensor_tensor(rem[:, :, :], rotb[:, b % 2, :, :], prt[:, b % 2, 0, :, :], ALU.subtract).then_inc(rem_ok, 1)

            def low(b):
                dve.wait_ge(mid_ok, b + 1)
                dve.wait_ge(rem_ok, b + 1)
                dve.tensor_tensor(prt[:, b % 2, 2, :, :], rem[:, :, :], prt[:, b % 2, 1, :, :], ALU.subtract).then_inc(lo_ok, 1)

            def hidden(u):
                dve.wait_ge(silu_ok, u + 1)
                dve.wait_ge(gu_done, 2 * u + 2)
                dve.tensor_tensor(hb[u % 2], sg[u % 2], ps[:, 2 * (u % 2) + 1, :], ALU.mult).then_inc(h_ok, 1)

            for b in range(NB):
                rotate(b)
                if b:
                    low(b - 1)
                split(b)
            hidden(0)

            dve.wait_ge(v_ok, NT)
            link(dve.tensor_reduce(rs[:, 0, :], lg[:, :, :], AX.X, ALU.max))
            dve.tensor_tensor(rt[:, 0, :, :], lg[:, :, :], rs[:, 0, :].unsqueeze(2).to_broadcast([P, NT, NEX]), ALU.subtract).then_inc(lgx_ok, 1)
            dve.wait_ge(ex_ok, 1)
            link(dve.tensor_reduce(rs[:, 1, :], rt[:, 1, :, :], AX.X, ALU.add))
            link(dve.reciprocal(rs[:, 2, :], rs[:, 1, :]))
            link(dve.tensor_tensor(rt[:, 2, :, :], rt[:, 1, :, :], rs[:, 2, :].unsqueeze(2).to_broadcast([P, NT, NEX]), ALU.mult))
            for e in range(NEX):
                mine = rt[:, 2, :, e:e + 1]
                ins = dve.tensor_tensor(cmp[:, e, :, 0:e + 1], mine.to_broadcast([P, NT, e + 1]), rt[:, 2, :, 0:e + 1], ALU.is_gt)
                if e < NEX - 1:
                    ins = dve.tensor_tensor(cmp[:, e, :, e + 1:], mine.to_broadcast([P, NT, NEX - 1 - e]), rt[:, 2, :, e + 1:], ALU.is_ge)
            link(ins)
            link(dve.tensor_reduce(rt[:, 0, :, :], cmp.rearrange("p a t e -> p t e a"), AX.X, ALU.add))
            link(dve.scalar_tensor_tensor(out=rt[:, 3, :, :], in0=rt[:, 0, :, :], scalar=1.5, in1=rt[:, 2, :, :],
                                          op0=ALU.is_lt, op1=ALU.mult))
            link(dve.tensor_reduce(rs[:, 3, :], rt[:, 3, :, :], AX.X, ALU.add))
            link(dve.reciprocal(rs[:, 0, :], rs[:, 3, :]))
            dve.tensor_tensor(wtok[:, :, :].rearrange("p e t -> p t e"), rt[:, 3, :, :],
                              rs[:, 0, :].unsqueeze(2).to_broadcast([P, NT, NEX]), ALU.mult).then_inc(wt_ok, 1)
            hidden(1)
            low(NB - 1)
            dve.wait_ge(wt_ok, 1)

            def row_max(n, dst, bank):
                dve.wait_ge(s1_done, n)
                dve.tensor_reduce(dst, ps[:, bank, :], AX.X, ALU.max).then_inc(s1_read, 1)

            def max_step(L, j, src):
                if j > 1:
                    dve.wait_ge(m_chain, L * 5 + (j - 1))
                if j == 1:
                    dve.tensor_reduce(mres[:, :].rearrange("p (h t) -> p h t", h=HG), src, AX.X, ALU.max).then_inc(m_chain, 1)
                elif j == 2:
                    dve.tensor_scalar(mneg[:, :], mres[:, :], -1.0, None, ALU.mult).then_inc(m_chain, 1)
                elif j == 3:
                    dve.tensor_copy(mpart[:, 0, :], mneg[:, :]).then_inc(m_chain, 1)
                elif j == 4:
                    dve.tensor_tensor(mres[:, :], mneg[:, :], mpart[:, 0, :], ALU.subtract).then_inc(m_chain, 1)
                elif j == 5:
                    dve.tensor_copy(mpart[:, 1, :], mres[:, :]).then_inc(m_chain, 1)
                else:
                    dve.tensor_tensor(mpart[:, 2, :], mres[:, :], mpart[:, 1, :], ALU.subtract).then_inc(mp_ok, 1)

            def max_parts(L, src):
                for j in range(1, 7):
                    max_step(L, j, src)

            def take_max(L):
                dve.wait_ge(mT_done, L + 1)
                if not is_first(L):
                    dve.wait_ge(md_st, L * 16)
                dve.tensor_copy(mt[:, :], mbank).then_inc(mt_ok, 1)

            m4 = mraw[:, :].rearrange("p (b h t k) -> p b h t k", h=HG, b=NB, t=TPB)
            for u in range(NUNIT):
                c0, n = ROWS_BEFORE[u], ROWS_BEFORE[u + 1] - ROWS_BEFORE[u]
                for r in range(n + 1):
                    if r == n // 2 and u in TURN_AT:
                        take_max(TURN_AT[u])
                    if r == HIDDEN_AT * n // 24 and u >= 2:
                        hidden(u)
                    if r < n:
                        c = c0 + r
                        row_max(c + 1, mraw[:, c:c + 1], 6 + c % 2)
                        if c % 64 == 63 and c < 192:
                            dve.wait_ge(s1_read, c + 3)
                            max_parts(c // 64, m4[:, c // 64, :, :, :])
            dve.wait_ge(s1_read, 256 + 2)

            mit = mnew[:, :].rearrange("p (h t k) -> p h t k", h=HG, t=TPB)

            def invert_spread(it):
                dve.wait_ge(dn_ld, it * 16 + 16)
                dve.reciprocal(dcol[:, 1, :], dcol[:, 0, :]).then_inc(inv_ok, 1)

            def invert(it, c):
                if c == 0:
                    dve.wait_ge(lb_done, 1)
                    dve.wait_ge(nrm_ok, it + 1)
                dve.reciprocal(den[:, P * c:P * (c + 1)], ps[:, 5, P * c:P * (c + 1)]).then_inc(den_ok, 1)

            def add_projected(i):
                dve.wait_ge(wo_done, i + 1)
                dve.tensor_tensor(xs[:, i, :], ps[:, 6 + i % 2, 0:E], xs[:, i, :], ALU.add).then_inc(wo_read, 1)
                dve.wait_ge(wo_read, i + 1)
                dve.bn_stats(stats[:, i, :], xs[:, i, :]).then_inc(st2_ok, 1)
                dve.wait_ge(st2_ok, i + 1)
                dve.bn_aggr(mv[:, i, :], stats[:, i, :]).then_inc(var2_ok, 1)

            def iteration(it, first, pass_1, max_before, projects=False):
                if max_before:
                    dve.wait_ge(s1_read, it * 64 + 258)
                    for j in range(1, 2 if pass_1 else 7):
                        max_step(it + 3, j, mit)
                for kt in range(NT):
                    if pass_1:
                        for kb in range(NB):
                            c = 4 * kt + kb
                            if c == 0 and max_before:
                                dve.wait_ge(m_chain, it * 5 + 16)
                            row_max(it * 64 + (256 + c + 1), mnew[:, c:c + 1], S1_BANKS[RING[c]])
                            if c < 5 and max_before:
                                max_step(it + 3, c + 2, mit)
                    if not first and kt == 3:
                        invert_spread(it - 1)
                    if kt == 7 and max_before:
                        take_max(it + 3)
                    if first and kt == 0:
                        max_parts(NB - 1, m4[:, NB - 1, :, :, :])
                    if first and kt == 4:
                        take_max(NB - 1)
                    if projects:
                        for i, g in project_steps(it, kt):
                            if g == NG - 1 and i < NT - TPB - 1:
                                add_projected(i)

            iteration(0, True, True, False)
            with dve.Fori(1, 12) as it:
                iteration(it, False, True, True)
            iteration(12, False, False, True)
            dve.wait_ge(acc_ok, 4 * NEX + 4)
            for it in range(13, NIT):
                iteration(it, False, False, False, projects=True)
            tail_dve(dve, invert, add_projected)


def kernel(**inputs):
    import concourse.bacc as bacc
    from concourse.bass_utils import run_bass_kernel_spmd as run

    a = {k: np.asarray(v) for k, v in inputs.items()}
    c = np.ascontiguousarray
    half = HD // 2
    rows = [np.array([h * HD + s * half + i for h in range(NH) for i in range(half)]) for s in range(2)]
    wq, wk = a["L0_attn_Wq"], a["L0_attn_Wk"]
    bq, bk = a["L0_attn_bq"], a["L0_attn_bk"]
    wqk = c(np.concatenate([wq[rows[0]], wk[rows[0]], wq[rows[1]], wk[rows[1]]]).T)
    bqk = c(np.stack([bq[rows[0]], bk[rows[0]], bq[rows[1]], bk[rows[1]]], axis=1))
    freq = (np.float32(1.0) / np.float32(10000.0) ** (np.arange(0, HD, 2, dtype=np.float32) / np.float32(HD))).astype(np.float32)
    angle = (np.arange(T, dtype=np.float32)[None, :] * freq[:, None]).astype(np.float32)
    cosT = c(np.tile(np.cos(angle).astype(np.float32), (NH, 1)))
    sinT = c(np.tile(np.sin(angle).astype(np.float32), (NH, 1)))
    wvr = c(np.concatenate([a["L0_attn_Wv"], a["L0_ffn_router_gate"]]).T)
    gu = a["L0_ffn_expert_gate_up"]
    wgu = c(np.concatenate([gu[:, :, 0::2], gu[:, :, 1::2]], axis=2))
    woT = np.zeros((NG, HG, 32, E), np.float32)
    woT[:, :, :HD, :] = a["L0_attn_Wo"].T.reshape(NG, HG, HD, E)
    four = ("k", "v", "g", "q")
    w4 = c(np.concatenate([a["L1_attn_W" + m] for m in four]).T)
    b4 = c(np.concatenate([a["L1_attn_b" + m].reshape(KH, P) for m in four]).T)
    feeds = dict(
        x=c(a["L0_attn_hidden_states"][0]), wqk=wqk, bqk=bqk, cosT=cosT, sinT=sinT, wvr=wvr, bv=a["L0_attn_bv"], bo=a["L0_attn_bo"],
        wgu=wgu, wdn=c(a["L0_ffn_expert_down"]), wo=woT.reshape(NG, P, E), w4=w4, b4=b4,
        wrb=c(np.tile(a["L1_ffn_Wr"], (1, P))), br=a["L1_ffn_br"], w1=a["L1_ffn_W1"], b1=c(a["L1_ffn_b1"].reshape(FC, P).T),
        w2=a["L1_ffn_W2"], b2=a["L1_ffn_b2"])
    nc = bacc.Bacc("TRN2", target_bir_lowering=False, num_devices=1)
    arrays = {f"in_{k}": c(v) for k, v in feeds.items()}
    aps = {k: nc.dram_tensor(f"in_{k}", feeds[k].shape, mybir.dt.from_np(feeds[k].dtype), kind="ExternalInput").ap() for k in feeds}
    out = nc.dram_tensor("out_0", (T, E), F32, kind="ExternalOutput").ap()
    program(nc, out=out, **aps)
    r = run(nc, [arrays], core_ids=[0])
    return r.results[0]["out_0"].reshape(1, T, E)
```
